# Optimizing a Trainium2 kernel written in Bass

```python
import numpy as np
import jax
import jax.numpy as jnp

def _softmax(x, axis=-1):
    return jax.nn.softmax(x, axis=axis)

def _gelu(x):
    return jax.nn.gelu(x, approximate=True)

def _silu(x):
    return jax.nn.silu(x)

def _sigmoid(x):
    return jax.nn.sigmoid(x)

def _layernorm(x, axis=-1, eps=1e-05):
    m = jnp.mean(x, axis=axis, keepdims=True)
    v = jnp.var(x, axis=axis, keepdims=True)
    return (x - m) / jnp.sqrt(v + eps)

def _scatter_add(tgt, idx, src, axis=0):
    return tgt.at[idx].add(src)

def _segment_sum(src, seg, n):
    return jax.ops.segment_sum(src, seg, n)
kernel_name = 'mk_xattn_ffn_d2_seqx_r4_1d6c0f'

def setup_inputs(seed: int=0):
    np.random.seed(seed)
    _w = jnp.asarray

    def _rec_inputs():
        import jax
        import jax.numpy as jnp
        _rk = jax.random.key(seed)
        x = -0.0002928 + 1 * jax.random.normal(jax.random.fold_in(_rk, 1), (16, 128, 256), jnp.float32)
        _lenS = 128 - jax.random.randint(jax.random.fold_in(_rk, 7), (16,), 0, max(1, 128 // 4) + 1, jnp.int32)
        _lenS2 = 128 - jax.random.randint(jax.random.fold_in(_rk, 8), (16,), 0, max(1, 128 // 4) + 1, jnp.int32)
        _ctx_1024P = jax.random.normal(jax.random.fold_in(_rk, 11), (16, 16, 256), jnp.float32)
        _ctx_1024c = jax.random.dirichlet(jax.random.fold_in(_rk, 511), 0.3 * jnp.ones((16,), jnp.float32), (16, 128))
        _ctx_1024t = jnp.einsum('bsk,bkd->bsd', _ctx_1024c, _ctx_1024P)
        _ctx_1024t = _ctx_1024t * jax.lax.rsqrt(jnp.mean(jnp.square(_ctx_1024t)) + 1e-12) * 0.953939
        ctx_1024 = -1.39393e-06 + 0.999914 * (_ctx_1024t + 0.3 * jax.random.normal(jax.random.fold_in(_rk, 611), (16, 128, 256), jnp.float32))
        fside_Bx16xSxS2_0 = 9.80324e-06 + 0.100009 * jax.random.normal(jax.random.fold_in(_rk, 12), (16, 16, 128, 128), jnp.float32)
        fside_SxS2_0 = -2.64403e-05 + 0.100002 * jax.random.normal(jax.random.fold_in(_rk, 14), (128, 128), jnp.float32)
        _validS = jnp.arange(128)[None, :] < _lenS[:, None]
        _validS2 = jnp.arange(128)[None, :] < _lenS2[:, None]
        _causal = jnp.tril(jnp.ones((128, 128), dtype=bool))
        mask_BxS2_bf0 = jnp.logical_not(jnp.ones((16, 128), dtype=bool))
        mask_SxS2_bk0 = jnp.logical_not(jnp.broadcast_to(_validS2[0:1, :], (128, 128)))
        return (x, ctx_1024, fside_Bx16xSxS2_0, fside_SxS2_0, mask_BxS2_bf0, mask_SxS2_bk0)
    x, ctx_1024, fside_Bx16xSxS2_0, fside_SxS2_0, mask_BxS2_bf0, mask_SxS2_bk0 = _rec_inputs()

    def _L0_xattn_setup():
        import jax, jax.numpy as jnp
        import numpy as np
        E = 256
        H = 16
        D = E // H
        key = jax.random.key(seed)
        ks = jax.random.split(key, 12)
        B, T, S = (2, 512, 512)
        inp = {'query': jax.random.normal(ks[0], (B, T, E), jnp.float32), 'key': jax.random.normal(ks[1], (B, S, E), jnp.float32), 'value': jax.random.normal(ks[2], (B, S, E), jnp.float32), 'spatial_bias': jax.random.normal(ks[3], (B, H, T, S), jnp.float32) * 0.1, 'directional_bias': jax.random.normal(ks[4], (B, H, T, S), jnp.float32) * 0.1, 'key_padding_mask': jnp.zeros((B, S), dtype=bool), 'attn_mask': jax.random.normal(ks[5], (T, S), jnp.float32) * 0.1, 'Wq': jax.random.normal(ks[6], (E, E), jnp.float32) / np.sqrt(E), 'bq': jnp.zeros((E,), jnp.float32), 'Wk': jax.random.normal(ks[7], (E, E), jnp.float32) / np.sqrt(E), 'bk': jnp.zeros((E,), jnp.float32), 'Wv': jax.random.normal(ks[8], (E, E), jnp.float32) / np.sqrt(E), 'bv': jnp.zeros((E,), jnp.float32), 'Wo': jax.random.normal(ks[9], (E, E), jnp.float32) / np.sqrt(E), 'bo': jnp.zeros((E,), jnp.float32)}
        return inp
    _L0_xattn_all = _L0_xattn_setup()
    _L0_xattn_in = {k: v for k, v in _L0_xattn_all.items() if k in ('Wq', 'bq', 'Wk', 'bk', 'Wv', 'bv', 'Wo', 'bo')}
    del _L0_xattn_all

    def _L0_ffn_setup():
        import jax, jax.numpy as jnp
        import numpy as np
        B, S, D, E, F = (2, 256, 256, 14, 512)
        key = jax.random.key(seed)
        k0, k1, k2, k3 = jax.random.split(key, 4)
        h = jax.random.normal(k0, (B, S, D), jnp.float32)
        gate_w = jax.random.normal(k1, (E, D), jnp.float32) * 0.02
        w1 = jax.random.normal(k2, (E, D, F), jnp.float32) * (1.0 / np.sqrt(D).astype(np.float32))
        b1 = jnp.zeros((E, F), jnp.float32)
        w2 = jax.random.normal(k3, (E, F, D), jnp.float32) * (1.0 / np.sqrt(F).astype(np.float32))
        b2 = jnp.zeros((E, D), jnp.float32)
        return {'h': h, 'gate_w': gate_w, 'w1': w1, 'b1': b1, 'w2': w2, 'b2': b2}
    _L0_ffn_all = _L0_ffn_setup()
    _L0_ffn_in = {k: v for k, v in _L0_ffn_all.items() if k in ('gate_w', 'w1', 'b1', 'w2', 'b2')}
    del _L0_ffn_all

    def _L1_xattn_setup():
        import jax, jax.numpy as jnp
        import numpy as np
        B, S, DIM, H = (4, 512, 256, 16)
        HD = DIM // H
        SCALE = HD ** (-0.5)

        def _heads(x):
            b, s, _ = x.shape
            return x.reshape(b, s, H, HD).transpose(0, 2, 1, 3)
        key = jax.random.key(seed)
        ks = jax.random.split(key, 7)
        init = 0.02
        return {'query': jax.random.normal(ks[0], (B, S, DIM), dtype=jnp.float32), 'key': jax.random.normal(ks[1], (B, S, DIM), dtype=jnp.float32), 'value': jax.random.normal(ks[2], (B, S, DIM), dtype=jnp.float32), 'attn_mask': jnp.tril(jnp.ones((S, S), dtype=bool)), 'Wq': jax.random.normal(ks[3], (DIM, DIM), dtype=jnp.float32) * init, 'Wk': jax.random.normal(ks[4], (DIM, DIM), dtype=jnp.float32) * init, 'Wv': jax.random.normal(ks[5], (DIM, DIM), dtype=jnp.float32) * init, 'Wo': jax.random.normal(ks[6], (DIM, DIM), dtype=jnp.float32) * init}
    _L1_xattn_all = _L1_xattn_setup()
    _L1_xattn_in = {k: v for k, v in _L1_xattn_all.items() if k in ('Wq', 'Wk', 'Wv', 'Wo')}
    del _L1_xattn_all

    def _L1_ffn_setup():
        import jax, jax.numpy as jnp
        import numpy as np
        import math
        N_EMBD = 256
        HIDDEN = 4 * N_EMBD
        N_EXPERTS = 8
        TOP_K = 2
        B, T = (4, 512)

        def new_gelu(x):
            c = math.sqrt(2.0 / math.pi)
            return 0.5 * x * (1.0 + jnp.tanh(c * (x + 0.044715 * x * x * x)))

        def _moe_forward(x, Wfc_s, bfc_s, Wproj_s, bproj_s, Wr, Wfc, bfc, Wproj, bproj):
            Bb, Tt, C = x.shape
            xf = x.reshape(Bb * Tt, C)
            N = Bb * Tt
            shared = new_gelu(xf @ Wfc_s + bfc_s) @ Wproj_s + bproj_s
            logits = xf @ Wr
            probs = jax.nn.softmax(logits, axis=-1)
            topk_p, topk_i = jax.lax.top_k(probs, TOP_K)
            topk_p = topk_p / jnp.sum(topk_p, axis=-1, keepdims=True)
            gate = jnp.zeros((N, N_EXPERTS), dtype=xf.dtype)
            gate = gate.at[jnp.arange(N)[:, None], topk_i].add(topk_p)
            routed = jnp.zeros_like(xf)
            for e in range(N_EXPERTS):
                h = new_gelu(xf @ Wfc[e] + bfc[e]) @ Wproj[e] + bproj[e]
                routed = routed + h * gate[:, e:e + 1]
            return (shared + routed).reshape(Bb, Tt, C)
        key = jax.random.key(seed)
        ks = jax.random.split(key, 10)
        s = 0.02
        return {'x': jax.random.normal(ks[0], (B, T, N_EMBD), dtype=jnp.float32), 'Wfc_s': jax.random.normal(ks[1], (N_EMBD, HIDDEN), dtype=jnp.float32) * s, 'bfc_s': jnp.zeros((HIDDEN,), dtype=jnp.float32), 'Wproj_s': jax.random.normal(ks[2], (HIDDEN, N_EMBD), dtype=jnp.float32) * s, 'bproj_s': jnp.zeros((N_EMBD,), dtype=jnp.float32), 'Wr': jax.random.normal(ks[3], (N_EMBD, N_EXPERTS), dtype=jnp.float32) * s, 'Wfc': jax.random.normal(ks[4], (N_EXPERTS, N_EMBD, HIDDEN), dtype=jnp.float32) * s, 'bfc': jnp.zeros((N_EXPERTS, HIDDEN), dtype=jnp.float32), 'Wproj': jax.random.normal(ks[5], (N_EXPERTS, HIDDEN, N_EMBD), dtype=jnp.float32) * s, 'bproj': jnp.zeros((N_EXPERTS, N_EMBD), dtype=jnp.float32)}
    _L1_ffn_all = _L1_ffn_setup()
    _L1_ffn_in = {k: v for k, v in _L1_ffn_all.items() if k in ('Wfc_s', 'bfc_s', 'Wproj_s', 'bproj_s', 'Wr', 'Wfc', 'bfc', 'Wproj', 'bproj')}
    del _L1_ffn_all
    return {'x': x, 'ctx_1024': ctx_1024, 'fside_Bx16xSxS2_0': fside_Bx16xSxS2_0, 'fside_SxS2_0': fside_SxS2_0, 'mask_BxS2_bf0': mask_BxS2_bf0, 'mask_SxS2_bk0': mask_SxS2_bk0, 'L0_xattn_Wq': _L0_xattn_in['Wq'], 'L0_xattn_bq': _L0_xattn_in['bq'], 'L0_xattn_Wk': _L0_xattn_in['Wk'], 'L0_xattn_bk': _L0_xattn_in['bk'], 'L0_xattn_Wv': _L0_xattn_in['Wv'], 'L0_xattn_bv': _L0_xattn_in['bv'], 'L0_xattn_Wo': _L0_xattn_in['Wo'], 'L0_xattn_bo': _L0_xattn_in['bo'], 'L0_ffn_gate_w': _L0_ffn_in['gate_w'], 'L0_ffn_w1': _L0_ffn_in['w1'], 'L0_ffn_b1': _L0_ffn_in['b1'], 'L0_ffn_w2': _L0_ffn_in['w2'], 'L0_ffn_b2': _L0_ffn_in['b2'], 'L1_xattn_Wq': _L1_xattn_in['Wq'], 'L1_xattn_Wk': _L1_xattn_in['Wk'], 'L1_xattn_Wv': _L1_xattn_in['Wv'], 'L1_xattn_Wo': _L1_xattn_in['Wo'], 'L1_ffn_Wfc_s': _L1_ffn_in['Wfc_s'], 'L1_ffn_bfc_s': _L1_ffn_in['bfc_s'], 'L1_ffn_Wproj_s': _L1_ffn_in['Wproj_s'], 'L1_ffn_bproj_s': _L1_ffn_in['bproj_s'], 'L1_ffn_Wr': _L1_ffn_in['Wr'], 'L1_ffn_Wfc': _L1_ffn_in['Wfc'], 'L1_ffn_bfc': _L1_ffn_in['bfc'], 'L1_ffn_Wproj': _L1_ffn_in['Wproj'], 'L1_ffn_bproj': _L1_ffn_in['bproj']}

def reference(x, ctx_1024, fside_Bx16xSxS2_0, fside_SxS2_0, mask_BxS2_bf0, mask_SxS2_bk0, L0_xattn_Wq, L0_xattn_bq, L0_xattn_Wk, L0_xattn_bk, L0_xattn_Wv, L0_xattn_bv, L0_xattn_Wo, L0_xattn_bo, L0_ffn_gate_w, L0_ffn_w1, L0_ffn_b1, L0_ffn_w2, L0_ffn_b2, L1_xattn_Wq, L1_xattn_Wk, L1_xattn_Wv, L1_xattn_Wo, L1_ffn_Wfc_s, L1_ffn_bfc_s, L1_ffn_Wproj_s, L1_ffn_bproj_s, L1_ffn_Wr, L1_ffn_Wfc, L1_ffn_bfc, L1_ffn_Wproj, L1_ffn_bproj):
    import jax
    import jax.numpy as jnp

    def _L0_xattn_ref(query, key, value, spatial_bias, directional_bias, key_padding_mask, attn_mask, Wq, bq, Wk, bk, Wv, bv, Wo, bo):
        import jax, jax.numpy as jnp
        import numpy as np
        E = 256
        H = 16
        D = E // H
        B, T, _ = query.shape
        S = key.shape[1]
        scale = D ** (-0.5)
        q = (query @ Wq.T + bq).reshape(B, T, H, D).transpose(0, 2, 1, 3)
        k = (key @ Wk.T + bk).reshape(B, S, H, D).transpose(0, 2, 1, 3)
        v = (value @ Wv.T + bv).reshape(B, S, H, D).transpose(0, 2, 1, 3)
        scores = jnp.einsum('bhtd,bhsd->bhts', q, k) * scale
        scores = scores + attn_mask[None, None, :, :]
        pad = key_padding_mask[:, None, None, :]
        scores = jnp.where(pad, -jnp.inf, scores)
        if T == S:
            scores = scores + spatial_bias + directional_bias
        probs = jax.nn.softmax(scores, axis=-1)
        out = jnp.einsum('bhts,bhsd->bhtd', probs, v)
        out = out.transpose(0, 2, 1, 3).reshape(B, T, E)
        return out @ Wo.T + bo

    def _L0_ffn_ref(h, gate_w, w1, b1, w2, b2):
        import jax, jax.numpy as jnp
        import numpy as np
        B, S, D, E, F = (2, 256, 256, 14, 512)
        Bb, Ss, Dd = h.shape
        x = h.reshape(Bb * Ss, Dd)
        logits = x @ gate_w.T
        probs = jax.nn.softmax(logits, axis=-1)
        top2_p, top2_i = jax.lax.top_k(probs, 2)
        w = top2_p / jnp.maximum(top2_p.sum(-1, keepdims=True), 1e-10)
        hh = jnp.einsum('nd,edf->nef', x, w1) + b1
        hh = jax.nn.gelu(hh, approximate=False)
        all_out = jnp.einsum('nef,efd->ned', hh, w2) + b2
        n = jnp.arange(x.shape[0])
        out0 = all_out[n, top2_i[:, 0]]
        out1 = all_out[n, top2_i[:, 1]]
        moe_out = w[:, 0:1] * out0 + w[:, 1:2] * out1
        result = jnp.clip(x + moe_out, -100.0, 100.0).reshape(Bb, Ss, Dd)
        return result

    def _L1_xattn_ref(query, key, value, attn_mask, Wq, Wk, Wv, Wo):
        import jax, jax.numpy as jnp
        import numpy as np
        B, S, DIM, H = (4, 512, 256, 16)
        HD = DIM // H
        SCALE = HD ** (-0.5)

        def _heads(x):
            b, s, _ = x.shape
            return x.reshape(b, s, H, HD).transpose(0, 2, 1, 3)
        q = _heads(query @ Wq.T)
        k = _heads(key @ Wk.T)
        v = _heads(value @ Wv.T)
        logits = jnp.einsum('bhqd,bhkd->bhqk', q, k) * SCALE
        mask = attn_mask[None, None, :, :]
        masked = jnp.where(mask, logits, -1000000000.0)
        weights = jax.nn.softmax(masked, axis=-1)
        weights = weights * mask.astype(weights.dtype)
        denom = jnp.maximum(weights.sum(axis=-1, keepdims=True), 1e-09)
        weights = weights / denom
        out = jnp.einsum('bhqk,bhkd->bhqd', weights, v)
        out = out.transpose(0, 2, 1, 3).reshape(query.shape[0], query.shape[1], -1)
        return out @ Wo.T

    def _L1_ffn_ref(x, Wfc_s, bfc_s, Wproj_s, bproj_s, Wr, Wfc, bfc, Wproj, bproj):
        import jax, jax.numpy as jnp
        import numpy as np
        import math
        N_EMBD = 256
        HIDDEN = 4 * N_EMBD
        N_EXPERTS = 8
        TOP_K = 2
        B, T = (4, 512)

        def new_gelu(x):
            c = math.sqrt(2.0 / math.pi)
            return 0.5 * x * (1.0 + jnp.tanh(c * (x + 0.044715 * x * x * x)))

        def _moe_forward(x, Wfc_s, bfc_s, Wproj_s, bproj_s, Wr, Wfc, bfc, Wproj, bproj):
            Bb, Tt, C = x.shape
            xf = x.reshape(Bb * Tt, C)
            N = Bb * Tt
            shared = new_gelu(xf @ Wfc_s + bfc_s) @ Wproj_s + bproj_s
            logits = xf @ Wr
            probs = jax.nn.softmax(logits, axis=-1)
            topk_p, topk_i = jax.lax.top_k(probs, TOP_K)
            topk_p = topk_p / jnp.sum(topk_p, axis=-1, keepdims=True)
            gate = jnp.zeros((N, N_EXPERTS), dtype=xf.dtype)
            gate = gate.at[jnp.arange(N)[:, None], topk_i].add(topk_p)
            routed = jnp.zeros_like(xf)
            for e in range(N_EXPERTS):
                h = new_gelu(xf @ Wfc[e] + bfc[e]) @ Wproj[e] + bproj[e]
                routed = routed + h * gate[:, e:e + 1]
            return (shared + routed).reshape(Bb, Tt, C)
        return _moe_forward(x, Wfc_s, bfc_s, Wproj_s, bproj_s, Wr, Wfc, bfc, Wproj, bproj)
    x = x + _L0_xattn_ref(_layernorm(x, axis=-1), ctx_1024, ctx_1024, fside_Bx16xSxS2_0, fside_Bx16xSxS2_0, mask_BxS2_bf0, fside_SxS2_0, L0_xattn_Wq, L0_xattn_bq, L0_xattn_Wk, L0_xattn_bk, L0_xattn_Wv, L0_xattn_bv, L0_xattn_Wo, L0_xattn_bo)
    x = x + _L0_ffn_ref(_layernorm(x, axis=-1), L0_ffn_gate_w, L0_ffn_w1, L0_ffn_b1, L0_ffn_w2, L0_ffn_b2)
    x = x + _L1_xattn_ref(_layernorm(x, axis=-1), ctx_1024, ctx_1024, mask_SxS2_bk0, L1_xattn_Wq, L1_xattn_Wk, L1_xattn_Wv, L1_xattn_Wo)
    x = x + _L1_ffn_ref(_layernorm(x, axis=-1), L1_ffn_Wfc_s, L1_ffn_bfc_s, L1_ffn_Wproj_s, L1_ffn_bproj_s, L1_ffn_Wr, L1_ffn_Wfc, L1_ffn_bfc, L1_ffn_Wproj, L1_ffn_bproj)
    return x

_drawn_inputs = setup_inputs


def setup_inputs(seed=0):
    import zlib

    import numpy as np

    out = dict(_drawn_inputs(seed))
    spreads = {'L0_xattn_bq': (0.0, 0.1),
     'L0_xattn_bk': (0.0, 0.8),
     'L0_xattn_bv': (0.0, 0.1),
     'L0_xattn_bo': (0.0, 0.1),
     'L0_ffn_b1': (0.0, 0.339),
     'L0_ffn_b2': (0.0, 0.1),
     'L1_ffn_bfc_s': (0.0, 0.482),
     'L1_ffn_bproj_s': (0.0, 0.1),
     'L1_ffn_bfc': (0.0, 0.727),
     'L1_ffn_bproj': (0.0, 0.1)}
    factors = {}
    for name, (base, spread) in spreads.items():
        noise = np.random.default_rng([zlib.crc32(name.encode()), seed]).standard_normal(out[name].shape)
        drawn = base * np.exp(spread * noise) if base else spread * noise
        out[name] = jnp.asarray(drawn.astype(out[name].dtype))
    for name, factor in factors.items():
        out[name] = (out[name] * factor).astype(out[name].dtype)
    return out
```

```python
from contextlib import ExitStack

import concourse.bass as bass
from concourse import mybir

F32 = mybir.dt.float32
I32 = mybir.dt.int32
U32 = mybir.dt.uint32
U8 = mybir.dt.uint8
ALU = mybir.AluOpType
ACT = mybir.ActivationFunctionType
AX = mybir.AxisListType

P = 128
B = 16
D = 256
DC = D // P
H = 16
HD = D // H
HG = 4
NG = H // HG
VW = 2 * HD
BIG = 3.0e38
EPS = 1e-5
TOPK = 2


def max_slots(experts):
    return (TOPK * B * P + experts * (P - 1)) // P


class Moe:

    def __init__(self, layer, experts, hidden, w1, w2, b2, act):
        self.layer, self.E, self.F, self.w1, self.w2, self.b2, self.act = layer, experts, hidden, w1, w2, b2, act
        self.FC = hidden // P
        self.slots = max_slots(experts)


def bcast(ap, shape):
    return ap.to_broadcast(shape)


def build(nc, a, out):
    with ExitStack() as top:
        top.enter_context(nc.allow_non_contiguous_dma(reason="small tables of the router"))
        names, phase_sems = [0], []

        def sem(name):
            names[0] += 1
            phase_sems.append(nc.alloc_semaphore(f"{name}_{names[0]}"))
            return phase_sems[-1]

        def end_phase():
            nc.clear_and_free_semaphores(phase_sems)
            phase_sems.clear()
            nc.all_engine_barrier()

        def alloc(stack):
            def sb(name, shape, dt=F32):
                names[0] += 1
                return stack.enter_context(nc.sbuf_tensor(f"{name}_{names[0]}", shape, dt))
            return sb

        sb = alloc(top)
        c = {}
        c["X"] = sb("X", [P, B, D])
        c["Hn"] = sb("Hn", [P, B, D])
        c["ST"] = sb("ST", [P, B, 6])
        c["MV"] = sb("MV", [P, B, 2])
        c["rstd"] = sb("rstd", [P, B])
        c["nmr"] = sb("nmr", [P, B])
        c["eps"] = sb("eps", [P, 1])
        c["ident"] = sb("ident", [P, P])
        c["before"] = sb("before", [P, P])
        c["ones"] = sb("ones", [P, P])
        c["WT"] = sb("WT", [P, 8, DC, D])
        c["vecT0"] = sb("vecT0", [P, 60])
        c["vecT1"] = sb("vecT1", [P, 72])
        c["bqs"] = sb("bqs", [P, DC])
        c["bv"] = sb("bv", [P, D])
        c["bo"] = sb("bo", [P, D])
        c["bps"] = sb("bps", [P, D])
        c["gT0"] = sb("gT0", [P, DC, 14])
        c["gT1"] = sb("gT1", [P, DC, 8])
        c["hmask"] = sb("hmask", [P, 8])
        c["M1"] = sb("M1", [P, P])
        c["rowany"] = sb("rowany", [P, 1])
        c["xg"] = nc.dram_tensor("slot_rows", (max_slots(14) * P, D), F32, kind="Internal").ap()
        c["yg"] = nc.dram_tensor("slot_outputs", (max_slots(14) * P, D), F32, kind="Internal").ap()

        moe0 = Moe(0, 14, 512, a["L0_ffn_w1"], a["L0_ffn_w2"], a["L0_ffn_b2"], ACT.Gelu)
        moe1 = Moe(1, 8, 1024, a["L1_ffn_Wfc"], a["L1_ffn_Wproj"], a["L1_ffn_bproj"], ACT.Gelu_apprx_tanh)
        setup(nc, sem, alloc, a, c)
        end_phase()
        attention(nc, sem, alloc, a, c, 0)
        end_phase()
        for moe in (moe0, moe1):
            if moe.layer == 1:
                attention(nc, sem, alloc, a, c, 1)
                end_phase()
            with ExitStack() as keep:
                r = route(nc, sem, alloc, alloc(keep), a, c, moe)
                end_phase()
                if moe.layer == 1:
                    shared_expert(nc, sem, alloc, a, c, moe, r)
                    end_phase()
                experts(nc, sem, alloc, a, c, moe, r)
                end_phase()
                combine(nc, sem, alloc, a, c, moe, r, out)
                end_phase()


def setup(nc, sem, alloc, a, c):
    with ExitStack() as stack:
        sb = alloc(stack)
        wst = sb("wst", [P, 8, DC, D])
        vec0 = sb("vec0", [60, P])
        vec1 = sb("vec1", [72, P])
        gst = sb("gst", [14, D])
        m1u = sb("m1u", [P, P], U8)
        m1f = sb("m1f", [P, P])
        zeros = sb("zeros", [P, D])
        bank = [stack.enter_context(nc.psum_tensor(f"setup_bank{i}", [P, 512], F32)) for i in range(8)]
        loaded_x, loaded_w, loaded_small = sem("loaded_x"), sem("loaded_w"), sem("loaded_small")
        zeros_ready, slots_zeroed = sem("zeros_ready"), sem("slots_zeroed")
        made, ident_ready, transposed, evacuated, step = (
            sem("made"), sem("ident_ready"), sem("transposed"), sem("evacuated"), sem("dve_step"))
        mats = [a[f"L{l}_xattn_{w}"] for l in range(2) for w in ("Wq", "Wk", "Wv", "Wo")]
        block = stack.enter_context(nc.Block())

        @block.sync
        def _(sp):
            for m, w in enumerate(mats):
                sp.dma_start(wst[:, m], w.rearrange("(c p) i -> p c i", p=P)).then_inc(loaded_w, 16)
            sp.dma_start(c["X"][:], a["x"].rearrange("b t d -> t b d")).then_inc(loaded_x, 16)
            sp.wait_ge(zeros_ready, 1)
            rows = c["xg"].shape[0] // P
            sp.dma_start(c["xg"].rearrange("(p r) d -> p r d", p=P),
                         bcast(zeros[:].rearrange("p (r d) -> p r d", r=1), [P, rows, D])).then_inc(slots_zeroed, 16)
            sp.wait_ge(slots_zeroed, 16)

        @block.scalar
        def _(act):
            small = [
                (vec0[0:2], a["L0_xattn_bq"].rearrange("(c p) -> c p", p=P)),
                (vec0[2:4], a["L0_xattn_bk"].rearrange("(c p) -> c p", p=P)),
                (vec0[4:60], a["L0_ffn_b1"].rearrange("e (c p) -> (e c) p", p=P)),
                (vec1[0:64], a["L1_ffn_bfc"].rearrange("e (c p) -> (e c) p", p=P)),
                (vec1[64:72], a["L1_ffn_bfc_s"].rearrange("(c p) -> c p", p=P)),
                (gst[:], a["L0_ffn_gate_w"]),
                (c["gT1"][:], a["L1_ffn_Wr"].rearrange("(c p) e -> p c e", p=P)),
                (c["bv"][:], bcast(a["L0_xattn_bv"].rearrange("(o d) -> o d", o=1), [P, D])),
                (c["bo"][:], bcast(a["L0_xattn_bo"].rearrange("(o d) -> o d", o=1), [P, D])),
                (c["bps"][:], bcast(a["L1_ffn_bproj_s"].rearrange("(o d) -> o d", o=1), [P, D])),
                (m1u[:], a["mask_SxS2_bk0"]),
            ]
            for to, of in small:
                act.dma_start(to, of).then_inc(loaded_small, 16)

        @block.gpsimd
        def _(pool):
            pool.memset(zeros[:], 0.0).then_inc(zeros_ready, 1)
            pool.memset(c["ident"][:], 0.0)
            pool.memset(c["before"][:], 0.0)
            pool.memset(c["ones"][:], 1.0)
            pool.memset(c["eps"][:], EPS)
            pool.memset(c["hmask"][:], 1.0).then_inc(made, 1)
            pool.wait_ge(made, 1)
            pool.affine_select(out=c["ident"][:], in_=c["ident"][:], compare_op=ALU.not_equal, fill=1.0,
                               base=0, pattern=[[-1, P]], channel_multiplier=1).then_inc(ident_ready, 1)
            pool.affine_select(out=c["before"][:], in_=c["before"][:], compare_op=ALU.is_ge, fill=1.0,
                               base=0, pattern=[[-1, P]], channel_multiplier=1)
            pool.affine_select(out=c["hmask"][:], in_=c["hmask"][:], compare_op=ALU.is_ge, fill=0.0,
                               base=0, pattern=[[-HD, 8]], channel_multiplier=1).then_inc(made, 1)
            pool.wait_ge(made, 2)
            pool.affine_select(out=c["hmask"][:], in_=c["hmask"][:], compare_op=ALU.is_ge, fill=0.0,
                               base=HD - 1, pattern=[[HD, 8]], channel_multiplier=-1).then_inc(made, 1)

        @block.tensor
        def _(pe):
            pe.wait_ge(ident_ready, 1)
            pe.wait_ge(loaded_w, 16 * len(mats))
            for m in range(8):
                if m >= 5:
                    pe.wait_ge(evacuated, m - 4)
                for ci in range(DC):
                    for co in range(DC):
                        last = pe.transpose(bank[m % 5][:, (ci * DC + co) * P:(ci * DC + co + 1) * P],
                                            wst[:, m, co, ci * P:(ci + 1) * P], c["ident"][:])
                last.then_inc(transposed, 1)
            pe.wait_ge(loaded_small, 16 * 11)
            pe.transpose(bank[5][:, 0:60], vec0[:], c["ident"][0:60, 0:60]).then_inc(transposed, 1)
            pe.transpose(bank[6][:, 0:72], vec1[:], c["ident"][0:72, 0:72]).then_inc(transposed, 1)
            for ci in range(DC):
                last = pe.transpose(bank[7][:, ci * 14:(ci + 1) * 14], gst[:, ci * P:(ci + 1) * P],
                                    c["ident"][0:14, 0:14])
            last.then_inc(transposed, 1)

        @block.vector
        def _(dve):
            for m in range(8):
                dve.wait_ge(transposed, m + 1)
                dve.tensor_copy(c["WT"][:, m].rearrange("p c o -> p (c o)"), bank[m % 5][:]).then_inc(evacuated, 1)
            dve.wait_ge(transposed, 9)
            dve.tensor_copy(c["vecT0"][:], bank[5][:, 0:60])
            dve.tensor_scalar(c["bqs"][:], bank[5][:, 0:DC], 0.5 * HD ** -0.5, None, ALU.mult)
            dve.wait_ge(transposed, 10)
            dve.tensor_copy(c["vecT1"][:], bank[6][:, 0:72])
            dve.wait_ge(transposed, 11)
            dve.tensor_copy(c["gT0"][:].rearrange("p c e -> p (c e)"), bank[7][:, 0:DC * 14])
            dve.wait_ge(loaded_small, 16 * 11)
            dve.tensor_copy(m1f[:], m1u[:]).then_inc(step, 1)
            dve.wait_ge(step, 1)
            dve.tensor_scalar(c["M1"][:], m1f[:], 1.0e9, -1.0e9, ALU.mult, ALU.add)
            dve.tensor_reduce(c["rowany"][:], m1f[:], AX.X, ALU.max)
            dve.wait_ge(loaded_x, 16)
            for b in range(B):
                dve.bn_stats(c["ST"][:, b], c["X"][:, b])


def ln_scales(nc, c, dve, act_in, act_out, step):
    for b in range(B):
        last = dve.bn_aggr(c["MV"][:, b], c["ST"][:, b])
    last.then_inc(act_in, 1)
    dve.wait_ge(act_out, 1)
    dve.reciprocal(c["rstd"][:], c["nmr"][:]).then_inc(step, 1)
    dve.wait_ge(step, 1)
    dve.scalar_tensor_tensor(c["nmr"][:], c["MV"][:, :, 0], -1.0, c["rstd"][:], ALU.mult, ALU.mult).then_inc(step, 1)
    dve.wait_ge(step, 2)


def ln_sqrt(nc, c, act, act_in, act_out):
    act.wait_ge(act_in, 1)
    act.activation(c["nmr"][:], c["MV"][:, :, 1], ACT.Sqrt, bias=c["eps"][:, 0:1]).then_inc(act_out, 1)


def attention(nc, sem, alloc, a, c, layer):
    with ExitStack() as stack:
        sb = alloc(stack)
        two = range(2)
        ctx_sb = [sb(f"ctx{i}", [P, D]) for i in two]
        xn = [sb(f"xn{i}", [P, D]) for i in two]
        xcT = [sb(f"xcT{i}", [P, 2 * DC, P]) for i in two]
        qT = [sb(f"qT{i}", [P, DC, P]) for i in two]
        kblk = [sb(f"kblk{i}", [P, DC, 8, P]) for i in two]
        vaug = [sb(f"vaug{i}", [P, H, VW]) for i in two]
        U = sb("U", [P, H, P])
        E_ = sb("E", [P, H, P])
        ET = sb("ET", [P, H, P])
        mx = [sb(f"mx{i}", [P, H]) for i in two]
        nmx = [sb(f"nmx{i}", [P, H]) for i in two]
        oT = sb("oT", [P, NG, P])
        rz = sb("rz", [P, H])
        on = sb("on", [P, D])
        onT = sb("onT", [P, DC, P])
        xo = sb("xo", [P, D])
        gate = sb("gate", [P, 1])
        bank = [stack.enter_context(nc.psum_tensor(f"attn{layer}_bank{i}", [P, 512], F32)) for i in range(8)]
        IN, QK, V, S, TE, O = bank[0], bank[1], bank[2], bank[3:5], bank[5:7], bank[7]
        if layer == 0:
            fs = [sb(f"fs{i}", [P, H, P]) for i in two]
            amb = sb("amb", [P, B, P])
            padu = sb("padu", [P, B, P], U8)
            amh = sb("amh", [P, P])
        wq, wk, wv, wo = (c["WT"][:, 4 * layer + i] for i in range(4))
        scale, twice = (0.5 * HD ** -0.5, 2.0) if layer == 0 else (HD ** -0.5, 1.0)

        ctx_loaded = [sem(f"ctx_loaded{i}") for i in two]
        fs_loaded = [sem(f"fs_loaded{i}") for i in two]
        small_loaded, amh_ready = sem("small_loaded"), sem("amh_ready")
        amb_ready, vones_ready = sem("amb_ready"), sem("vones_ready")
        std_in, std_out, ln_step = sem("std_in"), sem("std_out"), sem("ln_step")
        xn_ready = sem("xn_ready")
        bias_ready = sem("bias_ready")
        in_done = sem("in_done")
        xcT_ready = sem("xcT_ready")
        qk_done, v_done = sem("qk_done"), sem("v_done")
        qT_ready = sem("qT_ready")
        kblk_ready = sem("kblk_ready")
        v_ready = sem("v_ready")
        s_done = sem("s_done")
        mx_step = sem("mx_step")
        mx_ready = sem("mx_ready")
        e_ready = sem("e_ready")
        et_done = sem("et_done")
        eT_ready = sem("eT_ready")
        o_done = sem("o_done")
        oT_ready = sem("oT_ready")
        ob_done = sem("ob_done")
        rz_step = sem("rz_step")
        on_ready = sem("on_ready")
        onT_done, onT_ready = sem("onT_done"), sem("onT_ready")
        wo_done = sem("wo_done")
        xo_step = sem("xo_step")
        x_ready = sem("x_ready")
        rz_per_tile = 1 + layer
        block = stack.enter_context(nc.Block())

        def tiles(eng, tile):
            for b in range(4):
                tile(b, b % 2, b // 2)
            with eng.Fori(0, 5) as i:
                tile(i * 2 + 4, 0, i + 2)
                tile(i * 2 + 5, 1, i + 2)
            for b in range(B - 2, B):
                tile(b, b % 2, b // 2)

        @block.sync
        def _(sp):
            if layer == 0:
                pad = a["mask_BxS2_bf0"].rearrange("b s -> (b s)").rearrange("(o n) -> o n", o=1)
                sp.dma_start(padu[:].rearrange("p b s -> p (b s)"), bcast(pad, [P, B * P])).then_inc(small_loaded, 16)
                sp.dma_start(amh[:], a["fside_SxS2_0"]).then_inc(small_loaded, 16)

            def tile(b, par, k):
                if after(b, 2):
                    sp.wait_ge(in_done, b - 1)
                sp.dma_start(ctx_sb[par][:], a["ctx_1024"][b]).then_inc(ctx_loaded[par], 16)
                if layer == 0:
                    if after(b, 2):
                        sp.wait_ge(mx_ready, NG * (b - 1))
                    for half in two:
                        heads = slice(8 * half, 8 * half + 8)
                        sp.dma_start(fs[par][:, heads], a["fside_Bx16xSxS2_0"][b].rearrange("h t s -> t h s")[:, heads]
                                     ).then_inc(fs_loaded[par], 16)
            tiles(sp, tile)

        @block.gpsimd
        def _(pool):
            for i in two:
                pool.memset(vaug[i][:], 1.0).then_inc(vones_ready, 1)
            if layer == 0:
                pool.wait_ge(amb_ready, 1)

                def tile(b, par, k):
                    pool.wait_ge(fs_loaded[par], 32 * k + 32)
                    pool.tensor_tensor(fs[par][:], fs[par][:], bcast(amb[:, b:b + 1], [P, H, P]) if isinstance(b, int)
                                       else bcast(amb[:, bass.ds(b, 1)], [P, H, P]), ALU.add).then_inc(bias_ready, 1)
                tiles(pool, tile)

        @block.tensor
        def _(pe):
            def bring(b, par, k):
                pe.wait_ge(xn_ready, b + 1)
                pe.wait_ge(ctx_loaded[par], 16 * k + 16)
                if after(b, 3):
                    pe.wait_ge(on_ready, b - 2)
                if after(b, 1):
                    pe.wait_ge(xcT_ready, b)
                for i in range(DC):
                    pe.transpose(IN[:, i * P:(i + 1) * P], xn[par][:, i * P:(i + 1) * P], c["ident"][:])
                for i in range(DC):
                    last = pe.transpose(IN[:, (DC + i) * P:(DC + i + 1) * P], ctx_sb[par][:, i * P:(i + 1) * P],
                                        c["ident"][:])
                last.then_inc(in_done, 1)

            def project_qk(b, par):
                pe.wait_ge(xcT_ready, b + 1)
                if after(b, 1):
                    pe.wait_ge(qT_ready, b)
                    pe.wait_ge(kblk_ready, b)
                if after(b, 3):
                    pe.wait_ge(onT_ready, b - 2)
                for j, w in enumerate((wq, wk)):
                    for co in range(DC):
                        for ci in range(DC):
                            last = pe.matmul(QK[:, (j * DC + co) * P:(j * DC + co + 1) * P],
                                             w[:, ci, co * P:(co + 1) * P], xcT[par][:, j * DC + ci],
                                             start=(ci == 0), stop=(ci == DC - 1))
                last.then_inc(qk_done, 1)

            def project_v(b, par):
                if after(b, 1):
                    pe.wait_ge(v_ready, b)
                if after(b, 3):
                    pe.wait_ge(x_ready, b - 2)
                for ci in range(DC):
                    last = pe.matmul(V[:, 0:D], xcT[par][:, DC + ci], wv[:, ci], start=(ci == 0), stop=(ci == DC - 1))
                last.then_inc(v_done, 1)

            def scores(b, par, g):
                if g == 0:
                    pe.wait_ge(qT_ready, b + 1)
                    pe.wait_ge(kblk_ready, b + 1)
                if after(b, 1) or g >= 2:
                    pe.wait_ge(mx_ready, NG * b + g - 1)
                ch, lo = g // 2, (g % 2) * HG
                pe.matmul(S[g % 2][:], qT[par][:, ch],
                          kblk[par][:, ch, lo:lo + HG].rearrange("p h s -> p (h s)"),
                          start=True, stop=True).then_inc(s_done, 1)

            def turn_e(b, g):
                pe.wait_ge(e_ready, NG * b + g + 1)
                if after(b, 1) or g >= 2:
                    pe.wait_ge(eT_ready, NG * b + g - 1)
                for j in range(HG):
                    last = pe.transpose(TE[g % 2][:, j * P:(j + 1) * P], E_[:, HG * g + j], c["ident"][:])
                last.then_inc(et_done, 1)

            def outputs(b, par, g):
                if g == 0:
                    pe.wait_ge(v_ready, b + 1)
                    if after(b, 1):
                        pe.wait_ge(oT_ready, b)
                pe.wait_ge(eT_ready, NG * b + g + 1)
                for j in range(HG):
                    last = pe.matmul(O[VW * j:VW * j + VW, g * P:(g + 1) * P], vaug[par][:, HG * g + j],
                                     ET[:, HG * g + j], start=True, stop=True)
                last.then_inc(o_done, 1)

            def turn_back(b):
                pe.wait_ge(oT_ready, b + 1)
                if upto(b, B - 3):
                    pe.wait_ge(xcT_ready, b + 3)
                if after(b, 1):
                    pe.wait_ge(on_ready, b)
                for g in range(NG):
                    last = pe.transpose(IN[:, g * P:(g + 1) * P], oT[:, g], c["ident"][:])
                last.then_inc(ob_done, 1)

            def turn_out(b):
                pe.wait_ge(on_ready, b + 1)
                if upto(b, B - 3):
                    pe.wait_ge(kblk_ready, b + 3)
                if after(b, 1):
                    pe.wait_ge(onT_ready, b)
                for i in range(DC):
                    last = pe.transpose(QK[:, i * P:(i + 1) * P], on[:, i * P:(i + 1) * P], c["ident"][:])
                last.then_inc(onT_done, 1)

            def project_out(b):
                pe.wait_ge(onT_ready, b + 1)
                if upto(b, B - 3):
                    pe.wait_ge(v_ready, b + 3)
                if after(b, 1):
                    pe.wait_ge(x_ready, b)
                for ci in range(DC):
                    last = pe.matmul(V[:, 0:D], onT[:, ci], wo[:, ci], start=(ci == 0), stop=(ci == DC - 1))
                last.then_inc(wo_done, 1)

            def tile(b, par, k):
                nxt = upto(b, B - 2)
                nk = (b + 1) // 2 if isinstance(b, int) else (k if par == 0 else k + 1)
                scores(b, par, 0)
                if nxt:
                    bring(b + 1, 1 - par, nk)
                if after(b, 1):
                    turn_e(b - 1, 3)
                if after(b, 2):
                    project_out(b - 2)
                if after(b, 1):
                    outputs(b - 1, 1 - par, 2)
                scores(b, par, 1)
                if nxt:
                    project_qk(b + 1, 1 - par)
                if after(b, 1):
                    outputs(b - 1, 1 - par, 3)
                turn_e(b, 0)
                scores(b, par, 2)
                if after(b, 1):
                    turn_back(b - 1)
                if nxt:
                    project_v(b + 1, 1 - par)
                turn_e(b, 1)
                outputs(b, par, 0)
                scores(b, par, 3)
                turn_e(b, 2)
                outputs(b, par, 1)
                if after(b, 1):
                    turn_out(b - 1)

            bring(0, 0, 0)
            project_qk(0, 0)
            project_v(0, 0)
            tiles(pe, tile)
            last_par = (B - 1) % 2
            turn_e(B - 1, 3)
            project_out(B - 2)
            outputs(B - 1, last_par, 2)
            outputs(B - 1, last_par, 3)
            turn_back(B - 1)
            turn_out(B - 1)
            project_out(B - 1)

        @block.scalar
        def _(act):
            ln_sqrt(nc, c, act, std_in, std_out)

            def q_out(b, par):
                act.wait_ge(qk_done, b + 1)
                if after(b, 2):
                    act.wait_ge(s_done, NG * (b - 1))
                for ch in range(DC):
                    if layer == 0:
                        last = act.activation(qT[par][:, ch], QK[:, ch * P:(ch + 1) * P], ACT.Identity,
                                              bias=c["bqs"][:, ch:ch + 1], scale=scale)
                    else:
                        last = act.activation(qT[par][:, ch], QK[:, ch * P:(ch + 1) * P], ACT.Copy, scale=scale)
                last.then_inc(qT_ready, 1)

            def exps(b, par, g):
                act.wait_ge(mx_ready, NG * b + g + 1)
                if after(b, 1):
                    act.wait_ge(et_done, NG * (b - 1) + g + 1)
                for h in range(HG * g, HG * g + HG):
                    last = act.activation(E_[:, h], U[:, h], ACT.Exp, bias=nmx[par][:, h:h + 1], scale=twice)
                last.then_inc(e_ready, 1)

            def et_out(b, g):
                act.wait_ge(et_done, NG * b + g + 1)
                if after(b, 1):
                    act.wait_ge(o_done, NG * (b - 1) + g + 1)
                act.activation(ET[:, HG * g:HG * g + HG].rearrange("p h t -> p (h t)"), TE[g % 2][:],
                               ACT.Copy).then_inc(eT_ready, 1)

            def o_out(b):
                act.wait_ge(o_done, NG * b + NG)
                if after(b, 1):
                    act.wait_ge(ob_done, b)
                act.activation(oT[:].rearrange("p g t -> p (g t)"), O[:], ACT.Copy).then_inc(oT_ready, 1)

            def tile(b, par, k):
                exps(b, par, 0)
                if after(b, 1):
                    et_out(b - 1, 3)
                exps(b, par, 1)
                if upto(b, B - 2):
                    q_out(b + 1, 1 - par)
                if after(b, 1):
                    o_out(b - 1)
                et_out(b, 0)
                exps(b, par, 2)
                et_out(b, 1)
                exps(b, par, 3)
                et_out(b, 2)

            q_out(0, 0)
            tiles(act, tile)
            et_out(B - 1, 3)
            o_out(B - 1)

        @block.vector
        def _(dve):
            if layer == 0:
                dve.wait_ge(small_loaded, 32)
                dve.tensor_scalar(amh[:], amh[:], 0.5, None, ALU.mult).then_inc(amh_ready, 1)
                dve.tensor_scalar(amb[:], padu[:], -BIG, 10.0, ALU.mult, ALU.mult).then_inc(amh_ready, 1)
                dve.wait_ge(amh_ready, 2)
                dve.tensor_tensor(amb[:], amb[:], bcast(amh[:].rearrange("p (o s) -> p o s", o=1), [P, B, P]),
                                  ALU.add).then_inc(amb_ready, 1)
            ln_scales(nc, c, dve, std_in, std_out, ln_step)
            dve.wait_ge(vones_ready, 2)

            def normed(b, par):
                if after(b, 2):
                    dve.wait_ge(in_done, b - 1)
                dve.tensor_scalar(xn[par][:], c["X"][:, b], c["rstd"][:, at(b)], c["nmr"][:, at(b)],
                                  ALU.mult, ALU.add).then_inc(xn_ready, 1)

            def in_out(b, par):
                dve.wait_ge(in_done, b + 1)
                if after(b, 2):
                    dve.wait_ge(v_done, b - 1)
                dve.tensor_copy(xcT[par][:].rearrange("p c t -> p (c t)"), IN[:]).then_inc(xcT_ready, 1)

            def k_out(b, par, ch):
                if ch == 0:
                    dve.wait_ge(qk_done, b + 1)
                    dve.wait_ge(qT_ready, b + 1)
                    if after(b, 2):
                        dve.wait_ge(s_done, NG * (b - 1))
                kt = bcast(QK[:, (DC + ch) * P:(DC + ch + 1) * P].rearrange("p (o s) -> p o s", o=1), [P, 8, P])
                mask = bcast(c["hmask"][:].rearrange("p (h o) -> p h o", o=1), [P, 8, P])
                if layer == 0:
                    last = dve.scalar_tensor_tensor(kblk[par][:, ch], kt, c["vecT0"][:, 2 + ch:3 + ch], mask,
                                                    ALU.add, ALU.mult)
                else:
                    last = dve.tensor_tensor(kblk[par][:, ch], kt, mask, ALU.mult)
                if ch == DC - 1:
                    last.then_inc(kblk_ready, 1)

            def v_out(b, par):
                dve.wait_ge(v_done, b + 1)
                if after(b, 2):
                    dve.wait_ge(o_done, NG * (b - 1))
                to = vaug[par][:, :, 0:HD]
                of = V[:, 0:D].rearrange("p (h d) -> p h d", d=HD)
                if layer == 0:
                    dve.tensor_tensor(to, of, c["bv"][:].rearrange("p (h d) -> p h d", d=HD), ALU.add
                                      ).then_inc(v_ready, 1)
                else:
                    dve.tensor_copy(to, of).then_inc(v_ready, 1)

            def maxima(b, par, g):
                dve.wait_ge(s_done, NG * b + g + 1)
                if layer == 0 and g == 0:
                    dve.wait_ge(bias_ready, b + 1)
                if after(b, 1):
                    dve.wait_ge(e_ready, NG * (b - 1) + g + 1)
                dve.memset(gate[:], 0.0)
                for j in range(HG):
                    h = HG * g + j
                    last = dve.tensor_tensor_reduce(U[:, h], S[g % 2][:, j * P:(j + 1) * P],
                                                    fs[par][:, h] if layer == 0 else c["M1"][:],
                                                    1.0, -BIG, ALU.add, ALU.max, mx[par][:, h:h + 1])
                last.then_inc(mx_step, 1)
                dve.wait_ge(mx_step, NG * b + g + 1)
                dve.tensor_scalar(nmx[par][:, HG * g:HG * g + HG], mx[par][:, HG * g:HG * g + HG], -twice, None,
                                  ALU.mult).then_inc(mx_ready, 1)

            def divide(b):
                dve.wait_ge(ob_done, b + 1)
                if after(b, 1):
                    dve.wait_ge(onT_done, b)
                ob = IN[:].rearrange("p (h w) -> p h w", w=VW)
                dve.reciprocal(rz[:], ob[:, :, HD]).then_inc(rz_step, 1)
                dve.wait_ge(rz_step, b * rz_per_tile + 1)
                if layer == 1:
                    dve.tensor_scalar(rz[:], rz[:], c["rowany"][:, 0:1], None, ALU.mult).then_inc(rz_step, 1)
                    dve.wait_ge(rz_step, b * 2 + 2)
                dve.tensor_tensor(on[:].rearrange("p (h d) -> p h d", d=HD), ob[:, :, 0:HD],
                                  bcast(rz[:].rearrange("p (h o) -> p h o", o=1), [P, H, HD]), ALU.mult
                                  ).then_inc(on_ready, 1)

            def turned(b):
                dve.wait_ge(onT_done, b + 1)
                if after(b, 1):
                    dve.wait_ge(wo_done, b)
                dve.tensor_copy(onT[:].rearrange("p c t -> p (c t)"), QK[:, 0:D]).then_inc(onT_ready, 1)

            def residual(b):
                dve.wait_ge(wo_done, b + 1)
                if layer == 0:
                    dve.tensor_tensor(xo[:], V[:, 0:D], c["bo"][:], ALU.add).then_inc(xo_step, 1)
                else:
                    dve.tensor_copy(xo[:], V[:, 0:D]).then_inc(xo_step, 1)
                dve.wait_ge(xo_step, 2 * b + 1)
                dve.tensor_tensor(c["X"][:, b], c["X"][:, b], xo[:], ALU.add).then_inc(xo_step, 1)
                dve.wait_ge(xo_step, 2 * b + 2)
                dve.bn_stats(c["ST"][:, b], c["X"][:, b]).then_inc(x_ready, 1)
                dve.wait_ge(x_ready, b + 1)

            def tile(b, par, k):
                nxt = upto(b, B - 2)
                maxima(b, par, 0)
                if after(b, 2):
                    turned(b - 2)
                if nxt:
                    in_out(b + 1, 1 - par)
                maxima(b, par, 1)
                if after(b, 2):
                    residual(b - 2)
                if upto(b, B - 3):
                    normed(b + 2, par)
                if nxt:
                    k_out(b + 1, 1 - par, 0)
                maxima(b, par, 2)
                if after(b, 1):
                    divide(b - 1)
                if nxt:
                    k_out(b + 1, 1 - par, 1)
                    v_out(b + 1, 1 - par)
                maxima(b, par, 3)

            normed(0, 0)
            normed(1, 1)
            in_out(0, 0)
            k_out(0, 0, 0)
            k_out(0, 0, 1)
            v_out(0, 0)
            tiles(dve, tile)
            turned(B - 2)
            residual(B - 2)
            divide(B - 1)
            turned(B - 1)
            residual(B - 1)


def at(b):
    return slice(b, b + 1) if isinstance(b, int) else bass.ds(b, 1)


def after(b, n):
    return not isinstance(b, int) or b >= n


def upto(b, n):
    return not isinstance(b, int) or b <= n


def paired(eng, n, step, first=2):
    turns = (n - first - 2) // 2
    for i in range(first):
        step(i, i % 2, i // 2)
    with eng.Fori(0, turns) as i:
        step(i * 2 + first, 0, i + first // 2)
        step(i * 2 + first + 1, 1, i + first // 2)
    for i in range(first + 2 * turns, n):
        step(i, i % 2, i // 2)


def route(nc, sem, alloc, keep, a, c, moe):
    E, S, layer = moe.E, moe.slots, moe.layer
    r = {
        "w12": keep("w12", [P, B, 2]),
        "G": keep("G", [P, B, E]),
        "rows": keep("rows", [P, 2, B], I32),
        "expert": keep("expert", [P, S], I32),
        "b2": keep("b2", [E, D]),
    }
    with ExitStack() as stack:
        sb = alloc(stack)
        two = range(2)
        hb = [sb(f"hb{i}", [P, D]) for i in two]
        hT = [sb(f"hT{i}", [P, DC, P]) for i in two]
        LG = sb("LG", [P, B, E])
        top8 = sb("top8", [P, B, 8])
        ix8 = sb("ix8", [P, B, 8], U32)
        ixf = sb("ixf", [P, B, 2])
        hot = [sb(f"hot{j}", [P, B, E]) for j in two]
        both = sb("both", [P, B, E])
        diff = sb("diff", [P, B])
        e2 = sb("e2", [P, B])
        den = sb("den", [P, B])
        tmp = sb("tmp", [P, B, E])
        cnt = sb("cnt", [P, B, E])
        pre = sb("pre", [P, B + 1, E])
        over = sb("over", [P, E, B])
        nslot = sb("nslot", [P, E])
        first = sb("first", [P, E])
        base = sb("base", [P, E])
        pos = sb("pos", [P, B, E])
        rowf = sb("rowf", [P, 2, B])
        cmp = sb("cmp", [P, S, E - 1])
        expf = sb("expf", [P, S])
        iota_e = sb("iota_e", [P, E])
        iota_b = sb("iota_b", [P, B])
        iota_s = sb("iota_s", [P, S])
        bank = [stack.enter_context(nc.psum_tensor(f"route{layer}_bank{i}", [P, 512], F32)) for i in range(6)]
        gT = c[f"gT{layer}"]
        std_in, std_out, ln_step = sem("std_in"), sem("std_out"), sem("ln_step")
        h_ready = sem("h_ready")
        h_kept = sem("h_kept")
        hT_done = sem("hT_done")
        hT_ready = sem("hT_ready")
        lg_done = sem("lg_done")
        lg_ready = sem("lg_ready")
        iotas_ready = sem("iotas_ready")
        step = sem("dve_step")
        diff_ready, e2_ready, both_ready, ranks_done = sem("diff"), sem("e2"), sem("both"), sem("ranks")
        rows_ready, rows_sent, b2_loaded = sem("rows_ready"), sem("rows_sent"), sem("b2_loaded")
        block = stack.enter_context(nc.Block())

        @block.sync
        def _(sp):
            sp.dma_start(r["b2"][:], moe.b2).then_inc(b2_loaded, 16)
            sp.wait_ge(b2_loaded, 16)

        @block.scalar
        def _(act):
            ln_sqrt(nc, c, act, std_in, std_out)

            def tile(b, par, k):
                act.wait_ge(h_ready, b + 1)
                act.activation(c["Hn"][:, b], hb[par][:], ACT.Copy).then_inc(h_kept, 1)
            paired(act, B, tile)
            act.wait_ge(diff_ready, 1)
            act.activation(e2[:], diff[:], ACT.Exp).then_inc(e2_ready, 1)

        @block.tensor
        def _(pe):
            def turn(b, par):
                pe.wait_ge(h_ready, b + 1)
                if after(b, 2):
                    pe.wait_ge(hT_ready, b - 1)
                for i in range(DC):
                    last = pe.transpose(bank[par][:, i * P:(i + 1) * P], hb[par][:, i * P:(i + 1) * P], c["ident"][:])
                last.then_inc(hT_done, 1)

            def tile(b, par, k):
                pe.wait_ge(hT_ready, b + 1)
                if after(b, 2):
                    pe.wait_ge(lg_ready, b - 1)
                for i in range(DC):
                    last = pe.matmul(bank[2 + par][:, 0:E], hT[par][:, i], gT[:, i], start=(i == 0), stop=(i == DC - 1))
                last.then_inc(lg_done, 1)
                if upto(b, B - 3):
                    turn(b + 2, par)
            turn(0, 0)
            turn(1, 1)
            paired(pe, B, tile)
            pe.wait_ge(both_ready, 1)
            m = both[:].rearrange("p b e -> p (b e)")
            pe.matmul(bank[4][:, 0:B * E], c["before"][:], m, start=True, stop=True)
            pe.matmul(bank[5][:, 0:B * E], c["ones"][:], m, start=True, stop=True).then_inc(ranks_done, 1)

        @block.gpsimd
        def _(pool):
            pool.iota(iota_e[:], [[1, E]], base=0, channel_multiplier=0, allow_small_or_imprecise_dtypes=True)
            pool.iota(iota_b[:], [[P, B]], base=0, channel_multiplier=0, allow_small_or_imprecise_dtypes=True)
            pool.iota(iota_s[:], [[1, S]], base=0, channel_multiplier=0, allow_small_or_imprecise_dtypes=True
                      ).then_inc(iotas_ready, 1)
            if layer == 0:
                pool.wait_ge(h_kept, B)
                pool.wait_ge(rows_ready, 1)
                for b in range(B):
                    send_rows(pool, c, r, b, rows_sent)
                pool.wait_ge(rows_sent, 16 * TOPK * B)

        @block.vector
        def _(dve):
            ln_scales(nc, c, dve, std_in, std_out, ln_step)

            def normed(b, par):
                if after(b, 2):
                    dve.wait_ge(hT_done, b - 1)
                    dve.wait_ge(h_kept, b - 1)
                dve.tensor_scalar(hb[par][:], c["X"][:, b], c["rstd"][:, at(b)], c["nmr"][:, at(b)],
                                  ALU.mult, ALU.add).then_inc(h_ready, 1)

            def turned(b, par):
                dve.wait_ge(hT_done, b + 1)
                if after(b, 2):
                    dve.wait_ge(lg_done, b - 1)
                dve.tensor_copy(hT[par][:].rearrange("p c t -> p (c t)"), bank[par][:, 0:D]).then_inc(hT_ready, 1)

            def tile(b, par, k):
                if upto(b, B - 2):
                    turned(b + 1, 1 - par)
                if upto(b, B - 3):
                    normed(b + 2, par)
                dve.wait_ge(lg_done, b + 1)
                dve.tensor_copy(LG[:, b], bank[2 + par][:, 0:E]).then_inc(lg_ready, 1)
            normed(0, 0)
            normed(1, 1)
            turned(0, 0)
            paired(dve, B, tile)

            done = [0]

            def link(ins):
                done[0] += 1
                ins.then_inc(step, 1)
                dve.wait_ge(step, done[0])

            def col(ap, shape):
                return bcast(ap, shape)

            full = [P, B, E]
            dve.wait_ge(lg_ready, B)
            for b in range(B):
                last = dve.max(top8[:, b], LG[:, b])
            link(last)
            dve.tensor_tensor(diff[:], top8[:, :, 1], top8[:, :, 0], ALU.subtract).then_inc(diff_ready, 1)
            for b in range(B):
                last = dve.max_index(ix8[:, b], top8[:, b], LG[:, b])
            link(last)
            link(dve.tensor_copy(ixf[:], ix8[:, :, 0:2]))
            dve.wait_ge(iotas_ready, 1)
            ie = col(iota_e[:].rearrange("p (o e) -> p o e", o=1), full)
            for j in two:
                last = dve.tensor_tensor(hot[j][:], ie, col(ixf[:, :, j:j + 1], full), ALU.is_equal)
            link(last)
            dve.tensor_tensor(both[:], hot[0][:], hot[1][:], ALU.add).then_inc(both_ready, 1)
            dve.wait_ge(e2_ready, 1)
            link(dve.tensor_scalar(den[:], e2[:], 1.0, None, ALU.add))
            link(dve.reciprocal(r["w12"][:, :, 0], den[:]))
            link(dve.tensor_tensor(r["w12"][:, :, 1], r["w12"][:, :, 0], e2[:], ALU.mult))
            dve.tensor_tensor(tmp[:], hot[0][:], col(r["w12"][:, :, 0:1], full), ALU.mult)
            link(dve.tensor_tensor(r["G"][:], hot[1][:], col(r["w12"][:, :, 1:2], full), ALU.mult))
            link(dve.tensor_tensor(r["G"][:], r["G"][:], tmp[:], ALU.add))
            dve.memset(pre[:, 0], 0.0)
            dve.memset(first[:, 0:1], 0.0)
            dve.wait_ge(ranks_done, 1)
            link(dve.tensor_copy(cnt[:].rearrange("p b e -> p (b e)"), bank[5][:, 0:B * E]))
            for b in range(B):
                link(dve.tensor_tensor(pre[:, b + 1], pre[:, b], cnt[:, b], ALU.add))
            link(dve.tensor_tensor(over[:], col(pre[:, B].rearrange("p (e o) -> p e o", o=1), [P, E, B]),
                                   col(iota_b[:].rearrange("p (o b) -> p o b", o=1), [P, E, B]), ALU.is_gt))
            link(dve.tensor_reduce(nslot[:], over[:], AX.X, ALU.add))
            for e in range(1, E):
                link(dve.tensor_tensor(first[:, e:e + 1], first[:, e - 1:e], nslot[:, e - 1:e], ALU.add))
            link(dve.tensor_scalar(base[:], first[:], float(P), None, ALU.mult))
            link(dve.tensor_tensor(pos[:].rearrange("p b e -> p (b e)"), bank[4][:, 0:B * E],
                                   pre[:, 0:B].rearrange("p b e -> p (b e)"), ALU.add))
            link(dve.tensor_tensor(pos[:], pos[:], col(base[:].rearrange("p (o e) -> p o e", o=1), full), ALU.add))
            for j in two:
                link(dve.tensor_tensor(tmp[:], pos[:], hot[j][:], ALU.mult))
                link(dve.tensor_reduce(rowf[:, j], tmp[:], AX.X, ALU.add))
            dve.tensor_copy(r["rows"][:], rowf[:]).then_inc(rows_ready, 1)
            link(dve.tensor_tensor(cmp[:], col(iota_s[:].rearrange("p (s o) -> p s o", o=1), [P, S, E - 1]),
                                   col(first[:, 1:E].rearrange("p (o e) -> p o e", o=1), [P, S, E - 1]), ALU.is_ge))
            link(dve.tensor_reduce(expf[:], cmp[:], AX.X, ALU.add))
            dve.tensor_copy(r["expert"][:], expf[:])
    return r


def send_rows(pool, c, r, b, sent):
    for j in range(TOPK):
        pool.indirect_dma_start(out=c["xg"], out_offset=bass.IndirectOffsetOnAxis(
            ap=r["rows"][:, j, b:b + 1].bitcast(U32), axis=0), in_=c["Hn"][:, b], in_offset=None).then_inc(sent, 16)


def shared_expert(nc, sem, alloc, a, c, moe, r):
    weights = (a["L1_ffn_Wfc_s"], a["L1_ffn_Wproj_s"])
    expert_loop(nc, sem, alloc, c, moe, B, "shared", weights, r)


def experts(nc, sem, alloc, a, c, moe, r):
    expert_loop(nc, sem, alloc, c, moe, moe.slots, "routed", (moe.w1, moe.w2), r)


def expert_loop(nc, sem, alloc, c, moe, n_slots, kind, weights, r):
    routed = kind == "routed"
    FC, E = moe.FC, moe.E
    with ExitStack() as stack:
        sb = alloc(stack)
        two = range(2)
        nw = 2 if routed else 1
        w1 = [sb(f"w1_{i}", [P, DC, moe.F]) for i in range(nw)]
        w2 = [sb(f"w2_{i}", [P, FC, D]) for i in range(nw)]
        rows = [sb(f"rows{i}", [P, D]) for i in two]
        xT = [sb(f"xT{i}", [P, DC, P]) for i in two]
        hid = [sb(f"hid{i}", [P, FC, P]) for i in two]
        yb = [sb(f"yb{i}", [P, D]) for i in two]
        bank = [stack.enter_context(nc.psum_tensor(f"{kind}{moe.layer}_bank{i}", [P, 512], F32)) for i in range(8)]
        T, HB, Y = bank[0:2], bank[2:6], bank[6:8]
        w1_loaded = [sem(f"w1_loaded{i}") for i in two]
        w2_loaded = [sem(f"w2_loaded{i}") for i in two]
        rows_loaded = [sem(f"rows_loaded{i}") for i in two]
        rows_sent = sem("rows_sent")
        rows_copied = sem("rows_copied")
        xT_done = sem("xT_done")
        xT_ready = sem("xT_ready")
        hid_done = sem("hid_done")
        hid_ready = sem("hid_ready")
        y_done = sem("y_done")
        y_ready = sem("y_ready")
        y_step = sem("y_step")
        y_stored = [sem(f"y_stored{i}") for i in two]
        block = stack.enter_context(nc.Block())

        @block.sync
        def _(sp):
            if not routed:
                sp.dma_start(w1[0][:], weights[0].rearrange("(c p) f -> p c f", p=P)).then_inc(w1_loaded[0], 16)
                sp.dma_start(w2[0][:], weights[1].rearrange("(c p) d -> p c d", p=P)).then_inc(w2_loaded[0], 16)
                return

            def get(n, par):
                if after(n, 2):
                    sp.wait_ge(xT_done, n - 1)
                sp.dma_start(rows[par][:], row_block(c["xg"], n)).then_inc(rows_loaded[par], 16)

            def expert_of(n):
                return sp.value_load(r["expert"][0:1, at(n)], min_val=0, max_val=E - 1)

            def load(sem_, to, of, e):
                sp.dma_start(to[:], of[e].rearrange("(c p) f -> p c f", p=P)).then_inc(sem_, 16)

            def load_w2(n, par, e):
                if after(n, 2):
                    sp.wait_ge(y_done, n - 1)
                load(w2_loaded[par], w2[par], weights[1], e)

            def slot(n, par, k):
                e = expert_of(n)
                e_before = expert_of(n - 1) if after(n, 1) else None
                if after(n, 2):
                    sp.wait_ge(hid_done, FC * (n - 1))
                load(w1_loaded[par], w1[par], weights[0], e)
                if upto(n, n_slots - 2):
                    get(n + 1, 1 - par)
                if after(n, 1):
                    load_w2(n - 1, 1 - par, e_before)
            get(0, 0)
            paired(sp, n_slots, slot, 4)
            load_w2(n_slots - 1, (n_slots - 1) % 2, expert_of(n_slots - 1))

        @block.gpsimd
        def _(pool):
            def copy(n, par, k):
                if after(n, 2):
                    pool.wait_ge(xT_done, n - 1)
                pool.tensor_copy(rows[par][:], c["Hn"][:, n]).then_inc(rows_copied, 1)
                send_rows(pool, c, r, n, rows_sent)

            def store(n, par, k):
                pool.wait_ge(y_ready, n + 1)
                pool.dma_start(row_block(c["yg"], n), yb[par][:]).then_inc(y_stored[par], 16)
            if routed:
                paired(pool, n_slots, store)
            else:
                for n in range(B):
                    copy(n, n % 2, n // 2)
                pool.wait_ge(rows_sent, 16 * TOPK * B)
            if routed:
                for i in two:
                    pool.wait_ge(y_stored[i], 16 * ((n_slots + 1 - i) // 2))

        @block.tensor
        def _(pe):
            def turn(n, par, k):
                if routed:
                    pe.wait_ge(rows_loaded[par], 16 * k + 16)
                else:
                    pe.wait_ge(rows_copied, n + 1)
                if after(n, 2):
                    pe.wait_ge(xT_ready, n - 1)
                for i in range(DC):
                    last = pe.transpose(T[par][:, i * P:(i + 1) * P], rows[par][:, i * P:(i + 1) * P], c["ident"][:])
                last.then_inc(xT_done, 1)

            def up(n, par, k):
                pe.wait_ge(xT_ready, n + 1)
                if routed:
                    pe.wait_ge(w1_loaded[par], 16 * k + 16)
                else:
                    pe.wait_ge(w1_loaded[0], 16)
                w = w1[par if routed else 0]
                for f in range(FC):
                    if after(n, 1) or f >= 4:
                        pe.wait_ge(hid_ready, FC * n + f - 3)
                    for i in range(DC):
                        last = pe.matmul(HB[f % 4][:, 0:P], w[:, i, f * P:(f + 1) * P], xT[par][:, i],
                                         start=(i == 0), stop=(i == DC - 1))
                    last.then_inc(hid_done, 1)

            def down(n, par, k):
                if routed:
                    pe.wait_ge(w2_loaded[par], 16 * k + 16)
                else:
                    pe.wait_ge(w2_loaded[0], 16)
                if after(n, 2):
                    pe.wait_ge(y_ready, n - 1)
                w = w2[par if routed else 0]
                for f in range(FC):
                    pe.wait_ge(hid_ready, FC * n + f + 1)
                    last = pe.matmul(Y[par][:, 0:D], hid[par][:, f], w[:, f], start=(f == 0), stop=(f == FC - 1))
                last.then_inc(y_done, 1)

            def slot(n, par, k):
                if upto(n, n_slots - 2):
                    up(n + 1, 1 - par, (n + 1) // 2 if isinstance(n, int) else (k if par == 0 else k + 1))
                if upto(n, n_slots - 3):
                    turn(n + 2, par, k + 1)
                down(n, par, k)
            turn(0, 0, 0)
            turn(1, 1, 0)
            up(0, 0, 0)
            paired(pe, n_slots, slot)

        @block.scalar
        def _(act):
            def slot(n, par, k):
                if routed:
                    e = act.value_load(r["expert"][0:1, at(n)], min_val=0, max_val=E - 1)
                if after(n, 2):
                    act.wait_ge(y_done, n - 1)
                for f in range(FC):
                    if not routed:
                        bias = c["vecT1"][:, 64 + f:65 + f]
                    elif moe.layer == 0:
                        bias = c["vecT0"][:, bass.ds(e * FC + (4 + f), 1)]
                    else:
                        bias = c["vecT1"][:, bass.ds(e * FC + f, 1)]
                    act.wait_ge(hid_done, FC * n + f + 1)
                    act.activation(hid[par][:, f], HB[f % 4][:, 0:P], moe.act, bias=bias).then_inc(hid_ready, 1)
            paired(act, n_slots, slot)

        @block.vector
        def _(dve):
            def in_out(n, par):
                dve.wait_ge(xT_done, n + 1)
                if after(n, 2):
                    dve.wait_ge(hid_done, FC * (n - 1))
                dve.tensor_copy(xT[par][:].rearrange("p c t -> p (c t)"), T[par][:, 0:D]).then_inc(xT_ready, 1)

            def slot(n, par, k):
                if upto(n, n_slots - 3):
                    in_out(n + 2, par)
                dve.wait_ge(y_done, n + 1)
                if routed:
                    if after(n, 2):
                        dve.wait_ge(y_stored[par], 16 * k)
                    dve.tensor_copy(yb[par][:], Y[par][:, 0:D]).then_inc(y_ready, 1)
                else:
                    dve.tensor_tensor(yb[par][:], Y[par][:, 0:D], c["bps"][:], ALU.add).then_inc(y_ready, 1)
                    dve.wait_ge(y_ready, n + 1)
                    dve.tensor_tensor(c["X"][:, n], c["X"][:, n], yb[par][:], ALU.add).then_inc(y_step, 1)
                    dve.wait_ge(y_step, n + 1)
            in_out(0, 0)
            in_out(1, 1)
            paired(dve, n_slots, slot)


def row_block(rows, n):
    return rows.rearrange("(s p) d -> s p d", p=P)[n]


def combine(nc, sem, alloc, a, c, moe, r, out):
    E, layer = moe.E, moe.layer
    with ExitStack() as stack:
        sb = alloc(stack)
        two = range(2)
        y = [[sb(f"y{j}_{i}", [P, D]) for j in two] for i in two]
        gst = [sb(f"gst{i}", [P, E]) for i in two]
        gT = [sb(f"gTs{i}", [E, P]) for i in two]
        acc = [sb(f"acc{i}", [P, D]) for i in two]
        bank = [stack.enter_context(nc.psum_tensor(f"comb{layer}_bank{i}", [P, 512], F32)) for i in range(4)]
        GT, B2 = bank[0:2], bank[2:4]
        y_got = [sem(f"y_got{i}") for i in two]
        g_ready, gT_done, gT_ready, b2_done = sem("g_ready"), sem("gT_done"), sem("gT_ready"), sem("b2_done")
        acc_step = sem("acc_step")
        y_used = sem("y_used")
        x_ready, stored = sem("x_ready"), sem("stored")
        block = stack.enter_context(nc.Block())

        @block.gpsimd
        def _(pool):
            for b in range(B):
                if b >= 2:
                    pool.wait_ge(y_used, b - 1)
                for j in two:
                    pool.indirect_dma_start(out=y[b % 2][j][:], out_offset=None, in_=c["yg"],
                                            in_offset=bass.IndirectOffsetOnAxis(
                                                ap=r["rows"][:, j, b:b + 1].bitcast(U32), axis=0)
                                            ).then_inc(y_got[b % 2], 16)

        @block.tensor
        def _(pe):
            def tile(b, par, k):
                pe.wait_ge(g_ready, b + 1)
                if after(b, 2):
                    pe.wait_ge(gT_ready, b - 1)
                pe.transpose(GT[par][0:E, 0:P], gst[par][:], c["ident"][:]).then_inc(gT_done, 1)
                pe.wait_ge(gT_ready, b + 1)
                if after(b, 2):
                    pe.wait_ge(y_used, b - 1)
                pe.matmul(B2[par][:, 0:D], gT[par][:], r["b2"][:], start=True, stop=True).then_inc(b2_done, 1)
            paired(pe, B, tile)

        @block.scalar
        def _(act):
            def tile(b, par, k):
                act.wait_ge(gT_done, b + 1)
                if after(b, 2):
                    act.wait_ge(b2_done, b - 1)
                act.activation(gT[par][:], GT[par][0:E, 0:P], ACT.Copy).then_inc(gT_ready, 1)
            paired(act, B, tile)

        @block.vector
        def _(dve):
            ops = 4 + (layer == 0)

            def gates(b, par):
                if after(b, 2):
                    dve.wait_ge(gT_done, b - 1)
                dve.tensor_copy(gst[par][:], r["G"][:, b]).then_inc(g_ready, 1)

            def tile(b, par, k):
                if upto(b, B - 2):
                    gates(b + 1, 1 - par)
                t, at_step = acc[par], [0]

                def link(ins):
                    at_step[0] += 1
                    ins.then_inc(acc_step, 1)
                    dve.wait_ge(acc_step, b * ops + at_step[0])
                dve.wait_ge(b2_done, b + 1)
                if layer == 0:
                    link(dve.tensor_tensor(t[:], B2[par][:, 0:D], c["Hn"][:, b], ALU.add))
                else:
                    link(dve.tensor_copy(t[:], B2[par][:, 0:D]))
                dve.wait_ge(y_got[par], 32 * k + 32)
                for j in two:
                    w = r["w12"][:, at(b), j:j + 1].rearrange("p o j -> p (o j)")
                    link(dve.scalar_tensor_tensor(t[:], y[par][j][:], w, t[:], ALU.mult, ALU.add))
                if layer == 0:
                    link(dve.tensor_scalar(t[:], t[:], -100.0, 100.0, ALU.max, ALU.min))
                link(dve.tensor_tensor(c["X"][:, b], c["X"][:, b], t[:], ALU.add))
                dve.bn_stats(c["ST"][:, b], c["X"][:, b]).then_inc(y_used, 1)
            gates(0, 0)
            paired(dve, B, tile)

        @block.sync
        def _(sp):
            if layer == 1:
                def tile(b, par, k):
                    sp.wait_ge(y_used, b + 1)
                    sp.dma_start(out[b], c["X"][:, b]).then_inc(stored, 16)
                paired(sp, B, tile)
                sp.wait_ge(stored, 16 * B)


def kernel(**inputs):
    import numpy as _np
    import concourse.bacc as _bacc
    from concourse import mybir as _mybir
    from concourse.bass_utils import run_bass_kernel_spmd as _run

    nc = _bacc.Bacc("TRN2", target_bir_lowering=False, num_devices=1)
    arrays, args = {}, {}
    for name in inputs:
        v = _np.ascontiguousarray(inputs[name])
        arrays[f"in_{name}_dram"] = v
        args[name] = nc.dram_tensor(f"in_{name}_dram", v.shape, _mybir.dt.from_np(v.dtype), kind="ExternalInput").ap()
    out = nc.dram_tensor("out_0_dram", (B, P, D), F32, kind="ExternalOutput").ap()
    build(nc, args, out)
    r = _run(nc, [arrays], core_ids=[0])
    return r.results[0]["out_0_dram"]
```

```python
from contextlib import ExitStack

import concourse.bass as bass
from concourse import mybir

F32 = mybir.dt.float32
I32 = mybir.dt.int32
U32 = mybir.dt.uint32
U8 = mybir.dt.uint8
ALU = mybir.AluOpType
ACT = mybir.ActivationFunctionType
AX = mybir.AxisListType

P = 128
B = 16
D = 256
DC = D // P
H = 16
HD = D // H
HG = 4
NG = H // HG
VW = 2 * HD
BIG = 3.0e38
EPS = 1e-5
TOPK = 2


def max_slots(experts):
    return (TOPK * B * P + experts * (P - 1)) // P


class Moe:

    def __init__(self, layer, experts, hidden, w1, w2, b2, act):
        self.layer, self.E, self.F, self.w1, self.w2, self.b2, self.act = layer, experts, hidden, w1, w2, b2, act
        self.FC = hidden // P
        self.slots = max_slots(experts)


def bcast(ap, shape):
    return ap.to_broadcast(shape)


def build(nc, a, out):
    with ExitStack() as top:
        top.enter_context(nc.allow_non_contiguous_dma(reason="small tables of the router"))
        names, phase_sems = [0], []

        def sem(name):
            names[0] += 1
            phase_sems.append(nc.alloc_semaphore(f"{name}_{names[0]}"))
            return phase_sems[-1]

        def end_phase():
            nc.clear_and_free_semaphores(phase_sems)
            phase_sems.clear()
            nc.all_engine_barrier()

        def alloc(stack):
            def sb(name, shape, dt=F32):
                names[0] += 1
                return stack.enter_context(nc.sbuf_tensor(f"{name}_{names[0]}", shape, dt))
            return sb

        sb = alloc(top)
        c = {}
        c["X"] = sb("X", [P, B, D])
        c["Hn"] = sb("Hn", [P, B, D])
        c["ST"] = sb("ST", [P, B, 6])
        c["MV"] = sb("MV", [P, B, 2])
        c["rstd"] = sb("rstd", [P, B])
        c["nmr"] = sb("nmr", [P, B])
        c["mhalf"] = sb("mhalf", [P, B])
        for layer, experts_ in ((0, 14), (1, 8)):
            c[f"LG{layer}"] = sb(f"LG{layer}", [P, B, experts_])
        c["ident"] = sb("ident", [P, P])
        c["before"] = sb("before", [P, P])
        c["ones"] = sb("ones", [P, P])
        c["WT"] = sb("WT", [P, 8, DC, D])
        c["vecT0"] = sb("vecT0", [P, 60])
        c["vecT1"] = sb("vecT1", [P, 72])
        c["bqs"] = sb("bqs", [P, DC])
        c["bv"] = sb("bv", [P, D])
        c["bo"] = sb("bo", [P, D])
        c["gT0"] = sb("gT0", [P, DC, 14])
        c["gT1"] = sb("gT1", [P, DC, 8])
        c["hmask"] = sb("hmask", [P, 8])
        c["M1"] = sb("M1", [P, P])
        c["rowany"] = sb("rowany", [P, 1])
        c["xg"] = nc.dram_tensor("slot_rows", (max_slots(14) * P, D), F32, kind="Internal").ap()
        c["yg"] = nc.dram_tensor("slot_outputs", (max_slots(14) * P, D), F32, kind="Internal").ap()

        moe0 = Moe(0, 14, 512, a["L0_ffn_w1"], a["L0_ffn_w2"], a["L0_ffn_b2"], ACT.Gelu)
        moe1 = Moe(1, 8, 1024, a["L1_ffn_Wfc"], a["L1_ffn_Wproj"], a["L1_ffn_bproj"], ACT.Gelu_apprx_tanh)
        setup(nc, sem, alloc, a, c)
        end_phase()
        attention(nc, sem, alloc, a, c, 0)
        end_phase()
        for moe in (moe0, moe1):
            if moe.layer == 1:
                attention(nc, sem, alloc, a, c, 1)
                end_phase()
            with ExitStack() as keep:
                r = route(nc, sem, alloc, alloc(keep), a, c, moe)
                end_phase()
                if moe.layer == 0:
                    experts(nc, sem, alloc, c, moe, r)
                    end_phase()
                    combine(nc, sem, alloc, c, moe, r)
                    end_phase()
                else:
                    shared_expert(nc, sem, alloc, c, moe, r, 0)
                    end_phase()
                    experts(nc, sem, alloc, c, moe, r)
                    end_phase()
                    shared_expert(nc, sem, alloc, c, moe, r, 1, out)
                    end_phase()


def setup(nc, sem, alloc, a, c):
    with ExitStack() as stack:
        sb = alloc(stack)
        wst = sb("wst", [P, 8, DC, D])
        vec0 = sb("vec0", [60, P])
        vec1 = sb("vec1", [72, P])
        gst = sb("gst", [14, D])
        m1u = sb("m1u", [P, P], U8)
        m1f = sb("m1f", [P, P])
        zeros = sb("zeros", [P, D])
        bank = [stack.enter_context(nc.psum_tensor(f"setup_bank{i}", [P, 512], F32)) for i in range(8)]
        loaded_x, loaded_w, loaded_small = sem("loaded_x"), sem("loaded_w"), sem("loaded_small")
        zeros_ready, slots_zeroed = sem("zeros_ready"), sem("slots_zeroed")
        made, ident_ready, transposed, evacuated, step = (
            sem("made"), sem("ident_ready"), sem("transposed"), sem("evacuated"), sem("dve_step"))
        mats = [a[f"L{l}_xattn_{w}"] for l in range(2) for w in ("Wq", "Wk", "Wv", "Wo")]
        block = stack.enter_context(nc.Block())

        @block.sync
        def _(sp):
            for m, w in enumerate(mats):
                sp.dma_start(wst[:, m], w.rearrange("(c p) i -> p c i", p=P)).then_inc(loaded_w, 16)
            sp.dma_start(c["X"][:], a["x"].rearrange("b t d -> t b d")).then_inc(loaded_x, 16)
            sp.wait_ge(zeros_ready, 1)
            rows = c["xg"].shape[0] // P
            sp.dma_start(c["xg"].rearrange("(p r) d -> p r d", p=P),
                         bcast(zeros[:].rearrange("p (r d) -> p r d", r=1), [P, rows, D])).then_inc(slots_zeroed, 16)
            sp.wait_ge(slots_zeroed, 16)

        @block.scalar
        def _(act):
            small = [
                (vec0[0:2], a["L0_xattn_bq"].rearrange("(c p) -> c p", p=P)),
                (vec0[2:4], a["L0_xattn_bk"].rearrange("(c p) -> c p", p=P)),
                (vec0[4:60], a["L0_ffn_b1"].rearrange("e (c p) -> (e c) p", p=P)),
                (vec1[0:64], a["L1_ffn_bfc"].rearrange("e (c p) -> (e c) p", p=P)),
                (vec1[64:72], a["L1_ffn_bfc_s"].rearrange("(c p) -> c p", p=P)),
                (gst[:], a["L0_ffn_gate_w"]),
                (c["gT1"][:], a["L1_ffn_Wr"].rearrange("(c p) e -> p c e", p=P)),
                (c["bv"][:], bcast(a["L0_xattn_bv"].rearrange("(o d) -> o d", o=1), [P, D])),
                (c["bo"][:], bcast(a["L0_xattn_bo"].rearrange("(o d) -> o d", o=1), [P, D])),
                (m1u[:], a["mask_SxS2_bk0"]),
            ]
            for to, of in small:
                act.dma_start(to, of).then_inc(loaded_small, 16)

        @block.gpsimd
        def _(pool):
            pool.memset(zeros[:], 0.0).then_inc(zeros_ready, 1)
            pool.memset(c["ident"][:], 0.0)
            pool.memset(c["before"][:], 0.0)
            pool.memset(c["ones"][:], 1.0)
            pool.memset(c["mhalf"][:], -0.5)
            pool.memset(c["hmask"][:], 1.0).then_inc(made, 1)
            pool.wait_ge(made, 1)
            pool.affine_select(out=c["ident"][:], in_=c["ident"][:], compare_op=ALU.not_equal, fill=1.0,
                               base=0, pattern=[[-1, P]], channel_multiplier=1).then_inc(ident_ready, 1)
            pool.affine_select(out=c["before"][:], in_=c["before"][:], compare_op=ALU.is_ge, fill=1.0,
                               base=0, pattern=[[-1, P]], channel_multiplier=1)
            pool.affine_select(out=c["hmask"][:], in_=c["hmask"][:], compare_op=ALU.is_ge, fill=0.0,
                               base=0, pattern=[[-HD, 8]], channel_multiplier=1).then_inc(made, 1)
            pool.wait_ge(made, 2)
            pool.affine_select(out=c["hmask"][:], in_=c["hmask"][:], compare_op=ALU.is_ge, fill=0.0,
                               base=HD - 1, pattern=[[HD, 8]], channel_multiplier=-1).then_inc(made, 1)

        @block.tensor
        def _(pe):
            pe.wait_ge(ident_ready, 1)
            pe.wait_ge(loaded_w, 16 * len(mats))
            for m in range(8):
                if m >= 5:
                    pe.wait_ge(evacuated, m - 4)
                for ci in range(DC):
                    for co in range(DC):
                        last = pe.transpose(bank[m % 5][:, (ci * DC + co) * P:(ci * DC + co + 1) * P],
                                            wst[:, m, co, ci * P:(ci + 1) * P], c["ident"][:])
                last.then_inc(transposed, 1)
            pe.wait_ge(loaded_small, 16 * 10)
            pe.transpose(bank[5][:, 0:60], vec0[:], c["ident"][0:60, 0:60]).then_inc(transposed, 1)
            pe.transpose(bank[6][:, 0:72], vec1[:], c["ident"][0:72, 0:72]).then_inc(transposed, 1)
            for ci in range(DC):
                last = pe.transpose(bank[7][:, ci * 14:(ci + 1) * 14], gst[:, ci * P:(ci + 1) * P],
                                    c["ident"][0:14, 0:14])
            last.then_inc(transposed, 1)

        @block.vector
        def _(dve):
            for m in range(8):
                dve.wait_ge(transposed, m + 1)
                dve.tensor_copy(c["WT"][:, m].rearrange("p c o -> p (c o)"), bank[m % 5][:]).then_inc(evacuated, 1)
            dve.wait_ge(transposed, 9)
            dve.tensor_copy(c["vecT0"][:], bank[5][:, 0:60])
            dve.tensor_scalar(c["bqs"][:], bank[5][:, 0:DC], 0.5 * HD ** -0.5, None, ALU.mult)
            dve.wait_ge(transposed, 10)
            dve.tensor_copy(c["vecT1"][:], bank[6][:, 0:72])
            dve.wait_ge(transposed, 11)
            dve.tensor_copy(c["gT0"][:].rearrange("p c e -> p (c e)"), bank[7][:, 0:DC * 14])
            dve.wait_ge(loaded_small, 16 * 10)
            dve.tensor_copy(m1f[:], m1u[:]).then_inc(step, 1)
            dve.wait_ge(step, 1)
            dve.tensor_scalar(c["M1"][:], m1f[:], 1.0e9, -1.0e9, ALU.mult, ALU.add)
            dve.tensor_reduce(c["rowany"][:], m1f[:], AX.X, ALU.max)
            dve.wait_ge(loaded_x, 16)
            for b in range(B):
                dve.bn_stats(c["ST"][:, b], c["X"][:, b])


def ln_scales(c, dve, var_ready, root_ready, step):
    for b in range(B):
        last = dve.bn_aggr(c["MV"][:, b], c["ST"][:, b])
    last.then_inc(step, 1)
    dve.wait_ge(step, 1)
    dve.tensor_scalar(c["nmr"][:], c["MV"][:, :, 1], EPS, None, ALU.add).then_inc(var_ready, 1)
    dve.wait_ge(root_ready, 1)
    dve.scalar_tensor_tensor(c["nmr"][:], c["MV"][:, :, 0], -1.0, c["rstd"][:], ALU.mult, ALU.mult).then_inc(step, 1)
    dve.wait_ge(step, 2)


def ln_root(c, pool, var_ready, root_ready):
    pool.wait_ge(var_ready, 1)
    pool.tensor_tensor(c["rstd"][:], c["nmr"][:], c["mhalf"][:], ALU.pow).then_inc(root_ready, 1)


def attention(nc, sem, alloc, a, c, layer):
    E = (14, 8)[layer]
    with ExitStack() as stack:
        sb = alloc(stack)
        two = range(2)
        ctx_sb = [sb(f"ctx{i}", [P, D]) for i in two]
        xn = [sb(f"xn{i}", [P, D]) for i in two]
        xcT = [sb(f"xcT{i}", [P, 2 * DC, P]) for i in two]
        qT = [sb(f"qT{i}", [P, DC, P]) for i in two]
        kT = [sb(f"kT{i}", [P, DC, P]) for i in two]
        kblk = [sb(f"kblk{i}", [P, DC, 8, P]) for i in two]
        vaug = [sb(f"vaug{i}", [P, H, VW]) for i in two]
        U = sb("U", [P, H, P])
        E_ = sb("E", [P, H, P])
        ET = sb("ET", [P, H, P])
        mx = [sb(f"mx{i}", [P, H]) for i in two]
        nmx = [sb(f"nmx{i}", [P, H]) for i in two]
        oT = sb("oT", [P, NG, P])
        rz = sb("rz", [P, H])
        on = sb("on", [P, D])
        onT = sb("onT", [P, DC, P])
        xo = sb("xo", [P, D])
        gate = sb("gate", [P, 1])
        st = sb("st", [P, 6])
        mv = [sb(f"mv{i}", [P, 2]) for i in two]
        ve = [sb(f"ve{i}", [P, 1]) for i in two]
        rs = [sb(f"rs{i}", [P, 1]) for i in two]
        nm = [sb(f"nm{i}", [P, 1]) for i in two]
        hb = [sb(f"hb{i}", [P, D]) for i in two]
        hT = sb("hT", [P, DC, P])
        bank = [stack.enter_context(nc.psum_tensor(f"attn{layer}_bank{i}", [P, 512], F32)) for i in range(8)]
        IN, QK, V, S, TE, O = bank[0], bank[1], bank[2], bank[3:5], bank[5:7], bank[7]
        if layer == 0:
            fs = [sb(f"fs{i}", [P, H, P]) for i in two]
            amb = sb("amb", [P, B, P])
            padu = sb("padu", [P, B, P], U8)
            amh = sb("amh", [P, P])
        wq, wk, wv, wo = (c["WT"][:, 4 * layer + i] for i in range(4))
        scale, twice = (0.5 * HD ** -0.5, 2.0) if layer == 0 else (HD ** -0.5, 1.0)

        ctx_loaded = [sem(f"ctx_loaded{i}") for i in two]
        fs_loaded = [sem(f"fs_loaded{i}") for i in two]
        small_loaded, amh_ready = sem("small_loaded"), sem("amh_ready")
        amb_ready, vones_ready = sem("amb_ready"), sem("vones_ready")
        var_ready, root_ready, ln_step = sem("var_ready"), sem("root_ready"), sem("ln_step")
        xn_ready = sem("xn_ready")
        bias_ready = sem("bias_ready")
        in_done = sem("in_done")
        xcT_ready = sem("xcT_ready")
        qk_done, v_done = sem("qk_done"), sem("v_done")
        qkT_ready = sem("qkT_ready")
        kblk_ready = sem("kblk_ready")
        v_ready = sem("v_ready")
        s_done = sem("s_done")
        mx_step = sem("mx_step")
        mx_ready = sem("mx_ready")
        e_ready = sem("e_ready")
        et_done = sem("et_done")
        eT_ready = sem("eT_ready")
        o_done = sem("o_done")
        oT_ready = sem("oT_ready")
        ob_done = sem("ob_done")
        rz_step = sem("rz_step")
        on_ready = sem("on_ready")
        onT_done, onT_ready = sem("onT_done"), sem("onT_ready")
        wo_done = sem("wo_done")
        xo_step = sem("xo_step")
        x_ready = sem("x_ready")
        st_step = sem("st_step")
        ve_ready = sem("ve_ready")
        rs_ready = sem("rs_ready")
        nm_step = sem("nm_step")
        h_ready = sem("h_ready")
        h_kept = sem("h_kept")
        hT_done = sem("hT_done")
        hT_ready = sem("hT_ready")
        lg_done = sem("lg_done")
        lg_ready = sem("lg_ready")
        LG, wr = c[f"LG{layer}"], c[f"gT{layer}"]
        rz_per_tile = 1 + layer
        block = stack.enter_context(nc.Block())

        def tiles(eng, tile):
            for b in range(4):
                tile(b, b % 2, b // 2)
            with eng.Fori(0, 5) as i:
                tile(i * 2 + 4, 0, i + 2)
                tile(i * 2 + 5, 1, i + 2)
            for b in range(B - 2, B):
                tile(b, b % 2, b // 2)

        def next_k(b, par, k):
            return k + par

        @block.sync
        def _(sp):
            if layer == 0:
                pad = a["mask_BxS2_bf0"].rearrange("b s -> (b s)").rearrange("(o n) -> o n", o=1)
                sp.dma_start(padu[:].rearrange("p b s -> p (b s)"), bcast(pad, [P, B * P])).then_inc(small_loaded, 16)
                sp.dma_start(amh[:], a["fside_SxS2_0"]).then_inc(small_loaded, 16)

            def tile(b, par, k):
                if after(b, 2):
                    sp.wait_ge(in_done, b - 1)
                sp.dma_start(ctx_sb[par][:], a["ctx_1024"][b]).then_inc(ctx_loaded[par], 16)
                if layer == 0:
                    if after(b, 2):
                        sp.wait_ge(mx_ready, NG * (b - 1))
                    for half in two:
                        heads = slice(8 * half, 8 * half + 8)
                        sp.dma_start(fs[par][:, heads], a["fside_Bx16xSxS2_0"][b].rearrange("h t s -> t h s")[:, heads]
                                     ).then_inc(fs_loaded[par], 16)
            tiles(sp, tile)

        @block.gpsimd
        def _(pool):
            for i in two:
                pool.memset(vaug[i][:], 1.0).then_inc(vones_ready, 1)
            ln_root(c, pool, var_ready, root_ready)
            if layer == 0:
                pool.wait_ge(amb_ready, 1)

            def bias(b, par, k):
                pool.wait_ge(fs_loaded[par], 32 * k + 32)
                pool.tensor_tensor(fs[par][:], fs[par][:], bcast(amb[:, at(b)], [P, H, P]), ALU.add
                                   ).then_inc(bias_ready, 1)

            def root(b, par):
                pool.wait_ge(ve_ready, b + 1)
                pool.tensor_tensor(rs[par][:], ve[par][:], c["mhalf"][:, 0:1], ALU.pow).then_inc(rs_ready, 1)

            def tile(b, par, k):
                if layer == 0 and upto(b, B - 2):
                    bias(b + 1, 1 - par, next_k(b, par, k))
                if after(b, 2):
                    root(b - 2, par)
            if layer == 0:
                bias(0, 0, 0)
            tiles(pool, tile)
            root(B - 2, 0)
            root(B - 1, 1)

        @block.tensor
        def _(pe):
            def bring(b, par, k):
                pe.wait_ge(xn_ready, b + 1)
                pe.wait_ge(ctx_loaded[par], 16 * k + 16)
                if after(b, 3):
                    pe.wait_ge(on_ready, b - 2)
                if after(b, 1):
                    pe.wait_ge(xcT_ready, b)
                for i in range(DC):
                    pe.transpose(IN[:, i * P:(i + 1) * P], xn[par][:, i * P:(i + 1) * P], c["ident"][:])
                for i in range(DC):
                    last = pe.transpose(IN[:, (DC + i) * P:(DC + i + 1) * P], ctx_sb[par][:, i * P:(i + 1) * P],
                                        c["ident"][:])
                last.then_inc(in_done, 1)

            def project_qk(b, par):
                pe.wait_ge(xcT_ready, b + 1)
                if after(b, 1):
                    pe.wait_ge(qkT_ready, b)
                if after(b, 3):
                    pe.wait_ge(onT_ready, b - 2)
                for j, w in enumerate((wq, wk)):
                    for co in range(DC):
                        for ci in range(DC):
                            last = pe.matmul(QK[:, (j * DC + co) * P:(j * DC + co + 1) * P],
                                             w[:, ci, co * P:(co + 1) * P], xcT[par][:, j * DC + ci],
                                             start=(ci == 0), stop=(ci == DC - 1))
                last.then_inc(qk_done, 1)

            def project_v(b, par):
                if after(b, 1):
                    pe.wait_ge(v_ready, b)
                if after(b, 3):
                    pe.wait_ge(xo_step, 2 * (b - 3) + 1)
                for ci in range(DC):
                    last = pe.matmul(V[:, 0:D], xcT[par][:, DC + ci], wv[:, ci], start=(ci == 0), stop=(ci == DC - 1))
                last.then_inc(v_done, 1)

            def scores(b, par, g):
                if g == 0:
                    pe.wait_ge(qkT_ready, b + 1)
                if g % 2 == 0:
                    pe.wait_ge(kblk_ready, DC * b + (g // 2 + 1))
                if after(b, 1) or g >= 2:
                    pe.wait_ge(mx_ready, NG * b + g - 1)
                ch, lo = g // 2, (g % 2) * HG
                pe.matmul(S[g % 2][:], qT[par][:, ch],
                          kblk[par][:, ch, lo:lo + HG].rearrange("p h s -> p (h s)"),
                          start=True, stop=True).then_inc(s_done, 1)

            def turn_e(b, g):
                pe.wait_ge(e_ready, NG * b + g + 1)
                if after(b, 1) or g >= 2:
                    pe.wait_ge(eT_ready, NG * b + g - 1)
                for j in range(HG):
                    last = pe.transpose(TE[g % 2][:, j * P:(j + 1) * P], E_[:, HG * g + j], c["ident"][:])
                last.then_inc(et_done, 1)

            def outputs(b, par, g):
                if g == 0:
                    pe.wait_ge(v_ready, b + 1)
                    if after(b, 1):
                        pe.wait_ge(oT_ready, b)
                pe.wait_ge(eT_ready, NG * b + g + 1)
                for j in range(HG):
                    last = pe.matmul(O[VW * j:VW * j + VW, g * P:(g + 1) * P], vaug[par][:, HG * g + j],
                                     ET[:, HG * g + j], start=True, stop=True)
                last.then_inc(o_done, 1)

            def turn_back(b):
                pe.wait_ge(oT_ready, b + 1)
                if upto(b, B - 3):
                    pe.wait_ge(xcT_ready, b + 3)
                if after(b, 1):
                    pe.wait_ge(on_ready, b)
                for g in range(NG):
                    last = pe.transpose(IN[:, g * P:(g + 1) * P], oT[:, g], c["ident"][:])
                last.then_inc(ob_done, 1)

            def turn_out(b):
                pe.wait_ge(on_ready, b + 1)
                if upto(b, B - 3):
                    pe.wait_ge(qkT_ready, b + 3)
                if after(b, 1):
                    pe.wait_ge(onT_ready, b)
                for i in range(DC):
                    last = pe.transpose(QK[:, i * P:(i + 1) * P], on[:, i * P:(i + 1) * P], c["ident"][:])
                last.then_inc(onT_done, 1)

            def project_out(b):
                pe.wait_ge(onT_ready, b + 1)
                if upto(b, B - 3):
                    pe.wait_ge(v_ready, b + 3)
                if after(b, 1):
                    pe.wait_ge(lg_ready, b)
                for ci in range(DC):
                    last = pe.matmul(V[:, 0:D], onT[:, ci], wo[:, ci], start=(ci == 0), stop=(ci == DC - 1))
                last.then_inc(wo_done, 1)

            def turn_h(b, par):
                pe.wait_ge(h_ready, b + 1)
                if upto(b, B - 4):
                    pe.wait_ge(v_ready, b + 4)
                else:
                    pe.wait_ge(xo_step, 2 * b + 1)
                for i in range(DC):
                    last = pe.transpose(V[:, D + i * P:D + (i + 1) * P], hb[par][:, i * P:(i + 1) * P],
                                        c["ident"][:])
                last.then_inc(hT_done, 1)

            def logits(b):
                pe.wait_ge(hT_ready, b + 1)
                for i in range(DC):
                    last = pe.matmul(V[:, 0:E], hT[:, i], wr[:, i], start=(i == 0), stop=(i == DC - 1))
                last.then_inc(lg_done, 1)

            def tile(b, par, k):
                nxt = upto(b, B - 2)
                scores(b, par, 0)
                if after(b, 1):
                    turn_e(b - 1, 2)
                    outputs(b - 1, 1 - par, 1)
                if after(b, 2):
                    turn_out(b - 2)
                if nxt:
                    bring(b + 1, 1 - par, next_k(b, par, k))
                scores(b, par, 1)
                if after(b, 3):
                    turn_h(b - 3, 1 - par)
                if after(b, 1):
                    turn_e(b - 1, 3)
                    outputs(b - 1, 1 - par, 2)
                if nxt:
                    project_qk(b + 1, 1 - par)
                if after(b, 3):
                    logits(b - 3)
                scores(b, par, 2)
                turn_e(b, 0)
                if after(b, 1):
                    outputs(b - 1, 1 - par, 3)
                if after(b, 2):
                    project_out(b - 2)
                scores(b, par, 3)
                turn_e(b, 1)
                outputs(b, par, 0)
                if after(b, 1):
                    turn_back(b - 1)
                if nxt:
                    project_v(b + 1, 1 - par)

            bring(0, 0, 0)
            project_qk(0, 0)
            project_v(0, 0)
            tiles(pe, tile)
            turn_e(B - 1, 2)
            outputs(B - 1, 1, 1)
            turn_out(B - 2)
            turn_e(B - 1, 3)
            outputs(B - 1, 1, 2)
            turn_h(B - 3, 1)
            outputs(B - 1, 1, 3)
            logits(B - 3)
            project_out(B - 2)
            turn_back(B - 1)
            turn_h(B - 2, 0)
            logits(B - 2)
            turn_out(B - 1)
            project_out(B - 1)
            turn_h(B - 1, 1)
            logits(B - 1)

        @block.scalar
        def _(act):
            def qk_out(b, par):
                act.wait_ge(qk_done, b + 1)
                if after(b, 2):
                    act.wait_ge(s_done, NG * (b - 1))
                    act.wait_ge(kblk_ready, DC * (b - 1))
                for ch in range(DC):
                    q, k = (QK[:, (i * DC + ch) * P:(i * DC + ch + 1) * P] for i in two)
                    if layer == 0:
                        act.activation(qT[par][:, ch], q, ACT.Identity, bias=c["bqs"][:, ch:ch + 1], scale=scale)
                        last = act.activation(kT[par][:, ch], k, ACT.Identity, bias=c["vecT0"][:, 2 + ch:3 + ch])
                    else:
                        act.activation(qT[par][:, ch], q, ACT.Copy, scale=scale)
                        last = act.activation(kT[par][:, ch], k, ACT.Copy)
                last.then_inc(qkT_ready, 1)

            def exps(b, par, g):
                act.wait_ge(mx_ready, NG * b + g + 1)
                if after(b, 1):
                    act.wait_ge(et_done, NG * (b - 1) + g + 1)
                for h in range(HG * g, HG * g + HG):
                    last = act.activation(E_[:, h], U[:, h], ACT.Exp, bias=nmx[par][:, h:h + 1], scale=twice)
                last.then_inc(e_ready, 1)

            def et_out(b, g):
                act.wait_ge(et_done, NG * b + g + 1)
                if after(b, 1):
                    act.wait_ge(o_done, NG * (b - 1) + g + 1)
                act.activation(ET[:, HG * g:HG * g + HG].rearrange("p h t -> p (h t)"), TE[g % 2][:],
                               ACT.Copy).then_inc(eT_ready, 1)

            def o_out(b):
                act.wait_ge(o_done, NG * b + NG)
                if after(b, 1):
                    act.wait_ge(ob_done, b)
                act.activation(oT[:].rearrange("p g t -> p (g t)"), O[:], ACT.Copy).then_inc(oT_ready, 1)

            def hT_out(b):
                act.wait_ge(hT_done, b + 1)
                if after(b, 1):
                    act.wait_ge(lg_done, b)
                act.activation(hT[:].rearrange("p c t -> p (c t)"), V[:, D:2 * D], ACT.Copy).then_inc(hT_ready, 1)

            def keep_h(b, par):
                act.wait_ge(h_ready, b + 1)
                act.activation(c["Hn"][:, b], hb[par][:], ACT.Copy).then_inc(h_kept, 1)

            def tile(b, par, k):
                if after(b, 1):
                    et_out(b - 1, 2)
                exps(b, par, 0)
                if after(b, 3):
                    hT_out(b - 3)
                if after(b, 1):
                    et_out(b - 1, 3)
                exps(b, par, 1)
                if upto(b, B - 2):
                    qk_out(b + 1, 1 - par)
                et_out(b, 0)
                exps(b, par, 2)
                if after(b, 1):
                    o_out(b - 1)
                et_out(b, 1)
                exps(b, par, 3)
                if after(b, 3):
                    keep_h(b - 3, 1 - par)

            qk_out(0, 0)
            tiles(act, tile)
            et_out(B - 1, 2)
            et_out(B - 1, 3)
            hT_out(B - 3)
            keep_h(B - 3, 1)
            o_out(B - 1)
            hT_out(B - 2)
            keep_h(B - 2, 0)
            hT_out(B - 1)
            keep_h(B - 1, 1)

        @block.vector
        def _(dve):
            if layer == 0:
                dve.wait_ge(small_loaded, 32)
                dve.tensor_scalar(amh[:], amh[:], 0.5, None, ALU.mult).then_inc(amh_ready, 1)
                dve.tensor_scalar(amb[:], padu[:], -BIG, 10.0, ALU.mult, ALU.mult).then_inc(amh_ready, 1)
                dve.wait_ge(amh_ready, 2)
                dve.tensor_tensor(amb[:], amb[:], bcast(amh[:].rearrange("p (o s) -> p o s", o=1), [P, B, P]),
                                  ALU.add).then_inc(amb_ready, 1)
            ln_scales(c, dve, var_ready, root_ready, ln_step)
            dve.wait_ge(vones_ready, 2)

            def normed(b, par):
                if after(b, 2):
                    dve.wait_ge(in_done, b - 1)
                dve.tensor_scalar(xn[par][:], c["X"][:, b], c["rstd"][:, at(b)], c["nmr"][:, at(b)],
                                  ALU.mult, ALU.add).then_inc(xn_ready, 1)

            def in_out(b, par):
                dve.wait_ge(in_done, b + 1)
                if after(b, 2):
                    dve.wait_ge(v_done, b - 1)
                dve.tensor_copy(xcT[par][:].rearrange("p c t -> p (c t)"), IN[:]).then_inc(xcT_ready, 1)

            def k_out(b, par, ch):
                if ch == 0:
                    dve.wait_ge(qkT_ready, b + 1)
                    if after(b, 2):
                        dve.wait_ge(s_done, NG * (b - 1))
                dve.tensor_tensor(kblk[par][:, ch],
                                  bcast(kT[par][:, ch:ch + 1], [P, 8, P]),
                                  bcast(c["hmask"][:].rearrange("p (h o) -> p h o", o=1), [P, 8, P]), ALU.mult
                                  ).then_inc(kblk_ready, 1)

            def v_out(b, par):
                dve.wait_ge(v_done, b + 1)
                if after(b, 2):
                    dve.wait_ge(o_done, NG * (b - 1))
                to = vaug[par][:, :, 0:HD]
                of = V[:, 0:D].rearrange("p (h d) -> p h d", d=HD)
                if layer == 0:
                    dve.tensor_tensor(to, of, c["bv"][:].rearrange("p (h d) -> p h d", d=HD), ALU.add
                                      ).then_inc(v_ready, 1)
                else:
                    dve.tensor_copy(to, of).then_inc(v_ready, 1)

            def maxima(b, par, g):
                dve.wait_ge(s_done, NG * b + g + 1)
                if layer == 0 and g == 0:
                    dve.wait_ge(bias_ready, b + 1)
                if after(b, 1):
                    dve.wait_ge(e_ready, NG * (b - 1) + g + 1)
                dve.memset(gate[:], 0.0)
                for j in range(HG):
                    h = HG * g + j
                    last = dve.tensor_tensor_reduce(U[:, h], S[g % 2][:, j * P:(j + 1) * P],
                                                    fs[par][:, h] if layer == 0 else c["M1"][:],
                                                    1.0, -BIG, ALU.add, ALU.max, mx[par][:, h:h + 1])
                last.then_inc(mx_step, 1)
                dve.wait_ge(mx_step, NG * b + g + 1)
                dve.tensor_scalar(nmx[par][:, HG * g:HG * g + HG], mx[par][:, HG * g:HG * g + HG], -twice, None,
                                  ALU.mult).then_inc(mx_ready, 1)

            def divide(b):
                dve.wait_ge(ob_done, b + 1)
                if after(b, 1):
                    dve.wait_ge(onT_done, b)
                ob = IN[:].rearrange("p (h w) -> p h w", w=VW)
                dve.reciprocal(rz[:], ob[:, :, HD]).then_inc(rz_step, 1)
                dve.wait_ge(rz_step, b * rz_per_tile + 1)
                if layer == 1:
                    dve.tensor_scalar(rz[:], rz[:], c["rowany"][:, 0:1], None, ALU.mult).then_inc(rz_step, 1)
                    dve.wait_ge(rz_step, b * 2 + 2)
                dve.tensor_tensor(on[:].rearrange("p (h d) -> p h d", d=HD), ob[:, :, 0:HD],
                                  bcast(rz[:].rearrange("p (h o) -> p h o", o=1), [P, H, HD]), ALU.mult
                                  ).then_inc(on_ready, 1)

            def turned(b):
                dve.wait_ge(onT_done, b + 1)
                if after(b, 1):
                    dve.wait_ge(wo_done, b)
                dve.tensor_copy(onT[:].rearrange("p c t -> p (c t)"), QK[:, 0:D]).then_inc(onT_ready, 1)

            def projected(b):
                dve.wait_ge(wo_done, b + 1)
                if layer == 0:
                    dve.tensor_tensor(xo[:], V[:, 0:D], c["bo"][:], ALU.add).then_inc(xo_step, 1)
                else:
                    dve.tensor_copy(xo[:], V[:, 0:D]).then_inc(xo_step, 1)

            def residual(b, par):
                dve.wait_ge(xo_step, 2 * b + 1)
                dve.tensor_tensor(c["X"][:, b], c["X"][:, b], xo[:], ALU.add).then_inc(xo_step, 1)
                dve.wait_ge(xo_step, 2 * b + 2)
                dve.memset(gate[:], 0.0)
                dve.bn_stats(st[:], c["X"][:, b]).then_inc(x_ready, 1)
                dve.wait_ge(x_ready, b + 1)
                if after(b, 2):
                    dve.wait_ge(nm_step, b - 1)
                dve.memset(gate[:], 0.0)
                dve.bn_aggr(mv[par][:], st[:]).then_inc(st_step, 1)
                dve.wait_ge(st_step, b + 1)
                if after(b, 2):
                    dve.wait_ge(rs_ready, b - 1)
                dve.tensor_scalar(ve[par][:], mv[par][:, 1:2], EPS, None, ALU.add).then_inc(ve_ready, 1)

            def layer_norm(b, par):
                dve.wait_ge(rs_ready, b + 1)
                dve.scalar_tensor_tensor(nm[par][:], mv[par][:, 0:1], -1.0, rs[par][:], ALU.mult, ALU.mult
                                         ).then_inc(nm_step, 1)
                dve.wait_ge(nm_step, b + 1)
                if after(b, 2):
                    dve.wait_ge(hT_done, b - 1)
                    dve.wait_ge(h_kept, b - 1)
                dve.tensor_scalar(hb[par][:], c["X"][:, b], rs[par][:], nm[par][:], ALU.mult, ALU.add
                                  ).then_inc(h_ready, 1)

            def logits_out(b):
                dve.wait_ge(lg_done, b + 1)
                dve.tensor_copy(LG[:, b], V[:, 0:E]).then_inc(lg_ready, 1)

            def tile(b, par, k):
                nxt = upto(b, B - 2)
                if after(b, 2):
                    divide(b - 2)
                maxima(b, par, 0)
                if after(b, 2):
                    turned(b - 2)
                v_out(b, par)
                if after(b, 3):
                    layer_norm(b - 3, 1 - par)
                if nxt:
                    in_out(b + 1, 1 - par)
                maxima(b, par, 1)
                k_out(b, par, 1)
                if upto(b, B - 3):
                    normed(b + 2, par)
                if after(b, 3):
                    logits_out(b - 3)
                maxima(b, par, 2)
                if nxt:
                    k_out(b + 1, 1 - par, 0)
                if after(b, 2):
                    projected(b - 2)
                maxima(b, par, 3)
                if after(b, 2):
                    residual(b - 2, par)

            normed(0, 0)
            normed(1, 1)
            in_out(0, 0)
            k_out(0, 0, 0)
            tiles(dve, tile)
            divide(B - 2)
            turned(B - 2)
            layer_norm(B - 3, 1)
            logits_out(B - 3)
            projected(B - 2)
            residual(B - 2, 0)
            layer_norm(B - 2, 0)
            divide(B - 1)
            turned(B - 1)
            logits_out(B - 2)
            projected(B - 1)
            residual(B - 1, 1)
            layer_norm(B - 1, 1)
            logits_out(B - 1)


def at(b):
    return slice(b, b + 1) if isinstance(b, int) else bass.ds(b, 1)


def after(b, n):
    return not isinstance(b, int) or b >= n


def upto(b, n):
    return not isinstance(b, int) or b <= n


def paired(eng, n, step, first=2):
    turns = (n - first - 2) // 2
    for i in range(first):
        step(i, i % 2, i // 2)
    with eng.Fori(0, turns) as i:
        step(i * 2 + first, 0, i + first // 2)
        step(i * 2 + first + 1, 1, i + first // 2)
    for i in range(first + 2 * turns, n):
        step(i, i % 2, i // 2)


def route(nc, sem, alloc, keep, a, c, moe):
    E, S, layer = moe.E, moe.slots, moe.layer
    r = {
        "w12": keep("w12", [P, B, 2]),
        "G": keep("G", [P, B, E]),
        "rows": keep("rows", [P, 2, B], I32),
        "expert": keep("expert", [P, S], I32),
        "b2": keep("b2", [E + layer, D]),
    }
    if layer == 1:
        r["w1_shared"] = keep("w1_shared", [P, DC, moe.F])
        r["w2_shared"] = keep("w2_shared", [P, moe.FC, D])
    with ExitStack() as stack:
        sb = alloc(stack)
        two = range(2)
        top8 = sb("top8", [P, B, 8])
        ix8 = sb("ix8", [P, B, 8], U32)
        ixf = sb("ixf", [P, B, 2])
        hot = [sb(f"hot{j}", [P, B, E]) for j in two]
        both = sb("both", [P, B, E])
        diff = sb("diff", [P, B])
        e2 = sb("e2", [P, B])
        den = sb("den", [P, B])
        tmp = sb("tmp", [P, B, E])
        cnt = sb("cnt", [P, B, E])
        pre = sb("pre", [P, B + 1, E])
        over = sb("over", [P, E, B])
        nslot = sb("nslot", [P, E])
        first = sb("first", [P, E])
        base = sb("base", [P, E])
        pos = sb("pos", [P, B, E])
        rowf = sb("rowf", [P, 2, B])
        cmp = sb("cmp", [P, S, E - 1])
        expf = sb("expf", [P, S])
        iota_e = sb("iota_e", [P, E])
        iota_b = sb("iota_b", [P, B])
        iota_s = sb("iota_s", [P, S])
        bank = [stack.enter_context(nc.psum_tensor(f"route{layer}_bank{i}", [P, 512], F32)) for i in two]
        LG = c[f"LG{layer}"]
        iotas_ready = sem("iotas_ready")
        step = sem("dve_step")
        diff_ready, e2_ready, both_ready, ranks_done = sem("diff"), sem("e2"), sem("both"), sem("ranks")
        rows_ready, rows_sent, kept_loaded = sem("rows_ready"), sem("rows_sent"), sem("kept_loaded")
        block = stack.enter_context(nc.Block())

        @block.sync
        def _(sp):
            sp.dma_start(r["b2"][0:E], moe.b2).then_inc(kept_loaded, 16)
            if layer == 1:
                sp.dma_start(r["b2"][E:E + 1], a["L1_ffn_bproj_s"].rearrange("(o d) -> o d", o=1)
                             ).then_inc(kept_loaded, 16)
                sp.dma_start(r["w1_shared"][:], a["L1_ffn_Wfc_s"].rearrange("(c p) f -> p c f", p=P)
                             ).then_inc(kept_loaded, 16)
                sp.dma_start(r["w2_shared"][:], a["L1_ffn_Wproj_s"].rearrange("(c p) d -> p c d", p=P)
                             ).then_inc(kept_loaded, 16)
            sp.wait_ge(kept_loaded, 16 * (1 + 3 * layer))

        @block.scalar
        def _(act):
            act.wait_ge(diff_ready, 1)
            act.activation(e2[:], diff[:], ACT.Exp).then_inc(e2_ready, 1)

        @block.tensor
        def _(pe):
            pe.wait_ge(both_ready, 1)
            m = both[:].rearrange("p b e -> p (b e)")
            pe.matmul(bank[0][:, 0:B * E], c["before"][:], m, start=True, stop=True)
            pe.matmul(bank[1][:, 0:B * E], c["ones"][:], m, start=True, stop=True).then_inc(ranks_done, 1)

        @block.gpsimd
        def _(pool):
            pool.iota(iota_e[:], [[1, E]], base=0, channel_multiplier=0, allow_small_or_imprecise_dtypes=True)
            pool.iota(iota_b[:], [[P, B]], base=0, channel_multiplier=0, allow_small_or_imprecise_dtypes=True)
            pool.iota(iota_s[:], [[1, S]], base=0, channel_multiplier=0, allow_small_or_imprecise_dtypes=True
                      ).then_inc(iotas_ready, 1)
            if layer == 0:
                pool.wait_ge(rows_ready, 1)
                for b in range(B):
                    send_rows(pool, c, r, b, rows_sent)
                pool.wait_ge(rows_sent, 16 * TOPK * B)

        @block.vector
        def _(dve):
            done = [0]

            def link(ins):
                done[0] += 1
                ins.then_inc(step, 1)
                dve.wait_ge(step, done[0])

            def col(ap, shape):
                return bcast(ap, shape)

            full = [P, B, E]
            for b in range(B):
                last = dve.max(top8[:, b], LG[:, b])
            link(last)
            dve.tensor_tensor(diff[:], top8[:, :, 1], top8[:, :, 0], ALU.subtract).then_inc(diff_ready, 1)
            for b in range(B):
                last = dve.max_index(ix8[:, b], top8[:, b], LG[:, b])
            link(last)
            link(dve.tensor_copy(ixf[:], ix8[:, :, 0:2]))
            dve.wait_ge(iotas_ready, 1)
            ie = col(iota_e[:].rearrange("p (o e) -> p o e", o=1), full)
            for j in two:
                last = dve.tensor_tensor(hot[j][:], ie, col(ixf[:, :, j:j + 1], full), ALU.is_equal)
            link(last)
            dve.tensor_tensor(both[:], hot[0][:], hot[1][:], ALU.add).then_inc(both_ready, 1)
            dve.wait_ge(e2_ready, 1)
            link(dve.tensor_scalar(den[:], e2[:], 1.0, None, ALU.add))
            link(dve.reciprocal(r["w12"][:, :, 0], den[:]))
            link(dve.tensor_tensor(r["w12"][:, :, 1], r["w12"][:, :, 0], e2[:], ALU.mult))
            dve.tensor_tensor(tmp[:], hot[0][:], col(r["w12"][:, :, 0:1], full), ALU.mult)
            link(dve.tensor_tensor(r["G"][:], hot[1][:], col(r["w12"][:, :, 1:2], full), ALU.mult))
            link(dve.tensor_tensor(r["G"][:], r["G"][:], tmp[:], ALU.add))
            dve.memset(pre[:, 0], 0.0)
            dve.memset(first[:, 0:1], 0.0)
            dve.wait_ge(ranks_done, 1)
            link(dve.tensor_copy(cnt[:].rearrange("p b e -> p (b e)"), bank[1][:, 0:B * E]))
            for b in range(B):
                link(dve.tensor_tensor(pre[:, b + 1], pre[:, b], cnt[:, b], ALU.add))
            link(dve.tensor_tensor(over[:], col(pre[:, B].rearrange("p (e o) -> p e o", o=1), [P, E, B]),
                                   col(iota_b[:].rearrange("p (o b) -> p o b", o=1), [P, E, B]), ALU.is_gt))
            link(dve.tensor_reduce(nslot[:], over[:], AX.X, ALU.add))
            for e in range(1, E):
                link(dve.tensor_tensor(first[:, e:e + 1], first[:, e - 1:e], nslot[:, e - 1:e], ALU.add))
            link(dve.tensor_scalar(base[:], first[:], float(P), None, ALU.mult))
            link(dve.tensor_tensor(pos[:].rearrange("p b e -> p (b e)"), bank[0][:, 0:B * E],
                                   pre[:, 0:B].rearrange("p b e -> p (b e)"), ALU.add))
            link(dve.tensor_tensor(pos[:], pos[:], col(base[:].rearrange("p (o e) -> p o e", o=1), full), ALU.add))
            for j in two:
                link(dve.tensor_tensor(tmp[:], pos[:], hot[j][:], ALU.mult))
                link(dve.tensor_reduce(rowf[:, j], tmp[:], AX.X, ALU.add))
            dve.tensor_copy(r["rows"][:], rowf[:]).then_inc(rows_ready, 1)
            link(dve.tensor_tensor(cmp[:], col(iota_s[:].rearrange("p (s o) -> p s o", o=1), [P, S, E - 1]),
                                   col(first[:, 1:E].rearrange("p (o e) -> p o e", o=1), [P, S, E - 1]), ALU.is_ge))
            link(dve.tensor_reduce(expf[:], cmp[:], AX.X, ALU.add))
            dve.tensor_copy(r["expert"][:], expf[:])
    return r


def send_rows(pool, c, r, b, sent):
    for j in range(TOPK):
        pool.indirect_dma_start(out=c["xg"], out_offset=bass.IndirectOffsetOnAxis(
            ap=r["rows"][:, j, b:b + 1].bitcast(U32), axis=0), in_=c["Hn"][:, b], in_offset=None).then_inc(sent, 16)


def shared_expert(nc, sem, alloc, c, moe, r, half, out=None):
    FC, E = moe.FC, moe.E
    HALF = B // 2
    lo = half * HALF
    w1, w2 = r["w1_shared"], r["w2_shared"]
    with ExitStack() as stack:
        sb = alloc(stack)
        two = range(2)
        rows = [sb(f"rows{i}", [P, D + E + 1]) for i in two]
        xT = [sb(f"xT{i}", [P, DC, P]) for i in two]
        gT = [sb(f"gT{i}", [E + 1, P]) for i in two]
        hid = [sb(f"hid{i}", [P, FC, P]) for i in two]
        y = [[sb(f"y{i}_{j}", [P, D]) for j in two] for i in range(4)]
        bank = [stack.enter_context(nc.psum_tensor(f"shared{half}_bank{i}", [P, 512], F32)) for i in range(8)]
        T, HB, Y = bank[0:2], bank[2:6], bank[6:8]
        ones_ready = sem("ones_ready")
        rows_copied = sem("rows_copied")
        rows_sent = sem("rows_sent")
        xT_done = sem("xT_done")
        xT_ready = sem("xT_ready")
        hid_done = sem("hid_done")
        hid_ready = sem("hid_ready")
        y_done = sem("y_done")
        y_added = sem("y_added")
        routed_got = [sem(f"routed_got{i}") for i in range(4)]
        routed_step = sem("routed_step")
        routed_added = sem("routed_added")
        stored = sem("stored")
        block = stack.enter_context(nc.Block())

        @block.sync
        def _(sp):
            if half == 1:
                def store(b, par, k):
                    sp.wait_ge(routed_added, b + 1)
                    sp.dma_start(out[b], c["X"][:, b]).then_inc(stored, 16)
                paired(sp, B, store)
                sp.wait_ge(stored, 16 * B)

        @block.gpsimd
        def _(pool):
            def copy(n):
                if n >= 2:
                    pool.wait_ge(xT_done, n - 1)
                pool.tensor_copy(rows[n % 2][:, 0:D], c["Hn"][:, lo + n]).then_inc(rows_copied, 1)
                pool.tensor_copy(rows[n % 2][:, D:D + E], r["G"][:, lo + n]).then_inc(rows_copied, 1)

            def fetch(b):
                if b >= 4:
                    pool.wait_ge(routed_added, b - 3)
                for j in two:
                    pool.indirect_dma_start(out=y[b % 4][j][:], out_offset=None, in_=c["yg"],
                                            in_offset=bass.IndirectOffsetOnAxis(
                                                ap=r["rows"][:, j, b:b + 1].bitcast(U32), axis=0)
                                            ).then_inc(routed_got[b % 4], 16)
            for i in two:
                pool.memset(rows[i][:, D + E:D + E + 1], 1.0).then_inc(ones_ready, 1)
            copy(0)
            copy(1)
            for b in range(B):
                if half == 0:
                    send_rows(pool, c, r, b, rows_sent)
                else:
                    fetch(b)
                if b % 2 == 1 and b // 2 + 2 < HALF:
                    copy(b // 2 + 2)
            if half == 0:
                pool.wait_ge(rows_sent, 16 * TOPK * B)

        @block.tensor
        def _(pe):
            def turn(n, par):
                pe.wait_ge(rows_copied, 2 * n + 2)
                if after(n, 2):
                    pe.wait_ge(xT_ready, 2 * (n - 1))
                for i in range(DC):
                    pe.transpose(T[par][:, i * P:(i + 1) * P], rows[par][:, i * P:(i + 1) * P], c["ident"][:])
                pe.transpose(T[par][0:E + 1, D:D + P], rows[par][:, D:D + E + 1], c["ident"][:]
                             ).then_inc(xT_done, 1)

            def up(n, par):
                pe.wait_ge(xT_ready, 2 * n + 2)
                for f in range(FC):
                    if after(n, 1) or f >= 4:
                        pe.wait_ge(hid_ready, FC * n + f - 3)
                    for i in range(DC):
                        last = pe.matmul(HB[f % 4][:, 0:P], w1[:, i, f * P:(f + 1) * P], xT[par][:, i],
                                         start=(i == 0), stop=(i == DC - 1))
                    last.then_inc(hid_done, 1)

            def down(n, par):
                if after(n, 2):
                    pe.wait_ge(y_added, n - 1)
                pe.matmul(Y[par][:, 0:D], gT[par][:], r["b2"][:], start=True, stop=False)
                for f in range(FC):
                    pe.wait_ge(hid_ready, FC * n + f + 1)
                    last = pe.matmul(Y[par][:, 0:D], hid[par][:, f], w2[:, f], start=False, stop=(f == FC - 1))
                last.then_inc(y_done, 1)

            def tile(n, par, k):
                if upto(n, HALF - 2):
                    up(n + 1, 1 - par)
                if upto(n, HALF - 3):
                    turn(n + 2, par)
                down(n, par)
            pe.wait_ge(ones_ready, 2)
            turn(0, 0)
            turn(1, 1)
            up(0, 0)
            paired(pe, HALF, tile)

        @block.scalar
        def _(act):
            def tile(n, par, k):
                if after(n, 2):
                    act.wait_ge(y_done, n - 1)
                for f in range(FC):
                    act.wait_ge(hid_done, FC * n + f + 1)
                    act.activation(hid[par][:, f], HB[f % 4][:, 0:P], moe.act, bias=c["vecT1"][:, 64 + f:65 + f]
                                   ).then_inc(hid_ready, 1)
            paired(act, HALF, tile)

        @block.vector
        def _(dve):
            def in_out(n, par):
                dve.wait_ge(xT_done, n + 1)
                if after(n, 2):
                    dve.wait_ge(y_done, n - 1)
                dve.tensor_copy(xT[par][:].rearrange("p c t -> p (c t)"), T[par][:, 0:D]).then_inc(xT_ready, 1)
                dve.tensor_copy(gT[par][:], T[par][0:E + 1, D:D + P]).then_inc(xT_ready, 1)

            def add_routed(b, buf, k):
                dve.wait_ge(routed_got[buf], 32 * k + 32)
                w = [r["w12"][:, at(b), j:j + 1].rearrange("p o j -> p (o j)") for j in two]
                dve.scalar_tensor_tensor(c["X"][:, b], y[buf][0][:], w[0], c["X"][:, b], ALU.mult, ALU.add
                                         ).then_inc(routed_step, 1)
                dve.wait_ge(routed_step, b + 1)
                dve.scalar_tensor_tensor(c["X"][:, b], y[buf][1][:], w[1], c["X"][:, b], ALU.mult, ALU.add
                                         ).then_inc(routed_added, 1)

            def tile(n, par, k):
                if half == 1:
                    add_routed(n * 2, 2 * par, k)
                if upto(n, HALF - 3):
                    in_out(n + 2, par)
                dve.wait_ge(y_done, n + 1)
                dve.tensor_tensor(c["X"][:, n + lo], c["X"][:, n + lo], Y[par][:, 0:D], ALU.add).then_inc(y_added, 1)
                dve.wait_ge(y_added, n + 1)
                if half == 1:
                    add_routed(n * 2 + 1, 2 * par + 1, k)
            in_out(0, 0)
            in_out(1, 1)
            paired(dve, HALF, tile)


def experts(nc, sem, alloc, c, moe, r):
    FC, E, n_slots, weights = moe.FC, moe.E, moe.slots, (moe.w1, moe.w2)
    with ExitStack() as stack:
        sb = alloc(stack)
        two = range(2)
        w1 = [sb(f"w1_{i}", [P, DC, moe.F]) for i in two]
        w2 = [sb(f"w2_{i}", [P, FC, D]) for i in two]
        rows = [sb(f"rows{i}", [P, D]) for i in two]
        xT = [sb(f"xT{i}", [P, DC, P]) for i in two]
        hid = [sb(f"hid{i}", [P, FC, P]) for i in two]
        yb = [sb(f"yb{i}", [P, D]) for i in two]
        bank = [stack.enter_context(nc.psum_tensor(f"experts{moe.layer}_bank{i}", [P, 512], F32)) for i in range(8)]
        T, HB, Y = bank[0:2], bank[2:6], bank[6:8]
        w1_loaded = [sem(f"w1_loaded{i}") for i in two]
        w2_loaded = [sem(f"w2_loaded{i}") for i in two]
        rows_loaded = [sem(f"rows_loaded{i}") for i in two]
        xT_done = sem("xT_done")
        xT_ready = sem("xT_ready")
        hid_done = sem("hid_done")
        hid_ready = sem("hid_ready")
        y_done = sem("y_done")
        y_ready = sem("y_ready")
        y_stored = [sem(f"y_stored{i}") for i in two]
        block = stack.enter_context(nc.Block())

        @block.sync
        def _(sp):
            def get(n, par):
                if after(n, 2):
                    sp.wait_ge(xT_done, n - 1)
                sp.dma_start(rows[par][:], row_block(c["xg"], n)).then_inc(rows_loaded[par], 16)

            def expert_of(n):
                return sp.value_load(r["expert"][0:1, at(n)], min_val=0, max_val=E - 1)

            def load(sem_, to, of, e):
                sp.dma_start(to[:], of[e].rearrange("(c p) f -> p c f", p=P)).then_inc(sem_, 16)

            def load_w2(n, par, e):
                if after(n, 2):
                    sp.wait_ge(y_done, n - 1)
                load(w2_loaded[par], w2[par], weights[1], e)

            def slot(n, par, k):
                e = expert_of(n)
                e_before = expert_of(n - 1) if after(n, 1) else None
                if after(n, 2):
                    sp.wait_ge(hid_done, FC * (n - 1))
                load(w1_loaded[par], w1[par], weights[0], e)
                if upto(n, n_slots - 2):
                    get(n + 1, 1 - par)
                if after(n, 1):
                    load_w2(n - 1, 1 - par, e_before)
            get(0, 0)
            paired(sp, n_slots, slot, 4)
            load_w2(n_slots - 1, (n_slots - 1) % 2, expert_of(n_slots - 1))

        @block.gpsimd
        def _(pool):
            def store(n, par, k):
                pool.wait_ge(y_ready, n + 1)
                pool.dma_start(row_block(c["yg"], n), yb[par][:]).then_inc(y_stored[par], 16)
            paired(pool, n_slots, store)
            for i in two:
                pool.wait_ge(y_stored[i], 16 * ((n_slots + 1 - i) // 2))

        @block.tensor
        def _(pe):
            def turn(n, par, k):
                pe.wait_ge(rows_loaded[par], 16 * k + 16)
                if after(n, 2):
                    pe.wait_ge(xT_ready, n - 1)
                for i in range(DC):
                    last = pe.transpose(T[par][:, i * P:(i + 1) * P], rows[par][:, i * P:(i + 1) * P], c["ident"][:])
                last.then_inc(xT_done, 1)

            def up(n, par, k):
                pe.wait_ge(xT_ready, n + 1)
                pe.wait_ge(w1_loaded[par], 16 * k + 16)
                for f in range(FC):
                    if after(n, 1) or f >= 4:
                        pe.wait_ge(hid_ready, FC * n + f - 3)
                    for i in range(DC):
                        last = pe.matmul(HB[f % 4][:, 0:P], w1[par][:, i, f * P:(f + 1) * P], xT[par][:, i],
                                         start=(i == 0), stop=(i == DC - 1))
                    last.then_inc(hid_done, 1)

            def down(n, par, k):
                pe.wait_ge(w2_loaded[par], 16 * k + 16)
                if after(n, 2):
                    pe.wait_ge(y_ready, n - 1)
                for f in range(FC):
                    pe.wait_ge(hid_ready, FC * n + f + 1)
                    last = pe.matmul(Y[par][:, 0:D], hid[par][:, f], w2[par][:, f], start=(f == 0), stop=(f == FC - 1))
                last.then_inc(y_done, 1)

            def slot(n, par, k):
                if upto(n, n_slots - 2):
                    up(n + 1, 1 - par, (n + 1) // 2 if isinstance(n, int) else (k if par == 0 else k + 1))
                if upto(n, n_slots - 3):
                    turn(n + 2, par, k + 1)
                down(n, par, k)
            turn(0, 0, 0)
            turn(1, 1, 0)
            up(0, 0, 0)
            paired(pe, n_slots, slot)

        @block.scalar
        def _(act):
            def slot(n, par, k):
                e = act.value_load(r["expert"][0:1, at(n)], min_val=0, max_val=E - 1)
                if after(n, 2):
                    act.wait_ge(y_done, n - 1)
                for f in range(FC):
                    if moe.layer == 0:
                        bias = c["vecT0"][:, bass.ds(e * FC + (4 + f), 1)]
                    else:
                        bias = c["vecT1"][:, bass.ds(e * FC + f, 1)]
                    act.wait_ge(hid_done, FC * n + f + 1)
                    act.activation(hid[par][:, f], HB[f % 4][:, 0:P], moe.act, bias=bias).then_inc(hid_ready, 1)
            paired(act, n_slots, slot)

        @block.vector
        def _(dve):
            def in_out(n, par):
                dve.wait_ge(xT_done, n + 1)
                if after(n, 2):
                    dve.wait_ge(hid_done, FC * (n - 1))
                dve.tensor_copy(xT[par][:].rearrange("p c t -> p (c t)"), T[par][:, 0:D]).then_inc(xT_ready, 1)

            def slot(n, par, k):
                if upto(n, n_slots - 3):
                    in_out(n + 2, par)
                dve.wait_ge(y_done, n + 1)
                if after(n, 2):
                    dve.wait_ge(y_stored[par], 16 * k)
                dve.tensor_copy(yb[par][:], Y[par][:, 0:D]).then_inc(y_ready, 1)
            in_out(0, 0)
            in_out(1, 1)
            paired(dve, n_slots, slot)


def row_block(rows, n):
    return rows.rearrange("(s p) d -> s p d", p=P)[n]


def combine(nc, sem, alloc, c, moe, r):
    E = moe.E
    with ExitStack() as stack:
        sb = alloc(stack)
        two = range(2)
        y = [[sb(f"y{j}_{i}", [P, D]) for j in two] for i in two]
        gst = [sb(f"gst{i}", [P, E]) for i in two]
        gT = [sb(f"gTs{i}", [E, P]) for i in two]
        acc = [sb(f"acc{i}", [P, D]) for i in two]
        bank = [stack.enter_context(nc.psum_tensor(f"combine_bank{i}", [P, 512], F32)) for i in range(4)]
        GT, B2 = bank[0:2], bank[2:4]
        y_got = [sem(f"y_got{i}") for i in two]
        g_ready, gT_done, gT_ready, b2_done = sem("g_ready"), sem("gT_done"), sem("gT_ready"), sem("b2_done")
        acc_step = sem("acc_step")
        y_used = sem("y_used")
        block = stack.enter_context(nc.Block())

        @block.gpsimd
        def _(pool):
            for b in range(B):
                if b >= 2:
                    pool.wait_ge(y_used, b - 1)
                for j in two:
                    pool.indirect_dma_start(out=y[b % 2][j][:], out_offset=None, in_=c["yg"],
                                            in_offset=bass.IndirectOffsetOnAxis(
                                                ap=r["rows"][:, j, b:b + 1].bitcast(U32), axis=0)
                                            ).then_inc(y_got[b % 2], 16)

        @block.tensor
        def _(pe):
            def tile(b, par, k):
                pe.wait_ge(g_ready, b + 1)
                if after(b, 2):
                    pe.wait_ge(gT_ready, b - 1)
                pe.transpose(GT[par][0:E, 0:P], gst[par][:], c["ident"][:]).then_inc(gT_done, 1)
                pe.wait_ge(gT_ready, b + 1)
                if after(b, 2):
                    pe.wait_ge(y_used, b - 1)
                pe.matmul(B2[par][:, 0:D], gT[par][:], r["b2"][:], start=True, stop=True).then_inc(b2_done, 1)
            paired(pe, B, tile)

        @block.scalar
        def _(act):
            def tile(b, par, k):
                act.wait_ge(gT_done, b + 1)
                if after(b, 2):
                    act.wait_ge(b2_done, b - 1)
                act.activation(gT[par][:], GT[par][0:E, 0:P], ACT.Copy).then_inc(gT_ready, 1)
            paired(act, B, tile)

        @block.vector
        def _(dve):
            ops = 5

            def gates(b, par):
                if after(b, 2):
                    dve.wait_ge(gT_done, b - 1)
                dve.tensor_copy(gst[par][:], r["G"][:, b]).then_inc(g_ready, 1)

            def tile(b, par, k):
                if upto(b, B - 2):
                    gates(b + 1, 1 - par)
                t, at_step = acc[par], [0]

                def link(ins):
                    at_step[0] += 1
                    ins.then_inc(acc_step, 1)
                    dve.wait_ge(acc_step, b * ops + at_step[0])
                dve.wait_ge(b2_done, b + 1)
                link(dve.tensor_tensor(t[:], B2[par][:, 0:D], c["Hn"][:, b], ALU.add))
                dve.wait_ge(y_got[par], 32 * k + 32)
                for j in two:
                    w = r["w12"][:, at(b), j:j + 1].rearrange("p o j -> p (o j)")
                    link(dve.scalar_tensor_tensor(t[:], y[par][j][:], w, t[:], ALU.mult, ALU.add))
                link(dve.tensor_scalar(t[:], t[:], -100.0, 100.0, ALU.max, ALU.min))
                link(dve.tensor_tensor(c["X"][:, b], c["X"][:, b], t[:], ALU.add))
                dve.bn_stats(c["ST"][:, b], c["X"][:, b]).then_inc(y_used, 1)
            gates(0, 0)
            paired(dve, B, tile)


def kernel(**inputs):
    import numpy as _np
    import concourse.bacc as _bacc
    from concourse import mybir as _mybir
    from concourse.bass_utils import run_bass_kernel_spmd as _run

    nc = _bacc.Bacc("TRN2", target_bir_lowering=False, num_devices=1)
    arrays, args = {}, {}
    for name in inputs:
        v = _np.ascontiguousarray(inputs[name])
        arrays[f"in_{name}_dram"] = v
        args[name] = nc.dram_tensor(f"in_{name}_dram", v.shape, _mybir.dt.from_np(v.dtype), kind="ExternalInput").ap()
    out = nc.dram_tensor("out_0_dram", (B, P, D), F32, kind="ExternalOutput").ap()
    build(nc, args, out)
    r = _run(nc, [arrays], core_ids=[0])
    return r.results[0]["out_0_dram"]
```

```python
from contextlib import ExitStack

import concourse.bass as bass
from concourse import mybir

F32 = mybir.dt.float32
I32 = mybir.dt.int32
U32 = mybir.dt.uint32
U8 = mybir.dt.uint8
ALU = mybir.AluOpType
ACT = mybir.ActivationFunctionType
AX = mybir.AxisListType

P = 128
B = 16
D = 256
DC = D // P
H = 16
HD = D // H
HG = 4
NG = H // HG
VW = 2 * HD
BIG = 3.0e38
EPS = 1e-5
TOPK = 2
PIECE = 512


def max_slots(experts):
    return (TOPK * B * P + experts * (P - 1)) // P


class Moe:

    def __init__(self, layer, experts, hidden, w1, w2, b2, act):
        self.layer, self.E, self.F, self.w1, self.w2, self.b2, self.act = layer, experts, hidden, w1, w2, b2, act
        self.FC = hidden // P
        self.slots = max_slots(experts)


def bcast(ap, shape):
    return ap.to_broadcast(shape)


def build(nc, a, out):
    with ExitStack() as top:
        top.enter_context(nc.allow_non_contiguous_dma(reason="small tables of the router"))
        names, phase_sems = [0], []

        def sem(name):
            names[0] += 1
            phase_sems.append(nc.alloc_semaphore(f"{name}_{names[0]}"))
            return phase_sems[-1]

        def end_phase():
            nc.clear_and_free_semaphores(phase_sems)
            phase_sems.clear()
            nc.all_engine_barrier()

        def alloc(stack):
            def sb(name, shape, dt=F32):
                names[0] += 1
                return stack.enter_context(nc.sbuf_tensor(f"{name}_{names[0]}", shape, dt))
            return sb

        sb = alloc(top)
        c = {}
        c["X"] = sb("X", [P, B, D])
        c["Hn"] = sb("Hn", [P, B, D])
        c["ST"] = sb("ST", [P, B, 6])
        c["MV"] = sb("MV", [P, B, 2])
        c["rstd"] = sb("rstd", [P, B])
        c["nmr"] = sb("nmr", [P, B])
        c["mhalf"] = sb("mhalf", [P, B])
        for layer, experts_ in ((0, 14), (1, 8)):
            c[f"LG{layer}"] = sb(f"LG{layer}", [P, B, experts_])
        c["ident"] = sb("ident", [P, P])
        c["before"] = sb("before", [P, P])
        c["ones"] = sb("ones", [P, P])
        c["vecT0"] = sb("vecT0", [P, 60])
        c["vecT1"] = sb("vecT1", [P, 72])
        c["bqs"] = sb("bqs", [P, DC])
        c["bv"] = sb("bv", [P, D])
        c["bo"] = sb("bo", [P, D])
        c["gT0"] = sb("gT0", [P, DC, 14])
        c["gT1"] = sb("gT1", [P, DC, 8])
        c["hmask"] = sb("hmask", [P, 8])
        c["M1"] = sb("M1", [P, P])
        c["rowany"] = sb("rowany", [P, 1])
        c["xg"] = nc.dram_tensor("slot_rows", (max_slots(14) * P, D), F32, kind="Internal").ap()
        c["yg"] = nc.dram_tensor("slot_outputs", (max_slots(14) * P, D), F32, kind="Internal").ap()

        moe0 = Moe(0, 14, 512, a["L0_ffn_w1"], a["L0_ffn_w2"], a["L0_ffn_b2"], ACT.Gelu)
        moe1 = Moe(1, 8, 1024, a["L1_ffn_Wfc"], a["L1_ffn_Wproj"], a["L1_ffn_bproj"], ACT.Gelu_apprx_tanh)
        with ExitStack() as keep:
            c["zeros"] = alloc(keep)("zeros", [P, D])
            c["slots_zeroed"] = nc.alloc_semaphore("slots_zeroed")
            c["WT"] = alloc(keep)("WT", [P, 8, DC, D])
            setup(nc, sem, alloc, a, c)
            end_phase()
            weights = expert_w2(nc, alloc(keep), moe0)
            attention(nc, sem, alloc, a, c, 0, weights=weights, moe=moe0)
            end_phase()
            c["base"] = alloc(keep)("base", [P, B, D])
            routing = table(alloc(keep), moe0)
            with ExitStack() as held:
                expert_w1(alloc(held), moe0, weights)
                route(nc, sem, alloc, a, c, moe0, routing, weights)
                end_phase()
                dispatch(nc, sem, alloc, c, moe0, routing)
                end_phase()
                experts(nc, sem, alloc, c, moe0, routing, weights)
                end_phase()
            attention(nc, sem, alloc, a, c, 1, routing)
            end_phase()
        routing = table(alloc(top), moe1)
        weights = expert_w2(nc, alloc(top), moe1)
        expert_w1(alloc(top), moe1, weights)
        route(nc, sem, alloc, a, c, moe1, routing, weights)
        end_phase()
        shared_expert(nc, sem, alloc, c, moe1, routing, 0)
        end_phase()
        experts(nc, sem, alloc, c, moe1, routing, weights)
        end_phase()
        shared_expert(nc, sem, alloc, c, moe1, routing, 1, out)
        end_phase()


def setup(nc, sem, alloc, a, c):
    with ExitStack() as stack:
        sb = alloc(stack)
        wst = sb("wst", [P, 8, DC, D])
        vec0 = sb("vec0", [60, P])
        vec1 = sb("vec1", [72, P])
        gst = sb("gst", [14, D])
        m1u = sb("m1u", [P, P], U8)
        m1f = sb("m1f", [P, P])
        bank = [stack.enter_context(nc.psum_tensor(f"setup_bank{i}", [P, 512], F32)) for i in range(8)]
        loaded_x = [sem(f"loaded_x{q}") for q in range(4)]
        loaded_w, loaded_small = sem("loaded_w"), sem("loaded_small")
        var_ready, root_ready, ln_step = sem("var_ready"), sem("root_ready"), sem("ln_step")
        made, ident_ready, transposed, evacuated, step = (
            sem("made"), sem("ident_ready"), sem("transposed"), sem("evacuated"), sem("dve_step"))
        mats = [a[f"L{l}_xattn_{w}"] for l in range(2) for w in ("Wq", "Wk", "Wv", "Wo")]
        block = stack.enter_context(nc.Block())

        @block.sync
        def _(sp):
            for q in range(4):
                some = slice(q * B // 4, (q + 1) * B // 4)
                sp.dma_start(c["X"][:, some], a["x"].rearrange("b t d -> t b d")[:, some]).then_inc(loaded_x[q], 16)
            for m, w in enumerate(mats):
                sp.dma_start(wst[:, m], w.rearrange("(c p) i -> p c i", p=P)).then_inc(loaded_w, 16)

        @block.scalar
        def _(act):
            small = [
                (vec0[0:2], a["L0_xattn_bq"].rearrange("(c p) -> c p", p=P)),
                (vec0[2:4], a["L0_xattn_bk"].rearrange("(c p) -> c p", p=P)),
                (vec0[4:60], a["L0_ffn_b1"].rearrange("e (c p) -> (e c) p", p=P)),
                (vec1[0:64], a["L1_ffn_bfc"].rearrange("e (c p) -> (e c) p", p=P)),
                (vec1[64:72], a["L1_ffn_bfc_s"].rearrange("(c p) -> c p", p=P)),
                (gst[:], a["L0_ffn_gate_w"]),
                (c["gT1"][:], a["L1_ffn_Wr"].rearrange("(c p) e -> p c e", p=P)),
                (c["bv"][:], bcast(a["L0_xattn_bv"].rearrange("(o d) -> o d", o=1), [P, D])),
                (c["bo"][:], bcast(a["L0_xattn_bo"].rearrange("(o d) -> o d", o=1), [P, D])),
                (m1u[:], a["mask_SxS2_bk0"]),
            ]
            for to, of in small:
                act.dma_start(to, of).then_inc(loaded_small, 16)
            for m in range(8):
                act.wait_ge(transposed, m + 1)
                act.activation(c["WT"][:, m].rearrange("p c o -> p (c o)"), bank[m % 5][:], ACT.Copy
                               ).then_inc(evacuated, 1)

        @block.gpsimd
        def _(pool):
            pool.memset(c["zeros"][:], 0.0)
            pool.memset(c["ident"][:], 0.0)
            pool.memset(c["before"][:], 0.0)
            pool.memset(c["ones"][:], 1.0)
            pool.memset(c["mhalf"][:], -0.5)
            pool.memset(c["hmask"][:], 1.0).then_inc(made, 1)
            pool.wait_ge(made, 1)
            pool.affine_select(out=c["ident"][:], in_=c["ident"][:], compare_op=ALU.not_equal, fill=1.0,
                               base=0, pattern=[[-1, P]], channel_multiplier=1).then_inc(ident_ready, 1)
            pool.affine_select(out=c["before"][:], in_=c["before"][:], compare_op=ALU.is_ge, fill=1.0,
                               base=0, pattern=[[-1, P]], channel_multiplier=1)
            pool.affine_select(out=c["hmask"][:], in_=c["hmask"][:], compare_op=ALU.is_ge, fill=0.0,
                               base=0, pattern=[[-HD, 8]], channel_multiplier=1).then_inc(made, 1)
            pool.wait_ge(made, 2)
            pool.affine_select(out=c["hmask"][:], in_=c["hmask"][:], compare_op=ALU.is_ge, fill=0.0,
                               base=HD - 1, pattern=[[HD, 8]], channel_multiplier=-1).then_inc(made, 1)
            ln_root(c, pool, var_ready, root_ready)

        @block.tensor
        def _(pe):
            pe.wait_ge(ident_ready, 1)
            pe.wait_ge(loaded_w, 16 * len(mats))
            for m in range(8):
                if m >= 5:
                    pe.wait_ge(evacuated, m - 4)
                for ci in range(DC):
                    for co in range(DC):
                        last = pe.transpose(bank[m % 5][:, (ci * DC + co) * P:(ci * DC + co + 1) * P],
                                            wst[:, m, co, ci * P:(ci + 1) * P], c["ident"][:])
                last.then_inc(transposed, 1)
            pe.wait_ge(loaded_small, 16 * 10)
            pe.transpose(bank[5][:, 0:60], vec0[:], c["ident"][0:60, 0:60]).then_inc(transposed, 1)
            pe.transpose(bank[6][:, 0:72], vec1[:], c["ident"][0:72, 0:72]).then_inc(transposed, 1)
            for ci in range(DC):
                last = pe.transpose(bank[7][:, ci * 14:(ci + 1) * 14], gst[:, ci * P:(ci + 1) * P],
                                    c["ident"][0:14, 0:14])
            last.then_inc(transposed, 1)

        @block.vector
        def _(dve):
            for b in range(B):
                if b % (B // 4) == 0:
                    dve.wait_ge(loaded_x[b // (B // 4)], 16)
                dve.bn_stats(c["ST"][:, b], c["X"][:, b]).then_inc(ln_step, 1)
            ln_scales(c, dve, var_ready, root_ready, ln_step)
            dve.wait_ge(transposed, 9)
            dve.tensor_copy(c["vecT0"][:], bank[5][:, 0:60])
            dve.tensor_scalar(c["bqs"][:], bank[5][:, 0:DC], 0.5 * HD ** -0.5, None, ALU.mult)
            dve.wait_ge(transposed, 10)
            dve.tensor_copy(c["vecT1"][:], bank[6][:, 0:72])
            dve.wait_ge(transposed, 11)
            dve.tensor_copy(c["gT0"][:].rearrange("p c e -> p (c e)"), bank[7][:, 0:DC * 14])
            dve.wait_ge(loaded_small, 16 * 10)
            dve.tensor_copy(m1f[:], m1u[:]).then_inc(step, 1)
            dve.wait_ge(step, 1)
            dve.tensor_scalar(c["M1"][:], m1f[:], 1.0e9, -1.0e9, ALU.mult, ALU.add)
            dve.tensor_reduce(c["rowany"][:], m1f[:], AX.X, ALU.max)


def ln_scales(c, dve, var_ready, root_ready, step):
    dve.wait_ge(step, B)
    for b in range(B):
        last = dve.bn_aggr(c["MV"][:, b], c["ST"][:, b])
    last.then_inc(step, 1)
    dve.wait_ge(step, B + 1)
    dve.tensor_scalar(c["nmr"][:], c["MV"][:, :, 1], EPS, None, ALU.add).then_inc(var_ready, 1)
    dve.wait_ge(root_ready, 1)
    dve.scalar_tensor_tensor(c["nmr"][:], c["MV"][:, :, 0], -1.0, c["rstd"][:], ALU.mult, ALU.mult).then_inc(step, 1)
    dve.wait_ge(step, B + 2)


def ln_root(c, pool, var_ready, root_ready):
    pool.wait_ge(var_ready, 1)
    pool.tensor_tensor(c["rstd"][:], c["nmr"][:], c["mhalf"][:], ALU.pow).then_inc(root_ready, 1)


def attention(nc, sem, alloc, a, c, layer, routing=None, weights=None, moe=None):
    E = (14, 8)[layer]
    with ExitStack() as stack:
        sb = alloc(stack)
        two = range(2)
        ctx_sb = [sb(f"ctx{i}", [P, D]) for i in two]
        xn = [sb(f"xn{i}", [P, D]) for i in two]
        xcT = [sb(f"xcT{i}", [P, 2 * DC, P]) for i in two]
        qT = [sb(f"qT{i}", [P, DC, P]) for i in two]
        kT = [sb(f"kT{i}", [P, DC, P]) for i in two]
        kblk = [sb(f"kblk{i}", [P, DC, 8, P]) for i in two]
        vaug = [sb(f"vaug{i}", [P, H, VW]) for i in two]
        U = sb("U", [P, H, P])
        E_ = sb("E", [P, H, P])
        ET = sb("ET", [P, H, P])
        mx = [sb(f"mx{i}", [P, H]) for i in two]
        nmx = [sb(f"nmx{i}", [P, H]) for i in two]
        oT = sb("oT", [P, NG, P])
        rz = sb("rz", [P, H])
        on = sb("on", [P, D])
        onT = sb("onT", [P, DC, P])
        xo = sb("xo", [P, D])
        gate = sb("gate", [P, 1])
        warm = sb("warm", [P, 1])
        st = sb("st", [P, 6])
        mv = [sb(f"mv{i}", [P, 2]) for i in two]
        ve = [sb(f"ve{i}", [P, 1]) for i in two]
        rs = [sb(f"rs{i}", [P, 1]) for i in two]
        nm = [sb(f"nm{i}", [P, 1]) for i in two]
        hb = [sb(f"hb{i}", [P, D]) for i in two]
        hT = sb("hT", [P, DC, P])
        bank = [stack.enter_context(nc.psum_tensor(f"attn{layer}_bank{i}", [P, 512], F32)) for i in range(8)]
        IN, QK, V, S, TE, O = bank[0], bank[1], bank[2], bank[3:5], bank[5:7], bank[7]
        if layer == 0:
            fs = [sb(f"fs{i}", [P, H, P]) for i in two]
            amb = sb("amb", [P, B, P])
            padu = sb("padu", [P, B, P], U8)
            amh = sb("amh", [P, P])
        else:
            y = [[sb(f"y{i}_{j}", [P, D]) for j in two] for i in range(4)]
            sta = sb("sta", [P, 6])
            mva = [sb(f"mva{i}", [P, 2]) for i in two]
            vea = [sb(f"vea{i}", [P, 1]) for i in two]
            rsa = [sb(f"rsa{i}", [P, 1]) for i in two]
            nma = [sb(f"nma{i}", [P, 1]) for i in two]
        wq, wk, wv, wo = (c["WT"][:, 4 * layer + i] for i in range(4))
        scale, twice = (0.5 * HD ** -0.5, 2.0) if layer == 0 else (HD ** -0.5, 1.0)

        ctx_loaded = [sem(f"ctx_loaded{i}") for i in two]
        fs_loaded = [sem(f"fs_loaded{i}") for i in two]
        small_loaded, amh_ready = sem("small_loaded"), sem("amh_ready")
        amb_ready, vones_ready = sem("amb_ready"), sem("vones_ready")
        xn_ready = sem("xn_ready")
        bias_ready = sem("bias_ready")
        in_done = sem("in_done")
        xcT_ready = sem("xcT_ready")
        qk_done, v_done = sem("qk_done"), sem("v_done")
        qkT_ready = sem("qkT_ready")
        kblk_ready = sem("kblk_ready")
        v_ready = sem("v_ready")
        s_done = sem("s_done")
        mx_step = sem("mx_step")
        mx_ready = sem("mx_ready")
        e_ready = sem("e_ready")
        et_done = sem("et_done")
        eT_ready = sem("eT_ready")
        o_done = sem("o_done")
        oT_ready = sem("oT_ready")
        ob_done = sem("ob_done")
        rz_step = sem("rz_step")
        on_ready = sem("on_ready")
        onT_done, onT_ready = sem("onT_done"), sem("onT_ready")
        wo_done = sem("wo_done")
        xo_step = sem("xo_step")
        x_ready = sem("x_ready")
        st_step = sem("st_step")
        ve_ready = sem("ve_ready")
        rs_ready = sem("rs_ready")
        nm_step = sem("nm_step")
        h_ready = sem("h_ready")
        h_kept = sem("h_kept")
        hT_done = sem("hT_done")
        hT_ready = sem("hT_ready")
        lg_done = sem("lg_done")
        lg_ready = sem("lg_ready")
        LG, wr = c[f"LG{layer}"], c[f"gT{layer}"]
        y_got = [sem(f"y_got{i}") for i in range(4)]
        moe_step = sem("moe_step")
        lead_step = sem("lead_step")
        sta_ready = sem("sta_ready")
        vea_ready = sem("vea_ready")
        rsa_ready = sem("rsa_ready")
        nma_step = sem("nma_step")
        LEAD, MOE_STEPS = 3, 6
        rz_per_tile = 1 + layer
        block = stack.enter_context(nc.Block())

        def tiles(eng, tile):
            for b in range(4):
                tile(b, b % 2, b // 2)
            with eng.Fori(0, (B - 8) // 2) as i:
                tile(i * 2 + 4, 0, i + 2)
                tile(i * 2 + 5, 1, i + 2)
            for b in range(B - 4, B):
                tile(b, b % 2, b // 2)

        def next_k(b, par, k):
            return k + par

        @block.sync
        def _(sp):
            if layer == 0:
                pad = a["mask_BxS2_bf0"].rearrange("b s -> (b s)").rearrange("(o n) -> o n", o=1)
                sp.dma_start(padu[:].rearrange("p b s -> p (b s)"), bcast(pad, [P, B * P])).then_inc(small_loaded, 16)
                sp.dma_start(amh[:], a["fside_SxS2_0"]).then_inc(small_loaded, 16)

            def tile(b, par, k):
                if after(b, 2):
                    sp.wait_ge(in_done, b - 1)
                sp.dma_start(ctx_sb[par][:], a["ctx_1024"][b]).then_inc(ctx_loaded[par], 16)
                if layer == 0:
                    if after(b, 2):
                        sp.wait_ge(mx_ready, NG * (b - 1))
                    for half in two:
                        heads = slice(8 * half, 8 * half + 8)
                        sp.dma_start(fs[par][:, heads], a["fside_Bx16xSxS2_0"][b].rearrange("h t s -> t h s")[:, heads]
                                     ).then_inc(fs_loaded[par], 16)
                    if after(b, B - moe.E):
                        load_w2(sp, moe, weights, b - (B - moe.E))
                    if isinstance(b, int) and b < 4:
                        slots = c["xg"].shape[0] // P
                        some = slice(b * slots // 4, (b + 1) * slots // 4)
                        sp.dma_start(c["xg"].rearrange("(p r) d -> p r d", p=P)[:, some],
                                     bcast(c["zeros"][:].rearrange("p (r d) -> p r d", r=1),
                                           [P, some.stop - some.start, D])).then_inc(c["slots_zeroed"], 16)
            tiles(sp, tile)

        @block.gpsimd
        def _(pool):
            if layer == 0:
                for i in two:
                    pool.memset(vaug[i][:], 1.0).then_inc(vones_ready, 1)
                pool.wait_ge(amb_ready, 1)

            def bias(b, par, k):
                pool.wait_ge(fs_loaded[par], 32 * k + 32)
                pool.tensor_tensor(fs[par][:], fs[par][:], bcast(amb[:, at(b)], [P, H, P]), ALU.add
                                   ).then_inc(bias_ready, 1)

            def root(b, par):
                pool.wait_ge(ve_ready, b + 1)
                pool.tensor_tensor(rs[par][:], ve[par][:], c["mhalf"][:, 0:1], ALU.pow).then_inc(rs_ready, 1)

            def tile(b, par, k):
                if layer == 0 and upto(b, B - 2):
                    bias(b + 1, 1 - par, next_k(b, par, k))
                if after(b, 2):
                    root(b - 2, par)

            def fetch(b):
                if b >= 4 + LEAD:
                    pool.wait_ge(moe_step, MOE_STEPS * (b - 3 - LEAD))
                elif b >= 4:
                    pool.wait_ge(lead_step, 4 * (b - 3))
                for j in two:
                    pool.indirect_dma_start(out=y[b % 4][j][:], out_offset=None, in_=c["yg"],
                                            in_offset=bass.IndirectOffsetOnAxis(
                                                ap=routing["rows"][:, j, b:b + 1].bitcast(U32), axis=0)
                                            ).then_inc(y_got[b % 4], 16)

            def add_moe(b):
                pool.wait_ge(y_got[b % 4], 32 * (b // 4) + 32)
                y1, y2 = y[b % 4]
                pool.tensor_scalar(y1[:], y1[:], routing["w12"][:, b, 0:1], None, ALU.mult).then_inc(moe_step, 1)
                pool.tensor_scalar(y2[:], y2[:], routing["w12"][:, b, 1:2], None, ALU.mult).then_inc(moe_step, 1)
                pool.wait_ge(moe_step, MOE_STEPS * (b - LEAD) + 1)
                pool.tensor_tensor(y1[:], y1[:], c["base"][:, b], ALU.add).then_inc(moe_step, 1)
                pool.wait_ge(moe_step, MOE_STEPS * (b - LEAD) + 3)
                pool.tensor_tensor(y1[:], y1[:], y2[:], ALU.add).then_inc(moe_step, 1)
                pool.wait_ge(moe_step, MOE_STEPS * (b - LEAD) + 4)
                pool.tensor_scalar(y1[:], y1[:], -100.0, 100.0, ALU.max, ALU.min).then_inc(moe_step, 1)
                pool.wait_ge(moe_step, MOE_STEPS * (b - LEAD) + 5)
                pool.tensor_tensor(c["X"][:, b], c["X"][:, b], y1[:], ALU.add).then_inc(moe_step, 1)

            def root_ahead(b):
                pool.wait_ge(vea_ready, b + 1)
                pool.tensor_tensor(rsa[b % 2][:], vea[b % 2][:], c["mhalf"][:, 0:1], ALU.pow).then_inc(rsa_ready, 1)

            if layer == 0:
                bias(0, 0, 0)
                tiles(pool, tile)
            else:
                for b in range(3):
                    fetch(b)
                root_ahead(0)
                for i in two:
                    pool.memset(vaug[i][:], 1.0).then_inc(vones_ready, 1)
                fetch(3)
                root_ahead(1)
                fetch(4)
                add_moe(LEAD)
                fetch(5)
                root_ahead(2)
                fetch(6)
                fetch(7)
                for b in range(B):
                    if b + 4 < B:
                        add_moe(b + 4)
                    if b + 3 < B:
                        root_ahead(b + 3)
                    if b + 8 < B:
                        fetch(b + 8)
                    if b >= 2:
                        root(b - 2, b % 2)
            root(B - 2, 0)
            root(B - 1, 1)

        @block.tensor
        def _(pe):
            def bring(b, par, k):
                pe.wait_ge(xn_ready, b + 1)
                pe.wait_ge(ctx_loaded[par], 16 * k + 16)
                if after(b, 3):
                    pe.wait_ge(on_ready, b - 2)
                if after(b, 1):
                    pe.wait_ge(xcT_ready, b)
                for i in range(DC):
                    pe.transpose(IN[:, i * P:(i + 1) * P], xn[par][:, i * P:(i + 1) * P], c["ident"][:])
                for i in range(DC):
                    last = pe.transpose(IN[:, (DC + i) * P:(DC + i + 1) * P], ctx_sb[par][:, i * P:(i + 1) * P],
                                        c["ident"][:])
                last.then_inc(in_done, 1)

            def project_qk(b, par):
                pe.wait_ge(xcT_ready, b + 1)
                if after(b, 1):
                    pe.wait_ge(qkT_ready, b)
                if after(b, 3):
                    pe.wait_ge(onT_ready, b - 2)
                for j, w in enumerate((wq, wk)):
                    for co in range(DC):
                        for ci in range(DC):
                            last = pe.matmul(QK[:, (j * DC + co) * P:(j * DC + co + 1) * P],
                                             w[:, ci, co * P:(co + 1) * P], xcT[par][:, j * DC + ci],
                                             start=(ci == 0), stop=(ci == DC - 1))
                last.then_inc(qk_done, 1)

            def project_v(b, par):
                if after(b, 1):
                    pe.wait_ge(v_ready, b)
                if after(b, 3):
                    pe.wait_ge(xo_step, 2 * (b - 3) + 1)
                for ci in range(DC):
                    last = pe.matmul(V[:, 0:D], xcT[par][:, DC + ci], wv[:, ci], start=(ci == 0), stop=(ci == DC - 1))
                last.then_inc(v_done, 1)

            def scores(b, par, g):
                if g == 0:
                    pe.wait_ge(qkT_ready, b + 1)
                if g % 2 == 0:
                    pe.wait_ge(kblk_ready, DC * b + (g // 2 + 1))
                if after(b, 1) or g >= 2:
                    pe.wait_ge(mx_ready, NG * b + g - 1)
                ch, lo = g // 2, (g % 2) * HG
                pe.matmul(S[g % 2][:], qT[par][:, ch],
                          kblk[par][:, ch, lo:lo + HG].rearrange("p h s -> p (h s)"),
                          start=True, stop=True).then_inc(s_done, 1)

            def turn_e(b, g):
                pe.wait_ge(e_ready, NG * b + g + 1)
                if after(b, 1) or g >= 2:
                    pe.wait_ge(eT_ready, NG * b + g - 1)
                for j in range(HG):
                    last = pe.transpose(TE[g % 2][:, j * P:(j + 1) * P], E_[:, HG * g + j], c["ident"][:])
                last.then_inc(et_done, 1)

            def outputs(b, par, g):
                if g == 0:
                    pe.wait_ge(v_ready, b + 1)
                    if after(b, 1):
                        pe.wait_ge(oT_ready, b)
                pe.wait_ge(eT_ready, NG * b + g + 1)
                for j in range(HG):
                    last = pe.matmul(O[VW * j:VW * j + VW, g * P:(g + 1) * P], vaug[par][:, HG * g + j],
                                     ET[:, HG * g + j], start=True, stop=True)
                last.then_inc(o_done, 1)

            def turn_back(b):
                pe.wait_ge(oT_ready, b + 1)
                if upto(b, B - 3):
                    pe.wait_ge(xcT_ready, b + 3)
                if after(b, 1):
                    pe.wait_ge(on_ready, b)
                for g in range(NG):
                    last = pe.transpose(IN[:, g * P:(g + 1) * P], oT[:, g], c["ident"][:])
                last.then_inc(ob_done, 1)

            def turn_out(b):
                pe.wait_ge(on_ready, b + 1)
                if upto(b, B - 3):
                    pe.wait_ge(qkT_ready, b + 3)
                if after(b, 1):
                    pe.wait_ge(onT_ready, b)
                for i in range(DC):
                    last = pe.transpose(QK[:, i * P:(i + 1) * P], on[:, i * P:(i + 1) * P], c["ident"][:])
                last.then_inc(onT_done, 1)

            def project_out(b):
                pe.wait_ge(onT_ready, b + 1)
                if upto(b, B - 3):
                    pe.wait_ge(v_ready, b + 3)
                if upto(b, B - 2) and after(b, 1):
                    pe.wait_ge(lg_ready, b)
                elif not upto(b, B - 2):
                    pe.wait_ge(xo_step, 2 * (b - 1) + 1)
                for ci in range(DC):
                    last = pe.matmul(V[:, 0:D], onT[:, ci], wo[:, ci], start=(ci == 0), stop=(ci == DC - 1))
                last.then_inc(wo_done, 1)

            def turn_h(b, par):
                pe.wait_ge(h_ready, b + 1)
                if upto(b, B - 4):
                    pe.wait_ge(v_ready, b + 4)
                elif upto(b, B - 2):
                    pe.wait_ge(xo_step, 2 * (b + (b == B - 2)) + 1)
                else:
                    pe.wait_ge(lg_ready, b)
                for i in range(DC):
                    last = pe.transpose(V[:, D + i * P:D + (i + 1) * P], hb[par][:, i * P:(i + 1) * P],
                                        c["ident"][:])
                last.then_inc(hT_done, 1)

            def logits(b):
                pe.wait_ge(hT_ready, b + 1)
                for i in range(DC):
                    last = pe.matmul(V[:, 0:E], hT[:, i], wr[:, i], start=(i == 0), stop=(i == DC - 1))
                last.then_inc(lg_done, 1)

            def tile(b, par, k):
                nxt = upto(b, B - 2)
                scores(b, par, 0)
                if after(b, 1):
                    turn_e(b - 1, 2)
                    outputs(b - 1, 1 - par, 1)
                if after(b, 2):
                    turn_out(b - 2)
                if nxt:
                    bring(b + 1, 1 - par, next_k(b, par, k))
                scores(b, par, 1)
                if after(b, 3):
                    turn_h(b - 3, 1 - par)
                if after(b, 1):
                    turn_e(b - 1, 3)
                    outputs(b - 1, 1 - par, 2)
                if nxt:
                    project_qk(b + 1, 1 - par)
                if after(b, 3):
                    logits(b - 3)
                scores(b, par, 2)
                turn_e(b, 0)
                if after(b, 1):
                    outputs(b - 1, 1 - par, 3)
                if after(b, 2):
                    project_out(b - 2)
                scores(b, par, 3)
                turn_e(b, 1)
                outputs(b, par, 0)
                if after(b, 1):
                    turn_back(b - 1)
                if nxt:
                    project_v(b + 1, 1 - par)

            bring(0, 0, 0)
            project_qk(0, 0)
            project_v(0, 0)
            tiles(pe, tile)
            turn_e(B - 1, 2)
            outputs(B - 1, 1, 1)
            turn_out(B - 2)
            turn_e(B - 1, 3)
            outputs(B - 1, 1, 2)
            turn_h(B - 3, 1)
            outputs(B - 1, 1, 3)
            logits(B - 3)
            project_out(B - 2)
            turn_back(B - 1)
            turn_out(B - 1)
            project_out(B - 1)
            turn_h(B - 2, 0)
            logits(B - 2)
            turn_h(B - 1, 1)
            logits(B - 1)

        @block.scalar
        def _(act):
            act.activation(warm[:], c["mhalf"][:, 0:1], ACT.Exp)

            def qk_out(b, par):
                act.wait_ge(qk_done, b + 1)
                if after(b, 2):
                    act.wait_ge(s_done, NG * (b - 1))
                    act.wait_ge(kblk_ready, DC * (b - 1))
                for ch in range(DC):
                    q, k = (QK[:, (i * DC + ch) * P:(i * DC + ch + 1) * P] for i in two)
                    if layer == 0:
                        act.activation(qT[par][:, ch], q, ACT.Identity, bias=c["bqs"][:, ch:ch + 1], scale=scale)
                        last = act.activation(kT[par][:, ch], k, ACT.Identity, bias=c["vecT0"][:, 2 + ch:3 + ch])
                    else:
                        act.activation(qT[par][:, ch], q, ACT.Copy, scale=scale)
                        last = act.activation(kT[par][:, ch], k, ACT.Copy)
                last.then_inc(qkT_ready, 1)

            def exps(b, par, g):
                act.wait_ge(mx_ready, NG * b + g + 1)
                if after(b, 1):
                    act.wait_ge(et_done, NG * (b - 1) + g + 1)
                for h in range(HG * g, HG * g + HG):
                    last = act.activation(E_[:, h], U[:, h], ACT.Exp, bias=nmx[par][:, h:h + 1], scale=twice)
                last.then_inc(e_ready, 1)

            def et_out(b, g):
                act.wait_ge(et_done, NG * b + g + 1)
                if after(b, 1):
                    act.wait_ge(o_done, NG * (b - 1) + g + 1)
                act.activation(ET[:, HG * g:HG * g + HG].rearrange("p h t -> p (h t)"), TE[g % 2][:],
                               ACT.Copy).then_inc(eT_ready, 1)

            def o_out(b):
                act.wait_ge(o_done, NG * b + NG)
                if after(b, 1):
                    act.wait_ge(ob_done, b)
                act.activation(oT[:].rearrange("p g t -> p (g t)"), O[:], ACT.Copy).then_inc(oT_ready, 1)

            def hT_out(b):
                act.wait_ge(hT_done, b + 1)
                if after(b, 1):
                    act.wait_ge(lg_done, b)
                act.activation(hT[:].rearrange("p c t -> p (c t)"), V[:, D:2 * D], ACT.Copy).then_inc(hT_ready, 1)

            def keep_h(b, par):
                act.wait_ge(h_ready, b + 1)
                act.activation(c["Hn"][:, b], hb[par][:], ACT.Copy).then_inc(h_kept, 1)

            def tile(b, par, k):
                if after(b, 1):
                    et_out(b - 1, 2)
                exps(b, par, 0)
                if after(b, 3):
                    hT_out(b - 3)
                if after(b, 1):
                    et_out(b - 1, 3)
                exps(b, par, 1)
                if upto(b, B - 2):
                    qk_out(b + 1, 1 - par)
                et_out(b, 0)
                exps(b, par, 2)
                if after(b, 1):
                    o_out(b - 1)
                et_out(b, 1)
                exps(b, par, 3)
                if after(b, 3):
                    keep_h(b - 3, 1 - par)

            qk_out(0, 0)
            tiles(act, tile)
            et_out(B - 1, 2)
            et_out(B - 1, 3)
            hT_out(B - 3)
            keep_h(B - 3, 1)
            o_out(B - 1)
            hT_out(B - 2)
            keep_h(B - 2, 0)
            hT_out(B - 1)
            keep_h(B - 1, 1)

        @block.vector
        def _(dve):
            def mask():
                dve.wait_ge(small_loaded, 32)
                dve.tensor_scalar(amh[:], amh[:], 0.5, None, ALU.mult).then_inc(amh_ready, 1)
                dve.tensor_scalar(amb[:], padu[:], -BIG, 10.0, ALU.mult, ALU.mult).then_inc(amh_ready, 1)
                dve.wait_ge(amh_ready, 2)
                dve.tensor_tensor(amb[:], amb[:], bcast(amh[:].rearrange("p (o s) -> p o s", o=1), [P, B, P]),
                                  ALU.add).then_inc(amb_ready, 1)

            def normed(b, par):
                if after(b, 2):
                    dve.wait_ge(in_done, b - 1)
                if layer == 0:
                    scale_, shift = c["rstd"][:, at(b)], c["nmr"][:, at(b)]
                else:
                    dve.wait_ge(rsa_ready, b + 1)
                    dve.scalar_tensor_tensor(nma[par][:], mva[par][:, 0:1], -1.0, rsa[par][:], ALU.mult, ALU.mult
                                             ).then_inc(nma_step, 1)
                    dve.wait_ge(nma_step, b + 1)
                    scale_, shift = rsa[par][:], nma[par][:]
                dve.tensor_scalar(xn[par][:], c["X"][:, b], scale_, shift, ALU.mult, ALU.add).then_inc(xn_ready, 1)

            def lead(b):
                dve.wait_ge(y_got[b], 32)
                x, (y1, y2) = c["X"][:, b], y[b]
                dve.scalar_tensor_tensor(y1[:], y1[:], routing["w12"][:, b, 0:1], c["base"][:, b], ALU.mult, ALU.add
                                         ).then_inc(lead_step, 1)
                dve.wait_ge(lead_step, 4 * b + 1)
                dve.scalar_tensor_tensor(y1[:], y2[:], routing["w12"][:, b, 1:2], y1[:], ALU.mult, ALU.add
                                         ).then_inc(lead_step, 1)
                dve.wait_ge(lead_step, 4 * b + 2)
                dve.tensor_scalar(y1[:], y1[:], -100.0, 100.0, ALU.max, ALU.min).then_inc(lead_step, 1)
                dve.wait_ge(lead_step, 4 * b + 3)
                dve.tensor_tensor(x, x, y1[:], ALU.add).then_inc(lead_step, 1)
                dve.wait_ge(lead_step, 4 * b + 4)

            def stats_ahead(b, par):
                if after(b, LEAD):
                    dve.wait_ge(moe_step, MOE_STEPS * (b - (LEAD - 1)))
                dve.memset(gate[:], 0.0)
                dve.bn_stats(sta[:], c["X"][:, b]).then_inc(sta_ready, 1)
                dve.wait_ge(sta_ready, 2 * b + 1)
                dve.memset(gate[:], 0.0)
                dve.bn_aggr(mva[par][:], sta[:]).then_inc(sta_ready, 1)
                dve.wait_ge(sta_ready, 2 * b + 2)
                dve.tensor_scalar(vea[par][:], mva[par][:, 1:2], EPS, None, ALU.add).then_inc(vea_ready, 1)

            def in_out(b, par):
                dve.wait_ge(in_done, b + 1)
                if after(b, 2):
                    dve.wait_ge(v_done, b - 1)
                dve.tensor_copy(xcT[par][:].rearrange("p c t -> p (c t)"), IN[:]).then_inc(xcT_ready, 1)

            def k_out(b, par, ch):
                if ch == 0:
                    dve.wait_ge(qkT_ready, b + 1)
                    if after(b, 2):
                        dve.wait_ge(s_done, NG * (b - 1))
                dve.tensor_tensor(kblk[par][:, ch],
                                  bcast(kT[par][:, ch:ch + 1], [P, 8, P]),
                                  bcast(c["hmask"][:].rearrange("p (h o) -> p h o", o=1), [P, 8, P]), ALU.mult
                                  ).then_inc(kblk_ready, 1)

            def v_out(b, par):
                dve.wait_ge(v_done, b + 1)
                if after(b, 2):
                    dve.wait_ge(o_done, NG * (b - 1))
                to = vaug[par][:, :, 0:HD]
                of = V[:, 0:D].rearrange("p (h d) -> p h d", d=HD)
                if layer == 0:
                    dve.tensor_tensor(to, of, c["bv"][:].rearrange("p (h d) -> p h d", d=HD), ALU.add
                                      ).then_inc(v_ready, 1)
                else:
                    dve.tensor_copy(to, of).then_inc(v_ready, 1)

            def maxima(b, par, g):
                dve.wait_ge(s_done, NG * b + g + 1)
                if layer == 0 and g == 0:
                    dve.wait_ge(bias_ready, b + 1)
                if after(b, 1):
                    dve.wait_ge(e_ready, NG * (b - 1) + g + 1)
                dve.memset(gate[:], 0.0)
                for j in range(HG):
                    h = HG * g + j
                    last = dve.tensor_tensor_reduce(U[:, h], S[g % 2][:, j * P:(j + 1) * P],
                                                    fs[par][:, h] if layer == 0 else c["M1"][:],
                                                    1.0, -BIG, ALU.add, ALU.max, mx[par][:, h:h + 1])
                last.then_inc(mx_step, 1)
                dve.wait_ge(mx_step, NG * b + g + 1)
                dve.tensor_scalar(nmx[par][:, HG * g:HG * g + HG], mx[par][:, HG * g:HG * g + HG], -twice, None,
                                  ALU.mult).then_inc(mx_ready, 1)

            def divide(b):
                dve.wait_ge(ob_done, b + 1)
                if after(b, 1):
                    dve.wait_ge(onT_done, b)
                ob = IN[:].rearrange("p (h w) -> p h w", w=VW)
                dve.reciprocal(rz[:], ob[:, :, HD]).then_inc(rz_step, 1)
                dve.wait_ge(rz_step, b * rz_per_tile + 1)
                if layer == 1:
                    dve.tensor_scalar(rz[:], rz[:], c["rowany"][:, 0:1], None, ALU.mult).then_inc(rz_step, 1)
                    dve.wait_ge(rz_step, b * 2 + 2)
                dve.tensor_tensor(on[:].rearrange("p (h d) -> p h d", d=HD), ob[:, :, 0:HD],
                                  bcast(rz[:].rearrange("p (h o) -> p h o", o=1), [P, H, HD]), ALU.mult
                                  ).then_inc(on_ready, 1)

            def turned(b):
                dve.wait_ge(onT_done, b + 1)
                if after(b, 1):
                    dve.wait_ge(wo_done, b)
                dve.tensor_copy(onT[:].rearrange("p c t -> p (c t)"), QK[:, 0:D]).then_inc(onT_ready, 1)

            def projected(b):
                dve.wait_ge(wo_done, b + 1)
                if layer == 0:
                    dve.tensor_tensor(xo[:], V[:, 0:D], c["bo"][:], ALU.add).then_inc(xo_step, 1)
                else:
                    dve.tensor_copy(xo[:], V[:, 0:D]).then_inc(xo_step, 1)

            def residual(b, par):
                dve.wait_ge(xo_step, 2 * b + 1)
                dve.tensor_tensor(c["X"][:, b], c["X"][:, b], xo[:], ALU.add).then_inc(xo_step, 1)
                dve.wait_ge(xo_step, 2 * b + 2)
                dve.memset(gate[:], 0.0)
                dve.bn_stats(st[:], c["X"][:, b]).then_inc(x_ready, 1)
                dve.wait_ge(x_ready, b + 1)
                if after(b, 2):
                    dve.wait_ge(nm_step, b - 1)
                dve.memset(gate[:], 0.0)
                dve.bn_aggr(mv[par][:], st[:]).then_inc(st_step, 1)
                dve.wait_ge(st_step, b + 1)
                if after(b, 2):
                    dve.wait_ge(rs_ready, b - 1)
                dve.tensor_scalar(ve[par][:], mv[par][:, 1:2], EPS, None, ALU.add).then_inc(ve_ready, 1)

            def layer_norm(b, par):
                dve.wait_ge(rs_ready, b + 1)
                dve.scalar_tensor_tensor(nm[par][:], mv[par][:, 0:1], -1.0, rs[par][:], ALU.mult, ALU.mult
                                         ).then_inc(nm_step, 1)
                dve.wait_ge(nm_step, b + 1)
                if after(b, 2):
                    dve.wait_ge(hT_done, b - 1)
                    dve.wait_ge(h_kept, b - 1)
                dve.tensor_scalar(hb[par][:], c["X"][:, b], rs[par][:], nm[par][:], ALU.mult, ALU.add
                                  ).then_inc(h_ready, 1)

            def logits_out(b):
                dve.wait_ge(lg_done, b + 1)
                dve.tensor_copy(LG[:, b], V[:, 0:E]).then_inc(lg_ready, 1)

            def tile(b, par, k):
                nxt = upto(b, B - 2)
                if after(b, 2):
                    divide(b - 2)
                maxima(b, par, 0)
                if after(b, 2):
                    turned(b - 2)
                v_out(b, par)
                if after(b, 3):
                    layer_norm(b - 3, 1 - par)
                if nxt:
                    in_out(b + 1, 1 - par)
                maxima(b, par, 1)
                k_out(b, par, 1)
                if upto(b, B - 3):
                    normed(b + 2, par)
                if layer == 1 and upto(b, B - 4):
                    stats_ahead(b + 3, 1 - par)
                if after(b, 3):
                    logits_out(b - 3)
                maxima(b, par, 2)
                if nxt:
                    k_out(b + 1, 1 - par, 0)
                if after(b, 2):
                    projected(b - 2)
                maxima(b, par, 3)
                if after(b, 2):
                    residual(b - 2, par)

            if layer == 1:
                lead(0)
                stats_ahead(0, 0)
            normed(0, 0)
            if layer == 0:
                mask()
            if layer == 1:
                lead(1)
                stats_ahead(1, 1)
            in_out(0, 0)
            k_out(0, 0, 0)
            normed(1, 1)
            if layer == 1:
                lead(2)
                stats_ahead(2, 0)
            dve.wait_ge(vones_ready, 2)
            tiles(dve, tile)
            divide(B - 2)
            turned(B - 2)
            layer_norm(B - 3, 1)
            logits_out(B - 3)
            projected(B - 2)
            residual(B - 2, 0)
            divide(B - 1)
            turned(B - 1)
            layer_norm(B - 2, 0)
            projected(B - 1)
            residual(B - 1, 1)
            logits_out(B - 2)
            layer_norm(B - 1, 1)
            logits_out(B - 1)


def at(b):
    return slice(b, b + 1) if isinstance(b, int) else bass.ds(b, 1)


def after(b, n):
    return not isinstance(b, int) or b >= n


def upto(b, n):
    return not isinstance(b, int) or b <= n


def paired(eng, n, step, first=2):
    turns = (n - first - 2) // 2
    for i in range(first):
        step(i, i % 2, i // 2)
    with eng.Fori(0, turns) as i:
        step(i * 2 + first, 0, i + first // 2)
        step(i * 2 + first + 1, 1, i + first // 2)
    for i in range(first + 2 * turns, n):
        step(i, i % 2, i // 2)


def table(keep, moe):
    E, S, layer = moe.E, moe.slots, moe.layer
    routing = {
        "w12": keep("w12", [P, B, 2]),
        "G": keep("G", [P, B, E]),
        "rows": keep("rows", [P, 2, B], I32),
        "expert": keep("expert", [P, S], I32),
        "b2": keep("b2", [E + layer, D]),
    }
    if layer == 1:
        routing["w1_shared"] = keep("w1_shared", [P, DC, moe.F])
        routing["w2_shared"] = keep("w2_shared", [P, moe.FC, D])
    return routing


def expert_w2(nc, keep, moe):
    return {
        "w2": keep("w2", [P, moe.E * moe.FC * D]),
        "loaded": nc.alloc_semaphore(f"weights_loaded{moe.layer}"),
    }


def expert_w1(keep, moe, weights):
    weights["w1"] = keep("w1", [P, moe.E * DC * moe.F])


def load_w2(sp, moe, weights, e):
    sp.dma_start(weights["w2"][:, bass.ds(e * (moe.FC * D), moe.FC * D)].rearrange("p (c d) -> p c d", d=D),
                 moe.w2[e].rearrange("(c p) d -> p c d", p=P)).then_inc(weights["loaded"], 16)


def route(nc, sem, alloc, a, c, moe, routing, weights):
    E, S, layer = moe.E, moe.slots, moe.layer
    with ExitStack() as stack:
        sb = alloc(stack)
        two = range(2)
        top8 = sb("top8", [P, B, 8])
        ix8 = sb("ix8", [P, B, 8], U32)
        ixf = sb("ixf", [P, B, 2])
        hot = [sb(f"hot{j}", [P, B, E]) for j in two]
        both = sb("both", [P, B, E])
        diff = sb("diff", [P, B])
        e2 = sb("e2", [P, B])
        den = sb("den", [P, B])
        tmp = sb("tmp", [P, B, E])
        cnt = sb("cnt", [P, B + 1, E])
        pre = sb("pre", [P, B + 1, E])
        over = sb("over", [P, E, B])
        nslot = sb("nslot", [P, E])
        first = sb("first", [P, E])
        base = sb("base", [P, E])
        pos = sb("pos", [P, B, E])
        rowf = sb("rowf", [P, 2, B])
        cmp = sb("cmp", [P, S, E - 1])
        expf = sb("expf", [P, S])
        iota_e = sb("iota_e", [P, E])
        iota_b = sb("iota_b", [P, B])
        iota_s = sb("iota_s", [P, S])
        bank = [stack.enter_context(nc.psum_tensor(f"route{layer}_bank{i}", [P, 512], F32)) for i in two]
        LG = c[f"LG{layer}"]
        iotas_ready = sem("iotas_ready")
        step = sem("dve_step")
        diff_ready, e2_ready, both_ready, ranks_done = sem("diff"), sem("e2"), sem("both"), sem("ranks")
        kept_loaded = sem("kept_loaded")
        block = stack.enter_context(nc.Block())

        @block.sync
        def _(sp):
            sp.dma_start(routing["b2"][0:E], moe.b2).then_inc(kept_loaded, 16)
            if layer == 1:
                sp.dma_start(routing["b2"][E:E + 1], a["L1_ffn_bproj_s"].rearrange("(o d) -> o d", o=1)
                             ).then_inc(kept_loaded, 16)
                sp.dma_start(routing["w1_shared"][:], a["L1_ffn_Wfc_s"].rearrange("(c p) f -> p c f", p=P)
                             ).then_inc(kept_loaded, 16)
                sp.dma_start(routing["w2_shared"][:], a["L1_ffn_Wproj_s"].rearrange("(c p) d -> p c d", p=P)
                             ).then_inc(kept_loaded, 16)
            for e in range(E):
                sp.dma_start(weights["w1"][:, e * DC * moe.F:(e + 1) * DC * moe.F].rearrange("p (c f) -> p c f", c=DC),
                             moe.w1[e].rearrange("(c p) f -> p c f", p=P)).then_inc(weights["loaded"], 16)
                if layer == 1:
                    load_w2(sp, moe, weights, e)
            sp.wait_ge(kept_loaded, 16 * (1 + 3 * layer))

        @block.scalar
        def _(act):
            act.wait_ge(diff_ready, 1)
            act.activation(e2[:], diff[:], ACT.Exp).then_inc(e2_ready, 1)

        @block.tensor
        def _(pe):
            pe.wait_ge(both_ready, 1)
            m = both[:].rearrange("p b e -> p (b e)")
            pe.matmul(bank[0][:, 0:B * E], c["before"][:], m, start=True, stop=True)
            pe.matmul(bank[1][:, 0:B * E], c["ones"][:], m, start=True, stop=True).then_inc(ranks_done, 1)

        @block.gpsimd
        def _(pool):
            pool.iota(iota_e[:], [[1, E]], base=0, channel_multiplier=0, allow_small_or_imprecise_dtypes=True)
            pool.iota(iota_b[:], [[P, B]], base=0, channel_multiplier=0, allow_small_or_imprecise_dtypes=True)
            pool.iota(iota_s[:], [[1, S]], base=0, channel_multiplier=0, allow_small_or_imprecise_dtypes=True
                      ).then_inc(iotas_ready, 1)

        @block.vector
        def _(dve):
            done = [0]

            def link(ins):
                done[0] += 1
                ins.then_inc(step, 1)
                dve.wait_ge(step, done[0])

            def col(ap, shape):
                return bcast(ap, shape)

            full = [P, B, E]
            for b in range(B):
                last = dve.max(top8[:, b], LG[:, b])
            link(last)
            dve.tensor_tensor(diff[:], top8[:, :, 1], top8[:, :, 0], ALU.subtract).then_inc(diff_ready, 1)
            for b in range(B):
                last = dve.max_index(ix8[:, b], top8[:, b], LG[:, b])
            link(last)
            link(dve.tensor_copy(ixf[:], ix8[:, :, 0:2]))
            dve.wait_ge(iotas_ready, 1)
            ie = col(iota_e[:].rearrange("p (o e) -> p o e", o=1), full)
            for j in two:
                last = dve.tensor_tensor(hot[j][:], ie, col(ixf[:, :, j:j + 1], full), ALU.is_equal)
            link(last)
            dve.tensor_tensor(both[:], hot[0][:], hot[1][:], ALU.add).then_inc(both_ready, 1)
            dve.wait_ge(e2_ready, 1)
            link(dve.tensor_scalar(den[:], e2[:], 1.0, None, ALU.add))
            link(dve.reciprocal(routing["w12"][:, :, 0], den[:]))
            link(dve.tensor_tensor(routing["w12"][:, :, 1], routing["w12"][:, :, 0], e2[:], ALU.mult))
            dve.tensor_tensor(tmp[:], hot[0][:], col(routing["w12"][:, :, 0:1], full), ALU.mult)
            link(dve.tensor_tensor(routing["G"][:], hot[1][:], col(routing["w12"][:, :, 1:2], full), ALU.mult))
            link(dve.tensor_tensor(routing["G"][:], routing["G"][:], tmp[:], ALU.add))
            dve.memset(pre[:, 0], 0.0)
            dve.memset(first[:, 0:1], 0.0)
            dve.wait_ge(ranks_done, 1)
            src, to = pre, cnt
            link(dve.tensor_copy(src[:, 1:B + 1].rearrange("p b e -> p (b e)"), bank[1][:, 0:B * E]))
            for d in (1, 2, 4, 8):
                dve.tensor_copy(to[:, 1:d + 1], src[:, 1:d + 1])
                link(dve.tensor_tensor(to[:, d + 1:], src[:, d + 1:], src[:, 1:B + 1 - d], ALU.add))
                src, to = to, src
            link(dve.tensor_tensor(over[:], col(pre[:, B].rearrange("p (e o) -> p e o", o=1), [P, E, B]),
                                   col(iota_b[:].rearrange("p (o b) -> p o b", o=1), [P, E, B]), ALU.is_gt))
            link(dve.tensor_reduce(nslot[:], over[:], AX.X, ALU.add))
            link(dve.tensor_copy(first[:, 1:E], nslot[:, 0:E - 1]))
            begin, spare, d = first, base, 1
            while d < E - 1:
                dve.tensor_copy(spare[:, 0:d + 1], begin[:, 0:d + 1])
                link(dve.tensor_tensor(spare[:, d + 1:E], begin[:, d + 1:E], begin[:, 1:E - d], ALU.add))
                begin, spare, d = spare, begin, 2 * d
            link(dve.tensor_scalar(spare[:], begin[:], float(P), None, ALU.mult))
            link(dve.tensor_tensor(pos[:].rearrange("p b e -> p (b e)"), bank[0][:, 0:B * E],
                                   pre[:, 0:B].rearrange("p b e -> p (b e)"), ALU.add))
            link(dve.tensor_tensor(pos[:], pos[:], col(spare[:].rearrange("p (o e) -> p o e", o=1), full), ALU.add))
            for j in two:
                link(dve.tensor_tensor(tmp[:], pos[:], hot[j][:], ALU.mult))
                link(dve.tensor_reduce(rowf[:, j], tmp[:], AX.X, ALU.add))
            dve.tensor_copy(routing["rows"][:], rowf[:])
            link(dve.tensor_tensor(cmp[:], col(iota_s[:].rearrange("p (s o) -> p s o", o=1), [P, S, E - 1]),
                                   col(begin[:, 1:E].rearrange("p (o e) -> p o e", o=1), [P, S, E - 1]), ALU.is_ge))
            link(dve.tensor_reduce(expf[:], cmp[:], AX.X, ALU.add))
            dve.tensor_copy(routing["expert"][:], expf[:])


def send_rows(pool, c, routing, b, sent):
    for j in range(TOPK):
        pool.indirect_dma_start(out=c["xg"], out_offset=bass.IndirectOffsetOnAxis(
            ap=routing["rows"][:, j, b:b + 1].bitcast(U32), axis=0), in_=c["Hn"][:, b], in_offset=None).then_inc(sent, 16)


def shared_expert(nc, sem, alloc, c, moe, routing, half, out=None):
    FC, E = moe.FC, moe.E
    HALF = B // 2
    lo = half * HALF
    w1, w2 = routing["w1_shared"], routing["w2_shared"]
    with ExitStack() as stack:
        sb = alloc(stack)
        two = range(2)
        rows = [sb(f"rows{i}", [P, D + E + 1]) for i in two]
        xT = [sb(f"xT{i}", [P, DC, P]) for i in two]
        gT = [sb(f"gT{i}", [E + 1, P]) for i in two]
        hid = [sb(f"hid{i}", [P, FC, P]) for i in two]
        warm = sb("warm", [P, 1])
        y = [[sb(f"y{i}_{j}", [P, D]) for j in two] for i in range(4)]
        bank = [stack.enter_context(nc.psum_tensor(f"shared{half}_bank{i}", [P, 512], F32)) for i in range(8)]
        T, HB, Y = bank[0:2], bank[2:6], bank[6:8]
        ones_ready = sem("ones_ready")
        rows_copied = sem("rows_copied")
        rows_sent = sem("rows_sent")
        xT_done = sem("xT_done")
        xT_ready = sem("xT_ready")
        gT_ready = sem("gT_ready")
        hid_done = sem("hid_done")
        hid_ready = sem("hid_ready")
        y_done = sem("y_done")
        y_added = sem("y_added")
        routed_got = [sem(f"routed_got{i}") for i in range(4)]
        routed_step = sem("routed_step")
        routed_added = sem("routed_added")
        stored = sem("stored")
        block = stack.enter_context(nc.Block())

        @block.sync
        def _(sp):
            if half == 1:
                def store(b, par, k):
                    sp.wait_ge(routed_added, b + 1)
                    sp.dma_start(out[b], c["X"][:, b]).then_inc(stored, 16)
                paired(sp, B, store)
                sp.wait_ge(stored, 16 * B)

        @block.gpsimd
        def _(pool):
            def copy(n):
                if n >= 2:
                    pool.wait_ge(xT_done, n - 1)
                pool.tensor_copy(rows[n % 2][:, 0:D], c["Hn"][:, lo + n]).then_inc(rows_copied, 1)
                pool.tensor_copy(rows[n % 2][:, D:D + E], routing["G"][:, lo + n]).then_inc(rows_copied, 1)

            def fetch(b):
                if b >= 4:
                    pool.wait_ge(routed_added, b - 3)
                for j in two:
                    pool.indirect_dma_start(out=y[b % 4][j][:], out_offset=None, in_=c["yg"],
                                            in_offset=bass.IndirectOffsetOnAxis(
                                                ap=routing["rows"][:, j, b:b + 1].bitcast(U32), axis=0)
                                            ).then_inc(routed_got[b % 4], 16)
            for i in two:
                pool.memset(rows[i][:, D + E:D + E + 1], 1.0).then_inc(ones_ready, 1)
            copy(0)
            copy(1)
            for b in range(B):
                if half == 0:
                    send_rows(pool, c, routing, b, rows_sent)
                else:
                    fetch(b)
                if b % 2 == 1 and b // 2 + 2 < HALF:
                    copy(b // 2 + 2)
            if half == 0:
                pool.wait_ge(rows_sent, 16 * TOPK * B)

        @block.tensor
        def _(pe):
            def turn(n, par):
                pe.wait_ge(rows_copied, 2 * n + 2)
                if after(n, 2):
                    pe.wait_ge(gT_ready, n - 1)
                for i in range(DC):
                    pe.transpose(T[par][:, i * P:(i + 1) * P], rows[par][:, i * P:(i + 1) * P], c["ident"][:])
                pe.transpose(T[par][0:E + 1, D:D + P], rows[par][:, D:D + E + 1], c["ident"][:]
                             ).then_inc(xT_done, 1)

            def up(n, par):
                pe.wait_ge(xT_ready, n + 1)
                for f in range(FC):
                    if after(n, 1) or f >= 4:
                        pe.wait_ge(hid_ready, FC * n + f - 3)
                    for i in range(DC):
                        last = pe.matmul(HB[f % 4][:, 0:P], w1[:, i, f * P:(f + 1) * P], xT[par][:, i],
                                         start=(i == 0), stop=(i == DC - 1))
                    last.then_inc(hid_done, 1)

            def down(n, par):
                if after(n, 2):
                    pe.wait_ge(y_added, n - 1)
                pe.wait_ge(gT_ready, n + 1)
                pe.matmul(Y[par][:, 0:D], gT[par][:], routing["b2"][:], start=True, stop=False)
                for f in range(FC):
                    pe.wait_ge(hid_ready, FC * n + f + 1)
                    last = pe.matmul(Y[par][:, 0:D], hid[par][:, f], w2[:, f], start=False, stop=(f == FC - 1))
                last.then_inc(y_done, 1)

            def tile(n, par, k):
                if upto(n, HALF - 2):
                    up(n + 1, 1 - par)
                if upto(n, HALF - 3):
                    turn(n + 2, par)
                down(n, par)
            pe.wait_ge(ones_ready, 2)
            turn(0, 0)
            turn(1, 1)
            up(0, 0)
            paired(pe, HALF, tile)

        @block.scalar
        def _(act):
            act.activation(warm[:], c["mhalf"][:, 0:1], moe.act)

            def tile(n, par, k):
                if after(n, 2):
                    act.wait_ge(y_done, n - 1)
                for f in range(FC):
                    act.wait_ge(hid_done, FC * n + f + 1)
                    act.activation(hid[par][:, f], HB[f % 4][:, 0:P], moe.act, bias=c["vecT1"][:, 64 + f:65 + f]
                                   ).then_inc(hid_ready, 1)
            paired(act, HALF, tile)

        @block.vector
        def _(dve):
            def in_out(n, par):
                dve.wait_ge(xT_done, n + 1)
                if after(n, 2):
                    dve.wait_ge(hid_done, FC * (n - 1))
                dve.tensor_copy(xT[par][:].rearrange("p c t -> p (c t)"), T[par][:, 0:D]).then_inc(xT_ready, 1)
                if after(n, 2):
                    dve.wait_ge(y_done, n - 1)
                dve.tensor_copy(gT[par][:], T[par][0:E + 1, D:D + P]).then_inc(gT_ready, 1)

            def add_routed(b, buf, k):
                dve.wait_ge(routed_got[buf], 32 * k + 32)
                w = [routing["w12"][:, at(b), j:j + 1].rearrange("p o j -> p (o j)") for j in two]
                dve.scalar_tensor_tensor(c["X"][:, b], y[buf][0][:], w[0], c["X"][:, b], ALU.mult, ALU.add
                                         ).then_inc(routed_step, 1)
                dve.wait_ge(routed_step, b + 1)
                dve.scalar_tensor_tensor(c["X"][:, b], y[buf][1][:], w[1], c["X"][:, b], ALU.mult, ALU.add
                                         ).then_inc(routed_added, 1)

            def tile(n, par, k):
                if half == 1:
                    add_routed(n * 2, 2 * par, k)
                if upto(n, HALF - 3):
                    in_out(n + 2, par)
                dve.wait_ge(y_done, n + 1)
                dve.tensor_tensor(c["X"][:, n + lo], c["X"][:, n + lo], Y[par][:, 0:D], ALU.add).then_inc(y_added, 1)
                dve.wait_ge(y_added, n + 1)
                if half == 1:
                    add_routed(n * 2 + 1, 2 * par + 1, k)
            in_out(0, 0)
            in_out(1, 1)
            paired(dve, HALF, tile)


def experts(nc, sem, alloc, c, moe, routing, weights):
    FC, E, n_slots = moe.FC, moe.E, moe.slots
    CF = PIECE // P
    NP = moe.F // PIECE
    with ExitStack() as stack:
        sb = alloc(stack)
        two = range(2)
        wp = [sb(f"wp{i}", [P, DC, PIECE]) for i in two]
        rows = [sb(f"rows{i}", [P, D]) for i in two]
        xT = [sb(f"xT{i}", [P, DC, P]) for i in two]
        hid = [sb(f"hid{i}", [P, FC, P]) for i in two]
        warm = sb("warm", [P, 1])
        yb = [sb(f"yb{i}", [P, D]) for i in two]
        bank = [stack.enter_context(nc.psum_tensor(f"experts{moe.layer}_bank{i}", [P, 512], F32)) for i in range(8)]
        T, HB, Y = bank[0:2], bank[2:6], bank[6:8]
        rows_loaded = [sem(f"rows_loaded{i}") for i in two]
        wp_ready = sem("wp_ready")
        xT_done = sem("xT_done")
        xT_ready = sem("xT_ready")
        hid_done = sem("hid_done")
        hid_ready = sem("hid_ready")
        y_done = sem("y_done")
        y_ready = sem("y_ready")
        y_stored = [sem(f"y_stored{i}") for i in two]
        block = stack.enter_context(nc.Block())

        @block.sync
        def _(sp):
            def get(n, par, k):
                if after(n, 2):
                    sp.wait_ge(xT_done, n - 1)
                sp.dma_start(rows[par][:], row_block(c["xg"], n)).then_inc(rows_loaded[par], 16)
            paired(sp, n_slots, get)

        @block.gpsimd
        def _(pool):
            def store(n, par, k):
                pool.wait_ge(y_ready, n + 1)
                pool.dma_start(row_block(c["yg"], n), yb[par][:]).then_inc(y_stored[par], 16)
            paired(pool, n_slots, store)
            for i in two:
                pool.wait_ge(y_stored[i], 16 * ((n_slots + 1 - i) // 2))

        @block.tensor
        def _(pe):
            def turn(n, par, k):
                pe.wait_ge(rows_loaded[par], 16 * k + 16)
                if after(n, 2):
                    pe.wait_ge(xT_ready, n - 1)
                for i in range(DC):
                    last = pe.transpose(T[par][:, i * P:(i + 1) * P], rows[par][:, i * P:(i + 1) * P], c["ident"][:])
                last.then_inc(xT_done, 1)

            def expert_of(n):
                return pe.value_load(routing["expert"][0:1, at(n)], min_val=0, max_val=E - 1)

            def up(n, par, k):
                pe.wait_ge(xT_ready, n + 1)
                for f in range(FC):
                    piece = wp[par if NP == 1 else f // CF]
                    if f % CF == 0:
                        pe.wait_ge(wp_ready, NP * n + f // CF + 1)
                    if after(n, 1) or f >= 4:
                        pe.wait_ge(hid_ready, FC * n + f - 3)
                    for i in range(DC):
                        last = pe.matmul(HB[f % 4][:, 0:P], piece[:, i, (f % CF) * P:(f % CF + 1) * P], xT[par][:, i],
                                         start=(i == 0), stop=(i == DC - 1))
                    last.then_inc(hid_done, 1)

            def down(n, par, k):
                e = expert_of(n)
                if after(n, 2):
                    pe.wait_ge(y_ready, n - 1)
                for f in range(FC):
                    pe.wait_ge(hid_ready, FC * n + f + 1)
                    last = pe.matmul(Y[par][:, 0:D], hid[par][:, f],
                                     weights["w2"][:, bass.ds(e * (FC * D) + f * D, D)],
                                     start=(f == 0), stop=(f == FC - 1))
                last.then_inc(y_done, 1)

            def slot(n, par, k):
                if upto(n, n_slots - 2):
                    up(n + 1, 1 - par, (n + 1) // 2 if isinstance(n, int) else (k if par == 0 else k + 1))
                if upto(n, n_slots - 3):
                    turn(n + 2, par, k + 1)
                down(n, par, k)
            turn(0, 0, 0)
            turn(1, 1, 0)
            pe.wait_ge(weights["loaded"], 32 * E)
            up(0, 0, 0)
            paired(pe, n_slots, slot)

        @block.scalar
        def _(act):
            act.activation(warm[:], c["mhalf"][:, 0:1], moe.act)

            def slot(n, par, k):
                e = act.value_load(routing["expert"][0:1, at(n)], min_val=0, max_val=E - 1)
                if after(n, 2):
                    act.wait_ge(y_done, n - 1)
                for f in range(FC):
                    if moe.layer == 0:
                        bias = c["vecT0"][:, bass.ds(e * FC + (4 + f), 1)]
                    else:
                        bias = c["vecT1"][:, bass.ds(e * FC + f, 1)]
                    act.wait_ge(hid_done, FC * n + f + 1)
                    act.activation(hid[par][:, f], HB[f % 4][:, 0:P], moe.act, bias=bias).then_inc(hid_ready, 1)
            paired(act, n_slots, slot)

        @block.vector
        def _(dve):
            def in_out(n, par):
                dve.wait_ge(xT_done, n + 1)
                if after(n, 2):
                    dve.wait_ge(hid_done, FC * (n - 1))
                dve.tensor_copy(xT[par][:].rearrange("p c t -> p (c t)"), T[par][:, 0:D]).then_inc(xT_ready, 1)

            def bring_w1(n, par):
                e = dve.value_load(routing["expert"][0:1, at(n)], min_val=0, max_val=E - 1)
                for q in range(NP):
                    if after(n, 2) or NP * n + q >= 2:
                        dve.wait_ge(hid_done, n * FC + CF * (q - 1))
                    of = weights["w1"][:, bass.ds(e * (DC * moe.F), DC * moe.F)].rearrange("p (c f) -> p c f", c=DC)
                    dve.tensor_copy(wp[par if NP == 1 else q][:], of[:, :, q * PIECE:(q + 1) * PIECE]
                                    ).then_inc(wp_ready, 1)

            def slot(n, par, k):
                if upto(n, n_slots - 3):
                    bring_w1(n + 2, par)
                    in_out(n + 2, par)
                dve.wait_ge(y_done, n + 1)
                if after(n, 2):
                    dve.wait_ge(y_stored[par], 16 * k)
                dve.tensor_copy(yb[par][:], Y[par][:, 0:D]).then_inc(y_ready, 1)
            in_out(0, 0)
            in_out(1, 1)
            dve.wait_ge(weights["loaded"], 32 * E)
            bring_w1(0, 0)
            bring_w1(1, 1)
            paired(dve, n_slots, slot)


def row_block(rows, n):
    return rows.rearrange("(s p) d -> s p d", p=P)[n]


def dispatch(nc, sem, alloc, c, moe, routing):
    E = moe.E
    with ExitStack() as stack:
        sb = alloc(stack)
        two = range(2)
        gst = [sb(f"gst{i}", [P, E]) for i in two]
        gT = [sb(f"gTs{i}", [E, P]) for i in two]
        bank = [stack.enter_context(nc.psum_tensor(f"dispatch_bank{i}", [P, 512], F32)) for i in range(4)]
        GT, B2 = bank[0:2], bank[2:4]
        rows_sent = sem("rows_sent")
        g_ready = sem("g_ready")
        gT_done = sem("gT_done")
        gT_ready = sem("gT_ready")
        b2_done = sem("b2_done")
        base_ready = sem("base_ready")
        block = stack.enter_context(nc.Block())

        @block.gpsimd
        def _(pool):
            pool.wait_ge(c["slots_zeroed"], 16 * 4)
            for b in range(B):
                send_rows(pool, c, routing, b, rows_sent)
            pool.wait_ge(rows_sent, 16 * TOPK * B)

        @block.tensor
        def _(pe):
            def tile(b, par, k):
                pe.wait_ge(g_ready, b + 1)
                if after(b, 2):
                    pe.wait_ge(gT_ready, b - 1)
                pe.transpose(GT[par][0:E, 0:P], gst[par][:], c["ident"][:]).then_inc(gT_done, 1)
                pe.wait_ge(gT_ready, b + 1)
                if after(b, 2):
                    pe.wait_ge(base_ready, b - 1)
                pe.matmul(B2[par][:, 0:D], gT[par][:], routing["b2"][:], start=True, stop=True).then_inc(b2_done, 1)
            paired(pe, B, tile)

        @block.scalar
        def _(act):
            def tile(b, par, k):
                act.wait_ge(gT_done, b + 1)
                if after(b, 2):
                    act.wait_ge(b2_done, b - 1)
                act.activation(gT[par][:], GT[par][0:E, 0:P], ACT.Copy).then_inc(gT_ready, 1)
            paired(act, B, tile)

        @block.vector
        def _(dve):
            def gates(b, par):
                if after(b, 2):
                    dve.wait_ge(gT_done, b - 1)
                dve.tensor_copy(gst[par][:], routing["G"][:, b]).then_inc(g_ready, 1)

            def tile(b, par, k):
                if upto(b, B - 2):
                    gates(b + 1, 1 - par)
                dve.wait_ge(b2_done, b + 1)
                dve.tensor_tensor(c["base"][:, b], B2[par][:, 0:D], c["Hn"][:, b], ALU.add).then_inc(base_ready, 1)
            gates(0, 0)
            paired(dve, B, tile)


def kernel(**inputs):
    import numpy as _np
    import concourse.bacc as _bacc
    from concourse import mybir as _mybir
    from concourse.bass_utils import run_bass_kernel_spmd as _run

    nc = _bacc.Bacc("TRN2", target_bir_lowering=False, num_devices=1)
    arrays, args = {}, {}
    for name in inputs:
        v = _np.ascontiguousarray(inputs[name])
        arrays[f"in_{name}_dram"] = v
        args[name] = nc.dram_tensor(f"in_{name}_dram", v.shape, _mybir.dt.from_np(v.dtype), kind="ExternalInput").ap()
    out = nc.dram_tensor("out_0_dram", (B, P, D), F32, kind="ExternalOutput").ap()
    build(nc, args, out)
    r = _run(nc, [arrays], core_ids=[0])
    return r.results[0]["out_0_dram"]
```
